# Optimizing a Trainium2 kernel written in Bass

```python
import numpy as np
import jax
import jax.numpy as jnp

def _softmax(x, axis=-1):
    return jax.nn.softmax(x, axis=axis)

def _gelu(x):
    return jax.nn.gelu(x, approximate=True)

def _silu(x):
    return jax.nn.silu(x)

def _sigmoid(x):
    return jax.nn.sigmoid(x)

def _layernorm(x, axis=-1, eps=1e-05):
    m = jnp.mean(x, axis=axis, keepdims=True)
    v = jnp.var(x, axis=axis, keepdims=True)
    return (x - m) / jnp.sqrt(v + eps)

def _scatter_add(tgt, idx, src, axis=0):
    return tgt.at[idx].add(src)

def _segment_sum(src, seg, n):
    return jax.ops.segment_sum(src, seg, n)
kernel_name = 'mk_decoder_postln_d1_seqx_r8_85e4f0'

def setup_inputs(seed: int=0):
    np.random.seed(seed)
    _w = jnp.asarray

    def _rec_inputs():
        import jax
        import jax.numpy as jnp
        _rk = jax.random.key(seed)
        x = 7.22e-05 + 1 * jax.random.normal(jax.random.fold_in(_rk, 1), (4, 256, 256), jnp.float32)
        _lenS = 256 - jax.random.randint(jax.random.fold_in(_rk, 7), (4,), 0, max(1, 256 // 4) + 1, jnp.int32)
        _lenS2 = 256 - jax.random.randint(jax.random.fold_in(_rk, 8), (4,), 0, max(1, 256 // 4) + 1, jnp.int32)
        _ctx_1024P = jax.random.normal(jax.random.fold_in(_rk, 11), (4, 16, 128), jnp.float32)
        _ctx_1024c = jax.random.dirichlet(jax.random.fold_in(_rk, 511), 0.3 * jnp.ones((16,), jnp.float32), (4, 256))
        _ctx_1024t = jnp.einsum('bsk,bkd->bsd', _ctx_1024c, _ctx_1024P)
        _ctx_1024t = _ctx_1024t * jax.lax.rsqrt(jnp.mean(jnp.square(_ctx_1024t)) + 1e-12) * 0.953939
        ctx_1024 = 2.81802e-05 + 1.00001 * (_ctx_1024t + 0.3 * jax.random.normal(jax.random.fold_in(_rk, 611), (4, 256, 128), jnp.float32))
        return (x, ctx_1024)
    x, ctx_1024 = _rec_inputs()

    def _L0_attn_setup():
        import jax, jax.numpy as jnp
        import numpy as np
        D_MODEL = 256
        N_QUERY = 4
        N_HEAD = 8
        D_HEAD = D_MODEL // (N_QUERY * N_HEAD)
        D_KV = D_HEAD * N_HEAD
        BATCH, SEQ = (2, 256)
        key = jax.random.key(seed)
        ks = jax.random.split(key, 5)
        w_scale = 1.0 / np.sqrt(D_MODEL).astype(np.float32)
        x = jax.random.normal(ks[0], (BATCH, SEQ, D_MODEL), jnp.float32)
        Wq = jax.random.normal(ks[1], (D_MODEL, D_MODEL), jnp.float32) * w_scale
        Wk = jax.random.normal(ks[2], (D_KV, D_MODEL), jnp.float32) * w_scale
        Wv = jax.random.normal(ks[3], (D_KV, D_MODEL), jnp.float32) * w_scale
        memory = jax.random.normal(ks[4], (D_KV, D_KV), jnp.float32) * 0.02
        memory_norm = jnp.ones((D_KV, 1), jnp.float32)
        memory_weight = jnp.ones((1,), jnp.float32)
        return dict(x=x, Wq=Wq, Wk=Wk, Wv=Wv, memory=memory, memory_norm=memory_norm, memory_weight=memory_weight)
    _L0_attn_all = _L0_attn_setup()
    _L0_attn_in = {k: v for k, v in _L0_attn_all.items() if k in ('Wq', 'Wk', 'Wv', 'memory', 'memory_norm', 'memory_weight')}
    del _L0_attn_all

    def _L0_xattn_setup():
        import jax, jax.numpy as jnp
        import numpy as np
        key = jax.random.key(seed)
        ks = jax.random.split(key, 6)
        B, L, N, C, D = (8, 64, 256, 128, 128)
        return {'teacher_logits': jax.random.normal(ks[0], (B, L, N), dtype=jnp.float32), 'teacher_features': jax.random.normal(ks[1], (B, N, C), dtype=jnp.float32), 'Wq': jax.random.normal(ks[2], (D, C), dtype=jnp.float32) * (1.0 / np.sqrt(C)), 'bq': jnp.zeros((D,), dtype=jnp.float32), 'Wk': jax.random.normal(ks[3], (D, C), dtype=jnp.float32) * (1.0 / np.sqrt(C)), 'bk': jnp.zeros((D,), dtype=jnp.float32)}
    _L0_xattn_all = _L0_xattn_setup()
    _L0_xattn_in = {k: v for k, v in _L0_xattn_all.items() if k in ('Wq', 'bq', 'Wk', 'bk')}
    del _L0_xattn_all

    def _L0_ffn_setup():
        import jax, jax.numpy as jnp
        import numpy as np
        BLOCK = 64

        def dequant4bit(q, scale):
            return (q.astype(jnp.float32) - 7.5) * jnp.repeat(scale, BLOCK, axis=1)
        key = jax.random.key(seed)
        ks = jax.random.split(key, 11)
        B, S, D, H, R = (4, 256, 256, 1024, 16)
        return {'x1': jax.random.normal(ks[0], (B, S, D), jnp.float32), 'w_up_q': jax.random.randint(ks[1], (H, D), 0, 16, dtype=jnp.int32), 'w_up_scale': jax.random.uniform(ks[2], (H, D // BLOCK), jnp.float32) * 0.02, 'b_up': jax.random.normal(ks[3], (H,), jnp.float32) * 0.01, 'w_up_lora_a': jax.random.normal(ks[4], (D, R), jnp.float32) * 0.02, 'w_up_lora_b': jax.random.normal(ks[5], (R, H), jnp.float32) * 0.02, 'w_down_q': jax.random.randint(ks[6], (D, H), 0, 16, dtype=jnp.int32), 'w_down_scale': jax.random.uniform(ks[7], (D, H // BLOCK), jnp.float32) * 0.02, 'b_down': jax.random.normal(ks[8], (D,), jnp.float32) * 0.01, 'w_down_lora_a': jax.random.normal(ks[9], (H, R), jnp.float32) * 0.02, 'w_down_lora_b': jax.random.normal(ks[10], (R, D), jnp.float32) * 0.02}
    _L0_ffn_all = _L0_ffn_setup()
    _L0_ffn_in = {k: v for k, v in _L0_ffn_all.items() if k in ('w_up_q', 'w_up_scale', 'b_up', 'w_up_lora_a', 'w_up_lora_b', 'w_down_q', 'w_down_scale', 'b_down', 'w_down_lora_a', 'w_down_lora_b')}
    del _L0_ffn_all
    return {'x': x, 'ctx_1024': ctx_1024, 'L0_attn_Wq': _L0_attn_in['Wq'], 'L0_attn_Wk': _L0_attn_in['Wk'], 'L0_attn_Wv': _L0_attn_in['Wv'], 'L0_attn_memory': _L0_attn_in['memory'], 'L0_attn_memory_norm': _L0_attn_in['memory_norm'], 'L0_attn_memory_weight': _L0_attn_in['memory_weight'], 'L0_xattn_Wq': _L0_xattn_in['Wq'], 'L0_xattn_bq': _L0_xattn_in['bq'], 'L0_xattn_Wk': _L0_xattn_in['Wk'], 'L0_xattn_bk': _L0_xattn_in['bk'], 'L0_ffn_w_up_q': _L0_ffn_in['w_up_q'], 'L0_ffn_w_up_scale': _L0_ffn_in['w_up_scale'], 'L0_ffn_b_up': _L0_ffn_in['b_up'], 'L0_ffn_w_up_lora_a': _L0_ffn_in['w_up_lora_a'], 'L0_ffn_w_up_lora_b': _L0_ffn_in['w_up_lora_b'], 'L0_ffn_w_down_q': _L0_ffn_in['w_down_q'], 'L0_ffn_w_down_scale': _L0_ffn_in['w_down_scale'], 'L0_ffn_b_down': _L0_ffn_in['b_down'], 'L0_ffn_w_down_lora_a': _L0_ffn_in['w_down_lora_a'], 'L0_ffn_w_down_lora_b': _L0_ffn_in['w_down_lora_b']}

def reference(x, ctx_1024, L0_attn_Wq, L0_attn_Wk, L0_attn_Wv, L0_attn_memory, L0_attn_memory_norm, L0_attn_memory_weight, L0_xattn_Wq, L0_xattn_bq, L0_xattn_Wk, L0_xattn_bk, L0_ffn_w_up_q, L0_ffn_w_up_scale, L0_ffn_b_up, L0_ffn_w_up_lora_a, L0_ffn_w_up_lora_b, L0_ffn_w_down_q, L0_ffn_w_down_scale, L0_ffn_b_down, L0_ffn_w_down_lora_a, L0_ffn_w_down_lora_b):
    import jax
    import jax.numpy as jnp

    def _L0_attn_ref(x, Wq, Wk, Wv, memory, memory_norm, memory_weight):
        import jax, jax.numpy as jnp
        import numpy as np
        D_MODEL = 256
        N_QUERY = 4
        N_HEAD = 8
        D_HEAD = D_MODEL // (N_QUERY * N_HEAD)
        D_KV = D_HEAD * N_HEAD
        BATCH, SEQ = (2, 256)
        b, s, d = x.shape
        q = x @ Wq.T
        k = x @ Wk.T
        v = x @ Wv.T
        qh = q.reshape(b, s, N_QUERY, N_HEAD, D_HEAD)
        kh = k.reshape(b, s, N_HEAD, D_HEAD)
        vh = v.reshape(b, s, N_HEAD, D_HEAD)
        scale = np.float32(1.0 / np.sqrt(np.float32(D_HEAD)))
        scores = jnp.einsum('bsqhd,bthd->bqhst', qh, kh) * scale
        probs = jax.nn.softmax(scores, axis=-1)
        a_dot = jnp.einsum('bqhst,bthd->bsqhd', probs, vh)
        a_dot = a_dot.reshape(b, s, N_QUERY * N_HEAD, D_HEAD)
        sigma_q = jax.nn.elu(q.reshape(b, s, N_QUERY, D_KV))
        a_mem = sigma_q @ memory / (sigma_q @ memory_norm)
        a_mem = a_mem.reshape(b, s, N_QUERY * N_HEAD, D_HEAD)
        w = jax.nn.sigmoid(memory_weight)
        out = a_dot * (1.0 - w) + a_mem * w
        return out.reshape(b, s, D_MODEL)

    def _L0_xattn_ref(teacher_logits, teacher_features, Wq, bq, Wk, bk):
        import jax, jax.numpy as jnp
        import numpy as np
        query = jnp.einsum('bnc,dc->bnd', teacher_features, Wq) + bq
        key = jnp.einsum('bnc,dc->bnd', teacher_features, Wk) + bk
        energy = jnp.einsum('bnd,bmd->bnm', query, key)
        attention = jax.nn.softmax(energy, axis=-1)
        x_m = jnp.einsum('bln,bmn->blm', teacher_logits, attention)
        return x_m

    def _L0_ffn_ref(x1, w_up_q, w_up_scale, b_up, w_up_lora_a, w_up_lora_b, w_down_q, w_down_scale, b_down, w_down_lora_a, w_down_lora_b):
        import jax, jax.numpy as jnp
        import numpy as np
        BLOCK = 64

        def dequant4bit(q, scale):
            return (q.astype(jnp.float32) - 7.5) * jnp.repeat(scale, BLOCK, axis=1)
        w_up = dequant4bit(w_up_q, w_up_scale).T
        y1 = x1 @ w_up + b_up + x1 @ w_up_lora_a @ w_up_lora_b
        x2 = jax.nn.relu(y1)
        w_down = dequant4bit(w_down_q, w_down_scale).T
        y2 = x2 @ w_down + b_down + x2 @ w_down_lora_a @ w_down_lora_b
        return y2
    x = _layernorm(x + _L0_attn_ref(x, L0_attn_Wq, L0_attn_Wk, L0_attn_Wv, L0_attn_memory, L0_attn_memory_norm, L0_attn_memory_weight), axis=-1)
    x = _layernorm(x + _L0_xattn_ref(x, ctx_1024, L0_xattn_Wq, L0_xattn_bq, L0_xattn_Wk, L0_xattn_bk), axis=-1)
    x = _layernorm(x + _L0_ffn_ref(x, L0_ffn_w_up_q, L0_ffn_w_up_scale, L0_ffn_b_up, L0_ffn_w_up_lora_a, L0_ffn_w_up_lora_b, L0_ffn_w_down_q, L0_ffn_w_down_scale, L0_ffn_b_down, L0_ffn_w_down_lora_a, L0_ffn_w_down_lora_b), axis=-1)
    return x

_drawn_inputs = setup_inputs


def setup_inputs(seed=0):
    import zlib

    import numpy as np

    out = dict(_drawn_inputs(seed))
    spreads = {'L0_attn_memory_norm': (1.0, 0.2), 'L0_xattn_bq': (0.0, 0.1), 'L0_xattn_bk': (0.0, 0.8)}
    factors = {'L0_ffn_b_up': 7.444,
     'L0_ffn_w_up_lora_a': 2.692,
     'L0_ffn_w_up_lora_b': 2.674,
     'L0_ffn_b_down': 8.0,
     'L0_ffn_w_down_lora_a': 2.728,
     'L0_ffn_w_down_lora_b': 2.82}
    for name, (base, spread) in spreads.items():
        noise = np.random.default_rng([zlib.crc32(name.encode()), seed]).standard_normal(out[name].shape)
        drawn = base * np.exp(spread * noise) if base else spread * noise
        out[name] = jnp.asarray(drawn.astype(out[name].dtype))
    for name, factor in factors.items():
        out[name] = (out[name] * factor).astype(out[name].dtype)
    return out
```

```python
import concourse.bass as bass
from concourse import mybir
from contextlib import ExitStack

import numpy as np


def build_decoder(nc, x, ctx, wq, wk, wv, memory, memory_norm, memory_weight, xwq, xbq, xwk, xbk,
                  up_q, up_scale, up_bias, up_a, up_b, dn_q, dn_scale, dn_bias, dn_a, dn_b, out):
    fp32, fp32r, bf16, i32 = mybir.dt.float32, mybir.dt.float32r, mybir.dt.bfloat16, mybir.dt.int32
    ALU = mybir.AluOpType
    ACT = mybir.ActivationFunctionType
    X = mybir.AxisListType.X

    P = 128
    B, S, D = x.shape
    KV = wk.shape[0]
    G, H = D // KV, 8
    DH = KV // H
    C = ctx.shape[2]
    F = up_q.shape[0]
    R = up_a.shape[1]
    QB = D // up_scale.shape[1]
    HP, HH = H // 2, 2
    QP, QQ = G // 2, 2
    ST, CC = S // P, D // P
    FC = F // P
    TERM_Q = (0, 0, 0, 1, 1, 2)
    TERM_K = (0, 1, 2, 0, 1, 0)
    TERMS = len(TERM_Q)
    HD = HH * DH
    ROWS = TERMS * HD
    MROWS = HH * 2
    UNITS = B * HP
    SUB = 8
    VC = 32
    EPS = 1e-5
    SCALE = float(np.float32(1.0 / np.sqrt(np.float32(DH))))

    q_scratch = nc.dram_tensor("q_scratch", [B, 3, QP, HD, HP * QQ * S], bf16, kind="Internal").ap()
    k_scratch = nc.dram_tensor("k_scratch", [B, 3, HD, HP * HH * S], bf16, kind="Internal").ap()

    stack = ExitStack()
    with stack:
        def sb(name, shape, dt):
            return stack.enter_context(nc.sbuf_tensor(name, shape, dt))

        def sem(name):
            return stack.enter_context(nc.semaphore(name))

        ident = sb("ident", [P, P], fp32)
        identb = sb("identb", [P, P], bf16)
        pick = sb("pick", [KV, P], fp32)
        group_mask = sb("group_mask", [P, QQ], fp32)
        head_mask = sb("head_mask", [2 * 32, HH], fp32)
        xs = sb("xs", [P, B, ST, D], fp32)
        wq_nat = sb("wq_nat", [P, CC, D], fp32)
        wkv_nat = sb("wkv_nat", [P, D], fp32)
        wqT = sb("wqT", [P, CC, QP, P], fp32)
        wkvT = sb("wkvT", [P, CC, P], fp32)
        mem_nat = sb("mem_nat", [KV, KV + 1], fp32)
        mem_rhs = sb("mem_rhs", [P, QQ, KV + 1], fp32)
        mix = sb("mix", [P, 8], fp32)
        QT = sb("QT", [P, B, QP, HP, QQ, S], bf16)
        KT = sb("KT", [P, B, HP, HH, S], bf16)
        V = sb("V", [P, B, ST, H, VC], fp32)
        xattnT = sb("xattnT", [P, B, ST, S], fp32)
        energy = sb("energy", [P, ST, S], fp32)
        energy_stat = sb("energy_stat", [P, B, 3, ST], fp32)
        xw_nat = sb("xw_nat", [P, 2, C], fp32)
        xwT = sb("xwT", [P, 2, C], fp32)
        xb = sb("xb", [P, 2], fp32)
        upscale = sb("upscale", [P, FC, D // QB], fp32)
        dnscale = sb("dnscale", [P, CC, F // QB], fp32)
        upbias = sb("upbias", [P, FC], fp32)
        dnbias = sb("dnbias", [P, D], fp32)
        lora_up_a = sb("lora_up_a", [P, CC, R], fp32)
        lora_dn_a = sb("lora_dn_a", [P, FC, R], fp32)
        lora_up_b = sb("lora_up_b", [R, F], fp32)
        up_hi = sb("up_hi", [P, CC, F], fp32r)
        up_lo = sb("up_lo", [P, CC, F], fp32r)
        x2_hi = sb("x2_hi", [P, CC, S], fp32r)
        x2_lo = sb("x2_lo", [P, CC, S], fp32r)
        maxes = sb("maxes", [P, 2, ST, QP, QQ, HH], fp32)
        max_parts = sb("max_parts", [P, 2, ST, G, HH, 2], bf16)
        maxT = sb("maxT", [G * MROWS, 2, S], bf16)
        rec = sb("rec", [P, 2, 16], fp32)
        memrec = sb("memrec", [P, G], fp32)
        memterm = sb("memterm", [P, D], fp32)
        stats = sb("stats", [P, ST, 6], fp32)
        moments = sb("moments", [P, ST, 2], fp32)
        rstd = sb("rstd", [P, ST, 1], fp32)
        half = sb("half", [P, ST, 1], fp32)

        probs = sb("probs", [P, 3 * (SUB // 2), 512], fp32)
        avT = sb("avT", [P, 2, 512], fp32)
        adot = sb("adot", [P, 2, ST, D], fp32)

        with nc.sbuf_tensor("early", [P, 2 * (FC * S + FC * D)], fp32) as early:
            up_raw = early[:, 0:FC * D].rearrange("p (a b) -> p a b", a=FC)
            dn_raw = early[:, FC * S:FC * S + CC * F].rearrange("p (a b) -> p a b", a=CC)
            late = 2 * FC * S
            ctx_nat = early[:, late:late + 1024].rearrange("p (a b) -> p a b", a=B * ST)
            ctxT = early[:, late + 1024:late + 2048]
            xq = early[:, late + 2048:late + 3072]
            xk = early[:, late + 3072:late + 4096]
        y_hi = sb("y_hi", [P, FC, S], fp32r)
        y_lo = sb("y_lo", [P, FC, S], fp32r)
        dn_hi = sb("dn_hi", [P, FC, D], fp32r)
        dn_lo = sb("dn_lo", [P, FC, D], fp32r)

        arena_b = sb("arena_b", [P, 6656], fp32)
        xT = arena_b[:, 0:1024].rearrange("p (n c s) -> p n c s", n=2, c=CC)
        qf = arena_b[:, 1024:2048].rearrange("p (n c s) -> p n c s", n=2, c=QP)
        q_neg = arena_b[:, 2048:2560].rearrange("p (c s) -> p c s", c=QP)
        sigma = arena_b[:, 2560:3072].rearrange("p (c s) -> p c s", c=QP)
        kf = arena_b[0:KV, 3072:3584].rearrange("p (c s) -> p c s", c=HH)
        q_parts = arena_b[:, 3584:4352].bitcast(bf16).rearrange("p (n c s) -> p n c s", n=3, c=QP)
        k_parts = arena_b[0:KV, 4352:5120].bitcast(bf16).rearrange("p (n c s) -> p n c s", n=3, c=HH)
        lora_dn_aT = arena_b[0:R, 5120:6144]
        lora_up_aT = arena_b[0:R, 6144:6400]
        lora_dn_b = arena_b[0:R, 6400:6656]
        x1 = arena_b[:, 2048:2560].rearrange("p (t d) -> p t d", t=ST)
        x1T = arena_b[:, 2560:3072].rearrange("p (c s) -> p c s", c=CC)
        x2 = arena_b[:, 3072:3584].rearrange("p (t d) -> p t d", t=ST)
        x2T = arena_b[:, 3584:4096].rearrange("p (c s) -> p c s", c=CC)
        yf = arena_b[:, 4096:5120].rearrange("p (n f) -> p n f", n=2)
        x3 = arena_b[:, 5120:5632].rearrange("p (t d) -> p t d", t=ST)
        pre = arena_b[:, 5632:6144].rearrange("p (t d) -> p t d", t=ST)
        x2b = arena_b[:, 6144:6656].rearrange("p (t d) -> p t d", t=ST)
        rest = sb("rest", [P, 512], fp32)

        def bank(name):
            return stack.enter_context(nc.psum_tensor(name, [P, 512], fp32))

        exp_bank = [bank(f"exp_bank{i}") for i in range(3)]
        max_bank = [bank(f"max_bank{i}") for i in range(2)]
        pv_bank = bank("pv_bank")
        shared = [bank(f"shared{i}") for i in range(2)]

        ahead = [("wqT", 0), ("wkvT", 0), ("xT", 0), ("q", 0), ("kv", 0), ("mem_rhs", 0), ("xwT", 0), ("ctxT", 0),
                 ("xT", 1), ("mem", (0, 0)), ("mem", (0, 1)), ("q", 1), ("kv", 1), ("xq", 0), ("xk", 0), ("ctxT", 1),
                 ("energy", 0), ("xT", 2), ("mem", (1, 0)), ("xattnT", 0), ("mem", (1, 1)),
                 ("q", 2), ("kv", 2), ("xq", 1), ("xk", 1), ("energy", 1), ("loraT", 0), ("xattnT", 1),
                 ("mem", (2, 0)), ("mem", (2, 1)), ("energy", 2), ("xT", 3), ("xattnT", 2), ("q", 3), ("kv", 3),
                 ("energy", 3), ("loraT", 1), ("loraT", 2), ("mem", (3, 0)), ("xattnT", 3), ("mem", (3, 1)),
                 *[("up_w", j) for j in range(4)], *[("dn_w", j) for j in range(4)]]
        BEFORE = 13

        def post(b):
            return [("ln1_stats", b), ("ln1", b), ("x1T", b), ("cross", b), ("ln2_stats", b), ("ln2", b), ("x2T", b),
                    *[("up", (b, j)) for j in range(FC // 2)],
                    *[("down", (b, t)) for t in range(ST)], ("ln3_stats", b), ("ln3", b)]

        order, fill = ahead[:BEFORE], ahead[BEFORE:]

        def gap(n=1):
            for _ in range(min(n, len(fill))):
                order.append(fill.pop(0))

        for u in range(2):
            for i in range(SUB):
                order.append(("max", (u, i)))
                if i % 2:
                    gap()
            if u == 1:
                order.append(("maxT", 0))
        for u in range(UNITS):
            for i in range(SUB):
                order.append(("exp", (u, i)))
                if u + 2 < UNITS:
                    order.append(("max", (u + 2, i)))
                if i == 2 and u >= 1:
                    order.append(("pv", (u - 1, 1)))
                if i == 6:
                    order.append(("pv", (u, 0)))
                if i == 1 and u + 1 < UNITS:
                    order.append(("maxT", u + 1))
                if i == 5 and u >= 1:
                    order.append(("spread", u - 1))
                    if (u - 1) % HP == HP - 1:
                        fill += post((u - 1) // HP)
                gap(1 if u <= HP or i % 2 == 0 else 0)
        last = post(B - 1)
        order += [("pv", (UNITS - 1, 1))] + fill[:1] + [("spread", UNITS - 1)] + fill[1:] + last

        def a_step_later(stages):
            held = []
            for key in stages:
                if key[0] not in ("exp", "max", "pv", "maxT"):
                    yield from held
                    held = [key]
                else:
                    yield key
            yield from held

        behind = order

        sems = {}
        loads = ("wqkv", "memory", "context", "cross_w", "up_w", "dn_w", "lora", "biases")
        by_pool = ("pool_step", "identities", "constants", "k_rows", "v_zeroed", "up_dequant", "dn_dequant",
                   "q_split", "residual", "max_split", "attn_added", "rstd_ready", "x2_lo_done", "y_lo_done", "x2b_ready")
        by_act = ("wqT_ready", "wkvT_ready", "xT_ready", "qf_ready", "q_exp", "kf_ready", "v_ready", "xwT_ready",
                  "ctxT_ready", "xq_ready", "xk_ready", "loraT_ready", "energy_exp", "xattnT_ready", "w_hi_ready",
                  "mix_exp", "probs_ready", "maxT_ready", "avT_ready", "x1T_ready", "x2T_ready", "yf_ready")
        by_dve = ("dve_step", "masks", "mix_ready", "mem_rhs_ready", "q_parts_ready", "k_parts_ready", "sigma_ready",
                  "memterm_ready", "energy_max", "xattn_ready", "w_ready", "max_taken", "adot_ready", "moments_ready",
                  "x1_ready", "x2_ready", "cross_added", "x2_hi_done", "y_hi_done", "down_added", "x3_ready")
        by_pe = ("exp_scores", "max_scores", "pv_done")
        for name in (*("ld_" + n for n in loads), *by_pool, *by_act, *by_dve, *by_pe):
            sems[name] = sem(name)
        ld_x = [sem(f"ld_x{b}") for b in range(B)]
        q_written = [sem(f"q_written{b}") for b in range(B)]
        k_written = [sem(f"k_written{b}") for b in range(B)]
        qk_loaded = [sem(f"qk_loaded{b}") for b in range(B)]
        max_loaded = [sem(f"max_loaded{i}") for i in range(2)]
        stored = sem("stored")

        shared_full = [sem(f"shared_full{i}") for i in range(2)]
        release = {
            "wqT": lambda n: (sems["wqT_ready"], CC * QP), "wkvT": lambda n: (sems["wkvT_ready"], CC + 1),
            "xT": lambda b: (sems["xT_ready"], b + 1), "q": lambda b: (sems["qf_ready"], b + 1),
            "kv": lambda b: (sems["v_ready"], ST * (b + 1)), "mem_rhs": lambda n: (sems["mem_rhs_ready"], 2 * QQ),
            "mem": lambda n: (sems["memterm_ready"], ST * n[0] + n[1] + 1), "xwT": lambda n: (sems["xwT_ready"], 1),
            "ctxT": lambda n: (sems["ctxT_ready"], n + 1), "xq": lambda n: (sems["xq_ready"], n + 1),
            "xk": lambda n: (sems["xk_ready"], n + 1), "loraT": lambda n: (sems["loraT_ready"], n + 1),
            "energy": lambda b: (sems["energy_exp"], ST * (b + 1)), "xattnT": lambda b: (sems["xattnT_ready"], b + 1),
            "up_w": lambda j: (sems["w_ready"], j + 1), "dn_w": lambda j: (sems["w_ready"], 4 + j + 1),
            "maxT": lambda u: (sems["maxT_ready"], u + 1), "spread": lambda u: (sems["adot_ready"], ST * (u + 1)),
            "x1T": lambda b: (sems["x1T_ready"], b + 1), "cross": lambda b: (sems["cross_added"], b + 1),
            "x2T": lambda b: (sems["x2T_ready"], b + 1), "up": lambda n: (sems["yf_ready"], 2 * (n[0] * (FC // 2) + n[1] + 1)),
            "down": lambda n: (sems["down_added"], ST * n[0] + n[1] + 1),
        }
        in_turn = [k for k in order if k[0] in release]
        SLOT = {key: i for i, key in enumerate(in_turn)}

        def in_bank(eng, stage, n=0):
            i = SLOT[stage, n]
            eng.wait_ge(shared_full[i % 2], i // 2 + 1)
            return shared[i % 2]

        block = stack.enter_context(nc.Block())

        @block.sync
        def _(sp):
            sp.dma_start(wq_nat[:, :, :], wq.rearrange("(c p) d -> p c d", p=P)).then_inc(sems["ld_wqkv"], 16)
            sp.dma_start(xs[:, 0], x[0].rearrange("(t p) d -> p t d", p=P)).then_inc(ld_x[0], 16)
            sp.dma_start(wkv_nat[0:KV, :], wk).then_inc(sems["ld_wqkv"], 16)
            sp.dma_start(wkv_nat[KV:2 * KV, :], wv).then_inc(sems["ld_wqkv"], 16)
            for b in range(1, B):
                sp.dma_start(xs[:, b], x[b].rearrange("(t p) d -> p t d", p=P)).then_inc(ld_x[b], 16)
            sp.dma_start(up_raw.bitcast(i32), up_q.rearrange("(c p) d -> p c d", p=P)).then_inc(sems["ld_up_w"], 16)
            sp.dma_start(upscale[:, :, :], up_scale.rearrange("(c p) k -> p c k", p=P)).then_inc(sems["ld_up_w"], 16)
            sp.dma_start(ctx_nat, ctx.rearrange("b (t p) c -> p (b t) c", p=P)).then_inc(sems["ld_context"], 16)
            for stage, n in behind:
                if stage == "kv":
                    b = n
                    sp.wait_ge(sems["q_parts_ready"], b + 1)
                    for g in range(QP):
                        sp.dma_start(q_scratch[b, :, g].rearrange("n r (a t) -> (r a) n t", t=S),
                                     q_parts[:, :, g, :]).then_inc(q_written[b], 16)
                    sp.wait_ge(sems["k_parts_ready"], b + 1)
                    sp.dma_start(k_scratch[b].rearrange("n r (a t) -> (r a) n t", a=HP),
                                 k_parts.rearrange("p n c t -> p n (c t)")).then_inc(k_written[b], 16)
                if stage == "mem" and n[1] == 0:
                    b = n[0]
                    sp.wait_ge(q_written[b], 16 * QP)
                    sp.wait_ge(k_written[b], 16)
                    for part in range(3):
                        terms = TERM_Q.count(part)
                        rows = slice(TERM_Q.index(part) * HD, (TERM_Q.index(part) + terms) * HD)
                        for g in range(QP):
                            sp.dma_start(QT[rows, b, g].rearrange("p a c t -> p (a c t)"),
                                         q_scratch[b, part, g].unsqueeze(0).broadcast_to([terms, HD, HP * QQ * S]))\
                                .then_inc(qk_loaded[b], 16)
                        sp.dma_start(KT[rows, b].rearrange("p a c t -> p (a c t)"),
                                     k_scratch[b, 0:terms].rearrange("n r t -> (n r) t")).then_inc(qk_loaded[b], 16)
                if stage == "maxT":
                    u = n
                    b, hp = divmod(u, HP)
                    sp.wait_ge(sems["maxT_ready"], u + 1)
                    for g in range(G):
                        sp.dma_start(QT[ROWS:ROWS + MROWS, b, g // QQ, hp, g % QQ, :],
                                     maxT[g * MROWS:(g + 1) * MROWS, u % 2, :]).then_inc(max_loaded[u % 2], 16)
                if stage == "ln3":
                    sp.wait_ge(sems["x3_ready"], ST * (n + 1))
                    sp.dma_start(out[n].rearrange("(t p) d -> p t d", p=P), x3).then_inc(stored, 16)
            sp.wait_ge(stored, 16 * B)

        @block.gpsimd
        def _(pool):
            steps = [0]

            def step(ins):
                steps[0] += 1
                ins.then_inc(sems["pool_step"], 1)
                pool.wait_ge(sems["pool_step"], steps[0])

            for m in (ident, identb):
                step(pool.memset(m[:, :], 0.0))
                pool.affine_select(out=m[:, :], in_=m[:, :], compare_op=ALU.not_equal, fill=1.0, base=0,
                                   pattern=[[-1, P]], channel_multiplier=1).then_inc(sems["identities"], 1)
            pool.dma_start(mix[:, 0:1], memory_weight.partition_broadcast(P)).then_inc(sems["ld_memory"], 16)
            pool.dma_start(mem_nat[:, 0:KV], memory).then_inc(sems["ld_memory"], 16)
            pool.dma_start(mem_nat[:, KV:KV + 1], memory_norm).then_inc(sems["ld_memory"], 16)
            pool.dma_start(xw_nat[:, 0, :], xwq).then_inc(sems["ld_cross_w"], 16)
            pool.dma_start(xw_nat[:, 1, :], xwk).then_inc(sems["ld_cross_w"], 16)
            pool.dma_start(xb[:, 0:1], xbq.rearrange("(p o) -> p o", o=1)).then_inc(sems["ld_cross_w"], 16)
            pool.dma_start(xb[:, 1:2], xbk.rearrange("(p o) -> p o", o=1)).then_inc(sems["ld_cross_w"], 16)
            pool.dma_start(dn_raw.bitcast(i32), dn_q.rearrange("(c p) f -> p c f", p=P)).then_inc(sems["ld_dn_w"], 16)
            pool.dma_start(dnscale[:, :, :], dn_scale.rearrange("(c p) k -> p c k", p=P)).then_inc(sems["ld_dn_w"], 16)
            pool.dma_start(lora_up_a[:, :, :], up_a.rearrange("(c p) r -> p c r", p=P)).then_inc(sems["ld_lora"], 16)
            pool.dma_start(lora_dn_a[:, :, :], dn_a.rearrange("(c p) r -> p c r", p=P)).then_inc(sems["ld_lora"], 16)
            pool.dma_start(lora_up_b[:, :], up_b).then_inc(sems["ld_lora"], 16)
            pool.dma_start(lora_dn_b, dn_b).then_inc(sems["ld_lora"], 16)
            pool.dma_start(upbias[:, :], up_bias.rearrange("(c p) -> p c", p=P),
                           allow_slow_non_contiguous=True).then_inc(sems["ld_biases"], 16)
            pool.dma_start(dnbias[:, :], dn_bias.partition_broadcast(P)).then_inc(sems["ld_biases"], 16)
            pool.memset(half[:, :, :], -0.5).then_inc(sems["constants"], 1)

            def dequantise(raw, scale, loaded, done):
                pool.wait_ge(loaded, 32)
                flat = raw.rearrange("p a b -> p (a b)")
                step(pool.tensor_scalar(flat, flat.bitcast(i32), -7.5, 1.0, ALU.add, ALU.mult))
                blocks = flat.rearrange("p (k q) -> p k q", q=QB)
                sc = scale[:, :, :].rearrange("p a k -> p (a k)").unsqueeze(2)
                pool.tensor_tensor(blocks, blocks, sc.broadcast_to(blocks.shape), ALU.mult).then_inc(done, 1)

            def inverse_root(count):
                pool.wait_ge(sems["moments_ready"], count)
                step(pool.tensor_scalar(rstd[:, :, :], moments[:, :, 1:2], EPS, 1.0, ALU.add, ALU.mult))
                pool.tensor_tensor(rstd[:, :, :], rstd[:, :, :], half[:, :, :], ALU.pow).then_inc(sems["rstd_ready"], 1)

            pool.wait_ge(sems["constants"], 1)
            for stage, n in behind:
                if stage == "q":
                    b = n
                    pool.wait_ge(sems["qf_ready"], b + 1)
                    if b >= 1:
                        in_bank(pool, "mem", (b - 1, ST - 1))
                    step(pool.tensor_scalar(q_neg, qf[:, b % 2], 0.0, 1.0, ALU.min, ALU.mult))
                    pool.tensor_tensor(sigma, qf[:, b % 2], q_neg, ALU.subtract).then_inc(sems["q_split"], 1)
                if stage == "mem":
                    b, t = n
                    pool.wait_ge(sems["memterm_ready"], ST * b + t + 1)
                    in_bank(pool, "xT", b)
                    pool.tensor_tensor(xs[:, b, t], xs[:, b, t], memterm[:, :], ALU.add).then_inc(sems["residual"], 1)
                if stage == "mem" and n == (0, 1):
                    dequantise(up_raw, upscale, sems["ld_up_w"], sems["up_dequant"])
                if stage == "mem" and n == (3, 1):
                    dequantise(dn_raw, dnscale, sems["ld_dn_w"], sems["dn_dequant"])
                if stage == "max" and n[1] == SUB - 1:
                    u = n[0]
                    pool.wait_ge(sems["max_taken"], SUB * (u + 1))
                    if u >= 2:
                        in_bank(pool, "maxT", u - 2)
                    parts = max_parts[:, u % 2].rearrange("p t g h n -> p (t g h) n")
                    m = maxes[:, u % 2].rearrange("p t g q h -> p (t g q h)")
                    step(pool.tensor_copy(parts[:, :, 0], m))
                    pool.tensor_tensor(parts[:, :, 1], m, parts[:, :, 0], ALU.subtract).then_inc(sems["max_split"], 1)
                if stage == "ln1_stats":
                    b = n
                    pool.wait_ge(sems["adot_ready"], ST * HP * (b + 1))
                    pool.wait_ge(sems["residual"], ST * B)
                    if b >= 1:
                        pool.wait_ge(sems["x3_ready"], ST * b)
                    pool.tensor_tensor(pre, xs[:, b], adot[:, b % 2], ALU.add).then_inc(sems["attn_added"], 1)
                    inverse_root(3 * b + 1)
                if stage == "ln2_stats":
                    inverse_root(3 * n + 2)
                if stage == "ln3_stats":
                    inverse_root(3 * n + 3)
                if stage == "ln2":
                    b = n
                    pool.wait_ge(sems["x2_ready"], ST * (b + 1))
                    pool.wait_ge(sems["ld_biases"], 32)
                    pool.tensor_tensor(x2b, x2, dnbias[:, :].unsqueeze(1).broadcast_to([P, ST, D]), ALU.add)\
                        .then_inc(sems["x2b_ready"], 1)
                if stage == "x2T":
                    pool.wait_ge(sems["x2_hi_done"], n + 1)
                    pool.tensor_tensor(x2_lo[:, :, :], x2T, x2_hi[:, :, :].bitcast(fp32), ALU.subtract)\
                        .then_inc(sems["x2_lo_done"], 1)
                if stage == "up":
                    b, j = n
                    i = b * (FC // 2) + j
                    pool.wait_ge(sems["y_hi_done"], i + 1)
                    pool.tensor_tensor(y_lo[:, 2 * j:2 * j + 2].rearrange("p c t -> p (c t)"), yf[:, i % 2],
                                       y_hi[:, 2 * j:2 * j + 2].rearrange("p c t -> p (c t)").bitcast(fp32),
                                       ALU.subtract).then_inc(sems["y_lo_done"], 1)

        @block.scalar
        def _(act):
            for stage, n in behind:
                if stage == "wqT":
                    src = in_bank(act, stage)[:, :].rearrange("p (c g q a r) -> p c g r a q", c=CC, g=QP, q=QQ, a=HP)
                    for c in range(CC):
                        for g in range(QP):
                            act.activation(wqT[:, c, g].rearrange("p (r a q) -> p r a q", a=HP, q=QQ),
                                           src[:, c, g], ACT.Copy).then_inc(sems["wqT_ready"], 1)
                if stage == "wkvT":
                    src = in_bank(act, stage)[:, 0:CC * P].rearrange("p (c o) -> p c o", c=CC)
                    for c in range(CC):
                        act.activation(wkvT[:, c, 0:KV].rearrange("p (r a) -> p r a", a=HP),
                                       src[:, c, 0:KV].rearrange("p (a r) -> p r a", a=HP), ACT.Copy)\
                            .then_inc(sems["wkvT_ready"], 1)
                    act.activation(wkvT[:, :, KV:P], src[:, :, KV:P], ACT.Copy).then_inc(sems["wkvT_ready"], 1)
                if stage == "xT" and n == 0:
                    act.wait_ge(sems["ld_memory"], 48)
                    act.activation(mix[:, 1:2], mix[:, 0:1], ACT.Exp, scale=-1.0).then_inc(sems["mix_exp"], 1)
                if stage == "xT":
                    if n >= 2:
                        in_bank(act, "kv", n - 2)
                    ps = in_bank(act, stage, n)
                    act.activation(xT[:, n % 2].rearrange("p c t -> p (c t)"), ps[:, :], ACT.Copy)\
                        .then_inc(sems["xT_ready"], 1)
                if stage == "q":
                    if n >= 2:
                        act.wait_ge(sems["q_parts_ready"], n - 1)
                        act.wait_ge(sems["q_split"], n - 1)
                    ps = in_bank(act, stage, n)
                    act.activation(qf[:, n % 2].rearrange("p c t -> p (c t)"), ps[:, :], ACT.Copy)\
                        .then_inc(sems["qf_ready"], 1)
                if stage == "kv":
                    ps = in_bank(act, stage, n)
                    if n == 0:
                        act.wait_ge(sems["masks"], 5)
                        act.wait_ge(sems["mix_ready"], 3)
                        act.wait_ge(sems["v_zeroed"], 1)
                    if n >= 1:
                        act.wait_ge(sems["k_parts_ready"], n)
                    for hh in range(HH):
                        act.activation(kf[:, hh], ps[0:KV, 0:S], ACT.Copy, scale=head_mask[:, hh:hh + 1])\
                            .then_inc(sems["kf_ready"], 1)
                    for t in range(ST):
                        act.activation(V[:, n, t, :, 0:DH],
                                       ps[:, S + t * KV:S + (t + 1) * KV].rearrange("p (h d) -> p h d", h=H),
                                       ACT.Copy, scale=mix[:, 4:5]).then_inc(sems["v_ready"], 1)
                    act.wait_ge(sems["q_split"], n + 1)
                    act.activation(q_neg, q_neg, ACT.Exp).then_inc(sems["q_exp"], 1)
                if stage == "xwT":
                    ps = in_bank(act, stage)
                    act.activation(xwT[:, :, :].rearrange("p c t -> p (c t)"), ps[:, 0:2 * C], ACT.Copy)\
                        .then_inc(sems["xwT_ready"], 1)
                if stage == "ctxT":
                    ps = in_bank(act, stage, n)
                    act.activation(ctxT[:, n * 512:(n + 1) * 512], ps[:, :], ACT.Copy).then_inc(sems["ctxT_ready"], 1)
                if stage in ("xq", "xk"):
                    ps = in_bank(act, stage, n)
                    to, k, done = (xq, 0, sems["xq_ready"]) if stage == "xq" else (xk, 1, sems["xk_ready"])
                    act.activation(to[:, n * 512:(n + 1) * 512], ps[:, :], ACT.Identity, bias=xb[:, k:k + 1])\
                        .then_inc(done, 1)
                if stage == "loraT":
                    ps = in_bank(act, stage, n)
                    to = lora_up_aT if n == 0 else lora_dn_aT[:, (n - 1) * 512:n * 512]
                    act.activation(to, ps[0:R, 0:to.shape[1]], ACT.Copy).then_inc(sems["loraT_ready"], 1)
                if stage == "energy":
                    b = n
                    act.wait_ge(sems["energy_max"], b + 1)
                    if b >= 1:
                        in_bank(act, "xattnT", b - 1)
                    ps = in_bank(act, stage, b)
                    for t in range(ST):
                        act.activation(energy[:, t], ps[:, t * S:(t + 1) * S], ACT.Exp,
                                       bias=energy_stat[:, b, 0, t:t + 1],
                                       accum_out=energy_stat[:, b, 1, t:t + 1]).then_inc(sems["energy_exp"], 1)
                if stage == "xattnT":
                    ps = in_bank(act, stage, n)
                    act.activation(xattnT[:, n].rearrange("p c t -> p (c t)"), ps[:, :], ACT.Copy)\
                        .then_inc(sems["xattnT_ready"], 1)
                if stage == "up_w":
                    ps = in_bank(act, stage, n)
                    c, half_f = divmod(n, 2)
                    act.activation(up_hi[:, c, half_f * 512:(half_f + 1) * 512], ps[:, :], ACT.Copy)\
                        .then_inc(sems["w_hi_ready"], 1)
                if stage == "dn_w":
                    ps = in_bank(act, stage, n)
                    act.activation(dn_hi[:, 2 * n:2 * n + 2].rearrange("p c t -> p (c t)"), ps[:, :], ACT.Copy)\
                        .then_inc(sems["w_hi_ready"], 1)
                if stage == "maxT":
                    u = n
                    ps = in_bank(act, stage, u)
                    if u >= 2:
                        act.wait_ge(max_loaded[u % 2], 16 * G * (u // 2))
                    act.activation(maxT[:, u % 2, :], ps[0:G * MROWS, :].bitcast(bf16)[:, 0:S], ACT.Copy)\
                        .then_inc(sems["maxT_ready"], 1)
                if stage == "exp":
                    u, i = n
                    k = u * SUB + i
                    act.wait_ge(sems["exp_scores"], k + 1)
                    h, j = divmod(k, QP * HH)
                    if h >= 3 and j == 0:
                        act.wait_ge(sems["pv_done"], h - 2)
                    act.activation(probs[:, (h % 3) * QP * HH + j], exp_bank[k % 3][:, :], ACT.Exp, scale=SCALE)\
                        .then_inc(sems["probs_ready"], 1)
                if stage == "pv" and n[1] == ST - 1:
                    u = n[0]
                    act.wait_ge(sems["pv_done"], ST * (u + 1))
                    if u >= 2:
                        in_bank(act, "spread", u - 2)
                    act.activation(avT[:, u % 2], pv_bank[:, :], ACT.Copy).then_inc(sems["avT_ready"], 1)
                if stage == "x1T":
                    if n >= 1:
                        in_bank(act, "cross", n - 1)
                    ps = in_bank(act, stage, n)
                    act.activation(x1T.rearrange("p c t -> p (c t)"), ps[:, :], ACT.Copy).then_inc(sems["x1T_ready"], 1)
                if stage == "x2T":
                    if n >= 1:
                        act.wait_ge(sems["x2_lo_done"], n)
                    ps = in_bank(act, stage, n)
                    act.activation(x2T.rearrange("p c t -> p (c t)"), ps[:, :], ACT.Copy).then_inc(sems["x2T_ready"], 1)
                if stage == "up":
                    b, j = n
                    i = b * (FC // 2) + j
                    if i == 0:
                        act.wait_ge(sems["ld_biases"], 32)
                    if i >= 2:
                        act.wait_ge(sems["y_lo_done"], i - 1)
                    ps = in_bank(act, stage, n)
                    for a in range(2):
                        act.activation(yf[:, i % 2, a * S:(a + 1) * S], ps[:, a * S:(a + 1) * S], ACT.Relu,
                                       bias=upbias[:, 2 * j + a:2 * j + a + 1]).then_inc(sems["yf_ready"], 1)

        @block.tensor
        def _(pe):
            def claim(stage, n=0):
                i = SLOT[stage, n]
                if i >= 2:
                    before, m = in_turn[i - 2]
                    pe.wait_ge(*release[before](m))
                return shared[i % 2], shared_full[i % 2]

            def turn(to, src, n=P):
                return pe.transpose(to, src, ident[0:n, 0:n])

            pe.wait_ge(sems["identities"], 2)
            for stage, n in order:
                if stage == "wqT":
                    pe.wait_ge(sems["ld_wqkv"], 48)
                    ps, full = claim(stage)
                    for c in range(CC):
                        for o in range(CC):
                            last = turn(ps[:, c * D + o * P:c * D + (o + 1) * P], wq_nat[:, o, c * P:(c + 1) * P])
                    last.then_inc(full, 1)
                if stage == "wkvT":
                    ps, full = claim(stage)
                    for c in range(CC):
                        last = turn(ps[:, c * P:(c + 1) * P], wkv_nat[:, c * P:(c + 1) * P])
                    last.then_inc(full, 1)
                if stage == "xT":
                    pe.wait_ge(ld_x[n], 16)
                    ps, full = claim(stage, n)
                    for c in range(CC):
                        for t in range(ST):
                            last = turn(ps[:, c * S + t * P:c * S + (t + 1) * P], xs[:, n, t, c * P:(c + 1) * P])
                    last.then_inc(full, 1)
                if stage == "q":
                    pe.wait_ge(sems["xT_ready"], n + 1)
                    pe.wait_ge(sems["wqT_ready"], CC * QP)
                    ps, full = claim(stage, n)
                    for g in range(QP):
                        for c in range(CC):
                            last = pe.matmul(ps[:, g * S:(g + 1) * S], wqT[:, c, g, :], xT[:, n % 2, c, :],
                                             start=c == 0, stop=c == CC - 1)
                    last.then_inc(full, 1)
                if stage == "kv":
                    pe.wait_ge(sems["wkvT_ready"], CC + 1)
                    ps, full = claim(stage, n)
                    for c in range(CC):
                        pe.matmul(ps[0:KV, 0:S], wkvT[:, c, 0:KV], xT[:, n % 2, c, :], start=c == 0, stop=c == CC - 1)
                    for t in range(ST):
                        for c in range(CC):
                            last = pe.matmul(ps[:, S + t * KV:S + (t + 1) * KV], xT[:, n % 2, c, t * P:(t + 1) * P],
                                             wkvT[:, c, KV:P], start=c == 0, stop=c == CC - 1)
                    last.then_inc(full, 1)
                if stage == "mem_rhs":
                    pe.wait_ge(sems["ld_memory"], 48)
                    ps, full = claim(stage)
                    pe.wait_ge(sems["masks"], 6)
                    pe.matmul(ps[:, 0:KV + 1], pick[:, :], mem_nat[:, :], start=True, stop=True).then_inc(full, 1)
                if stage == "mem":
                    b, t = n
                    pe.wait_ge(sems["mem_rhs_ready"], 2 * QQ)
                    pe.wait_ge(sems["sigma_ready"], b + 1)
                    ps, full = claim(stage, n)
                    width = QQ * (KV + 1)
                    for g in range(QP):
                        last = pe.matmul(ps[:, g * width:(g + 1) * width], sigma[:, g, t * P:(t + 1) * P],
                                         mem_rhs[:, :, :].rearrange("p q e -> p (q e)"), start=True, stop=True)
                    last.then_inc(full, 1)
                if stage == "xwT":
                    pe.wait_ge(sems["ld_cross_w"], 64)
                    ps, full = claim(stage)
                    for k in range(2):
                        last = turn(ps[:, k * C:(k + 1) * C], xw_nat[:, k, :])
                    last.then_inc(full, 1)
                if stage == "ctxT":
                    pe.wait_ge(sems["ld_context"], 16)
                    ps, full = claim(stage, n)
                    for k in range(4):
                        last = turn(ps[:, k * P:(k + 1) * P], ctx_nat[:, 4 * n + k, :])
                    last.then_inc(full, 1)
                if stage in ("xq", "xk"):
                    pe.wait_ge(sems["xwT_ready"], 1)
                    pe.wait_ge(sems["ctxT_ready"], n + 1)
                    ps, full = claim(stage, n)
                    pe.matmul(ps[:, :], xwT[:, 0 if stage == "xq" else 1, :], ctxT[:, n * 512:(n + 1) * 512],
                              start=True, stop=True).then_inc(full, 1)
                if stage == "loraT":
                    pe.wait_ge(sems["ld_lora"], 64)
                    ps, full = claim(stage, n)
                    tiles = [lora_up_a[:, c, :] for c in range(CC)] if n == 0 else \
                        [lora_dn_a[:, 4 * (n - 1) + k, :] for k in range(4)]
                    for k, tile in enumerate(tiles):
                        last = turn(ps[0:R, k * P:(k + 1) * P], tile)
                    last.then_inc(full, 1)
                if stage == "energy":
                    pe.wait_ge(sems["xq_ready"], n // 2 + 1)
                    pe.wait_ge(sems["xk_ready"], n // 2 + 1)
                    ps, full = claim(stage, n)
                    for t in range(ST):
                        last = pe.matmul(ps[:, t * S:(t + 1) * S], xq[:, n * S + t * P:n * S + (t + 1) * P],
                                         xk[:, n * S:(n + 1) * S], start=True, stop=True)
                    last.then_inc(full, 1)
                if stage == "xattnT":
                    pe.wait_ge(sems["xattn_ready"], ST * (n + 1))
                    ps, full = claim(stage, n)
                    for c in range(ST):
                        for t in range(ST):
                            last = turn(ps[:, c * S + t * P:c * S + (t + 1) * P], energy[:, t, c * P:(c + 1) * P])
                    last.then_inc(full, 1)
                if stage == "up_w":
                    c, half_f = divmod(n, 2)
                    pe.wait_ge(sems["loraT_ready"], 3)
                    pe.wait_ge(sems["up_dequant"], 1)
                    ps, full = claim(stage, n)
                    pe.matmul(ps[:, :], lora_up_aT[:, c * P:(c + 1) * P], lora_up_b[:, half_f * 512:(half_f + 1) * 512],
                              start=True, stop=False)
                    for k in range(4):
                        last = pe.matmul(ps[:, k * P:(k + 1) * P], up_raw[:, 4 * half_f + k, c * P:(c + 1) * P],
                                         ident[:, :], start=False, stop=k == 3)
                    last.then_inc(full, 1)
                if stage == "dn_w":
                    pe.wait_ge(sems["dn_dequant"], 1)
                    ps, full = claim(stage, n)
                    for a in range(2):
                        f = slice((2 * n + a) * P, (2 * n + a + 1) * P)
                        pe.matmul(ps[:, a * D:(a + 1) * D], lora_dn_aT[:, f], lora_dn_b, start=True, stop=False)
                        for c in range(CC):
                            last = pe.matmul(ps[:, a * D + c * P:a * D + (c + 1) * P], dn_raw[:, c, f], ident[:, :],
                                             start=False, stop=c == CC - 1)
                    last.then_inc(full, 1)
                if stage == "max":
                    u, i = n
                    b, hp = divmod(u, HP)
                    k = u * SUB + i
                    gq, t = divmod(i, ST)
                    if i == 0 and hp == 0:
                        pe.wait_ge(qk_loaded[b], 16 * 3 * (QP + 1))
                    if k >= 2:
                        pe.wait_ge(sems["max_taken"], k - 1)
                    pe.matmul(max_bank[k % 2][:, :], QT[0:ROWS, b, gq // QQ, hp, gq % QQ, t * P:(t + 1) * P],
                              KT[0:ROWS, b, hp].rearrange("p h t -> p (h t)"), start=True, stop=True)\
                        .then_inc(sems["max_scores"], 1)
                if stage == "maxT":
                    u = n
                    pe.wait_ge(sems["max_split"], u + 1)
                    ps, full = claim(stage, u)
                    for t in range(ST):
                        last = pe.transpose(ps[0:G * MROWS, :].bitcast(bf16)[:, t * P:(t + 1) * P],
                                            max_parts[:, u % 2, t].rearrange("p g h n -> p (g h n)"), identb[:, :])
                    last.then_inc(full, 1)
                if stage == "exp":
                    u, i = n
                    b, hp = divmod(u, HP)
                    k = u * SUB + i
                    t, g, hh = i // (QP * HH), i // HH % QP, i % HH
                    if i == 0:
                        pe.wait_ge(max_loaded[u % 2], 16 * G * (u // 2 + 1))
                        pe.wait_ge(sems["k_rows"], HH)
                    if k >= 3:
                        pe.wait_ge(sems["probs_ready"], k - 2)
                    pe.matmul(exp_bank[k % 3][:, :], KT[0:ROWS + MROWS, b, hp, hh, t * P:(t + 1) * P],
                              QT[0:ROWS + MROWS, b, g, hp].rearrange("p q t -> p (q t)"), start=True, stop=True)\
                        .then_inc(sems["exp_scores"], 1)
                if stage == "pv":
                    u, t = n
                    b, hp = divmod(u, HP)
                    h = ST * u + t
                    pe.wait_ge(sems["probs_ready"], QP * HH * (h + 1))
                    if t == 0:
                        pe.wait_ge(sems["v_ready"], ST * (b + 1))
                    if u >= 1 and t == 0:
                        pe.wait_ge(sems["avT_ready"], u)
                    for hh in range(HH):
                        for g in range(QP):
                            j = hh * QP + g
                            last = pe.matmul(pv_bank[j * VC:(j + 1) * VC, :], V[:, b, t, HH * hp + hh, :],
                                             probs[:, (h % 3) * QP * HH + g * HH + hh],
                                             start=t == 0, stop=t == ST - 1)
                    last.then_inc(sems["pv_done"], 1)
                if stage == "spread":
                    u = n
                    pe.wait_ge(sems["avT_ready"], u + 1)
                    ps, full = claim(stage, u)
                    cols = ps[:, :].rearrange("p (t j q c) -> p t q j c", t=ST, j=HH * QP, q=QQ)
                    for q in range(QQ):
                        for t in range(ST):
                            last = turn(cols[:, t, q], avT[:, u % 2, (q * ST + t) * P:(q * ST + t + 1) * P])
                    last.then_inc(full, 1)
                if stage in ("x1T", "x2T"):
                    src, ready = (x1, sems["x1_ready"]) if stage == "x1T" else (x2, sems["x2_ready"])
                    pe.wait_ge(ready, ST * (n + 1))
                    ps, full = claim(stage, n)
                    for c in range(CC):
                        for t in range(ST):
                            last = turn(ps[:, c * S + t * P:c * S + (t + 1) * P], src[:, t, c * P:(c + 1) * P])
                    last.then_inc(full, 1)
                if stage == "cross":
                    pe.wait_ge(sems["x1T_ready"], n + 1)
                    pe.wait_ge(sems["xattnT_ready"], n + 1)
                    ps, full = claim(stage, n)
                    for t in range(ST):
                        for c in range(CC):
                            last = pe.matmul(ps[:, t * S:(t + 1) * S], x1T[:, c, t * P:(t + 1) * P], xattnT[:, n, c, :],
                                             start=c == 0, stop=c == CC - 1)
                    last.then_inc(full, 1)
                if stage == "up":
                    b, j = n
                    pe.wait_ge(sems["x2_lo_done"], b + 1)
                    pe.wait_ge(sems["w_ready"], 8)
                    ps, full = claim(stage, n)
                    for a in range(2):
                        f = slice((2 * j + a) * P, (2 * j + a + 1) * P)
                        products = [(w, xx, c) for c in range(CC)
                                    for w, xx in ((up_hi, x2_hi), (up_hi, x2_lo), (up_lo, x2_hi))]
                        for m, (w, xx, c) in enumerate(products):
                            last = pe.matmul(ps[:, a * S:(a + 1) * S], w[:, c, f], xx[:, c, :],
                                             start=m == 0, stop=m == len(products) - 1)
                    last.then_inc(full, 1)
                if stage == "down":
                    b, t = n
                    pe.wait_ge(sems["y_lo_done"], (FC // 2) * (b + 1))
                    ps, full = claim(stage, n)
                    products = [(yy, w, f) for f in range(FC)
                                for yy, w in ((y_hi, dn_hi), (y_hi, dn_lo), (y_lo, dn_hi))]
                    for m, (yy, w, f) in enumerate(products):
                        last = pe.matmul(ps[:, 0:D], yy[:, f, t * P:(t + 1) * P], w[:, f, :],
                                         start=m == 0, stop=m == len(products) - 1)
                    last.then_inc(full, 1)

        @block.vector
        def _(dve):
            steps = [0]

            def step(ins):
                steps[0] += 1
                ins.then_inc(sems["dve_step"], 1)
                dve.wait_ge(sems["dve_step"], steps[0])

            for hh in range(HH):
                for row in range(HH):
                    dve.memset(head_mask[row * 32:(row + 1) * 32, hh:hh + 1], float(row == hh)).then_inc(sems["masks"], 1)
            dve.wait_ge(sems["identities"], 1)
            dve.tensor_reduce(group_mask[:, :], ident[:, :].rearrange("p (j q) -> p q j", q=QQ), X, ALU.add)\
                .then_inc(sems["masks"], 1)
            dve.tensor_copy(pick[:, :].rearrange("k (r a q) -> k r a q", a=HP, q=QQ),
                            ident[0:KV, 0:KV].rearrange("k (a r) -> k r a", a=HP).unsqueeze(3)
                            .broadcast_to([KV, HD, HP, QQ])).then_inc(sems["masks"], 1)
            step(dve.memset(V[:, :, :, :, :], 0.0))
            dve.memset(V[:, :, :, :, DH:DH + 1], 1.0).then_inc(sems["v_zeroed"], 1)
            dve.wait_ge(sems["mix_exp"], 1)
            dve.tensor_scalar(mix[:, 2:3], mix[:, 1:2], 1.0, None, ALU.add).then_inc(sems["mix_ready"], 1)
            dve.wait_ge(sems["mix_ready"], 1)
            dve.reciprocal(mix[:, 3:4], mix[:, 2:3]).then_inc(sems["mix_ready"], 1)
            dve.wait_ge(sems["mix_ready"], 2)
            dve.tensor_scalar(mix[:, 4:5], mix[:, 3:4], -1.0, 1.0, ALU.mult, ALU.add).then_inc(sems["mix_ready"], 1)

            def split3(parts, src, spare, done):
                step(dve.tensor_copy(parts[:, 0], src))
                step(dve.tensor_tensor(spare, src, parts[:, 0], ALU.subtract))
                step(dve.tensor_copy(parts[:, 1], spare))
                dve.tensor_tensor(parts[:, 2], spare, parts[:, 1], ALU.subtract).then_inc(done, 1)

            norms, normalised = [0], []

            def statistics():
                if normalised:
                    dve.wait_ge(*normalised.pop())
                for t in range(ST):
                    last = dve.bn_stats(stats[:, t, :], pre[:, t])
                step(last)
                norms[0] += 1
                for t in range(ST):
                    last = dve.bn_aggr(moments[:, t, :], stats[:, t, :])
                last.then_inc(sems["moments_ready"], 1)

            def normalise(to, done, b):
                dve.wait_ge(sems["rstd_ready"], norms[0])
                dve.wait_ge(sems["moments_ready"], norms[0])
                for t in range(ST):
                    dve.tensor_scalar(to[:, t], pre[:, t], moments[:, t, 0:1], rstd[:, t, :],
                                      ALU.subtract, ALU.mult).then_inc(done, 1)
                normalised.append((done, ST * (b + 1)))

            for stage, n in behind:
                if stage == "q":
                    dve.wait_ge(sems["qf_ready"], n + 1)
                    if n >= 1:
                        dve.wait_ge(sems["k_parts_ready"], n)
                        dve.wait_ge(q_written[n - 1], 16 * QP)
                    split3(q_parts, qf[:, n % 2], rest[:, :].rearrange("p (c t) -> p c t", c=QP), sems["q_parts_ready"])
                if stage == "kv":
                    dve.wait_ge(sems["kf_ready"], HH * (n + 1))
                    if n >= 1:
                        dve.wait_ge(k_written[n - 1], 16)
                    dve.wait_ge(sems["q_parts_ready"], n + 1)
                    split3(k_parts, kf, rest[0:KV, :].rearrange("p (c t) -> p c t", c=HH), sems["k_parts_ready"])
                    dve.wait_ge(sems["q_exp"], n + 1)
                    dve.scalar_tensor_tensor(out=sigma, in0=q_neg, scalar=-1.0, in1=sigma, op0=ALU.add, op1=ALU.add)\
                        .then_inc(sems["sigma_ready"], 1)
                if stage == "xwT":
                    for hh in range(HH):
                        own, other = (0.0, -1.0) if hh else (-1.0, 0.0)
                        step(dve.memset(KT[ROWS:ROWS + MROWS, :, :, hh, :], other))
                        dve.memset(KT[ROWS:ROWS + 2, :, :, hh, :], own).then_inc(sems["k_rows"], 1)
                if stage == "mem_rhs":
                    ps = in_bank(dve, stage)
                    dve.wait_ge(sems["mix_ready"], 3)
                    dve.wait_ge(sems["masks"], 5)
                    for q in range(QQ):
                        dve.tensor_scalar(mem_rhs[:, q, 0:KV], ps[:, 0:KV], group_mask[:, q:q + 1], mix[:, 3:4],
                                          ALU.mult, ALU.mult).then_inc(sems["mem_rhs_ready"], 1)
                        dve.tensor_scalar(mem_rhs[:, q, KV:KV + 1], ps[:, KV:KV + 1], group_mask[:, q:q + 1], None,
                                          ALU.mult).then_inc(sems["mem_rhs_ready"], 1)
                if stage == "mem":
                    b, t = n
                    ps = in_bank(dve, stage, n)[:, 0:G * (KV + 1)].rearrange("p (g e) -> p g e", g=G)
                    if n != (0, 0):
                        dve.wait_ge(sems["memterm_ready"], ST * b + t)
                    step(dve.reciprocal(memrec[:, :], ps[:, :, KV]))
                    if n != (0, 0):
                        dve.wait_ge(sems["residual"], ST * b + t)
                    dve.tensor_tensor(memterm[:, :].rearrange("p (g e) -> p g e", g=G), ps[:, :, 0:KV],
                                      memrec[:, :].unsqueeze(2).broadcast_to([P, G, KV]), ALU.mult)\
                        .then_inc(sems["memterm_ready"], 1)
                if stage == "energy":
                    ps = in_bank(dve, stage, n)
                    dve.tensor_reduce(energy_stat[:, n, 0, :], ps[:, :].rearrange("p (t c) -> p t c", t=ST), X, ALU.max,
                                      negate=True).then_inc(sems["energy_max"], 1)
                if stage == "xattnT":
                    dve.wait_ge(sems["energy_exp"], ST * (n + 1))
                    step(dve.reciprocal(energy_stat[:, n, 2, :], energy_stat[:, n, 1, :]))
                    for t in range(ST):
                        dve.tensor_scalar(energy[:, t], energy[:, t], energy_stat[:, n, 2, t:t + 1], None, ALU.mult)\
                            .then_inc(sems["xattn_ready"], 1)
                if stage in ("up_w", "dn_w"):
                    i = n + (4 if stage == "dn_w" else 0)
                    dve.wait_ge(sems["w_hi_ready"], i + 1)
                    ps = in_bank(dve, stage, n)
                    if stage == "up_w":
                        c, half_f = divmod(n, 2)
                        hi, lo = (m[:, c, half_f * 512:(half_f + 1) * 512] for m in (up_hi, up_lo))
                    else:
                        hi, lo = (m[:, 2 * n:2 * n + 2].rearrange("p c t -> p (c t)") for m in (dn_hi, dn_lo))
                    dve.tensor_tensor(lo, ps[:, :], hi.bitcast(fp32), ALU.subtract).then_inc(sems["w_ready"], 1)
                if stage == "max":
                    u, i = n
                    k = u * SUB + i
                    gq, t = divmod(i, ST)
                    if u >= 2 and i == 0:
                        dve.wait_ge(sems["max_split"], u - 1)
                    dve.wait_ge(sems["max_scores"], k + 1)
                    dve.tensor_reduce(maxes[:, u % 2, t, gq // QQ, gq % QQ, :],
                                      max_bank[k % 2][:, :].rearrange("p (h t) -> p h t", h=HH), X, ALU.max)\
                        .then_inc(sems["max_taken"], 1)
                if stage == "spread":
                    u = n
                    b, hp = divmod(u, HP)
                    ps = in_bank(dve, stage, u)[:, :].rearrange("p (t h g c) -> p t h g c", t=ST, h=HH, g=G)
                    r = rec[:, u % 2, :].rearrange("p (t h g) -> p t h g", t=ST, h=HH)
                    if u >= 2:
                        dve.wait_ge(sems["adot_ready"], ST * (u - 1))
                    step(dve.reciprocal(r.rearrange("p t h g -> p (t h g)"),
                                        ps.rearrange("p t h g c -> p (t h g) c")[:, :, DH]))
                    if b >= 2 and hp == 0:
                        dve.wait_ge(sems["attn_added"], b - 1)
                    for t in range(ST):
                        to = adot[:, b % 2, t].rearrange("p (g a h d) -> p a h g d", g=G, a=HP, h=HH)[:, hp]
                        dve.tensor_tensor(to, ps[:, t, :, :, 0:DH], r[:, t].unsqueeze(3).broadcast_to([P, HH, G, DH]),
                                          ALU.mult).then_inc(sems["adot_ready"], 1)
                if stage == "ln1_stats":
                    dve.wait_ge(sems["attn_added"], n + 1)
                    statistics()
                if stage == "ln1":
                    if n >= 1:
                        dve.wait_ge(sems["cross_added"], n)
                    normalise(x1, sems["x1_ready"], n)
                if stage == "cross":
                    ps = in_bank(dve, stage, n)
                    dve.wait_ge(sems["x1_ready"], ST * (n + 1))
                    dve.tensor_tensor(pre.rearrange("p t d -> p (t d)"), ps[:, :], x1.rearrange("p t d -> p (t d)"),
                                      ALU.add).then_inc(sems["cross_added"], 1)
                if stage == "ln2_stats":
                    dve.wait_ge(sems["cross_added"], n + 1)
                    statistics()
                if stage == "ln2":
                    if n >= 1:
                        dve.wait_ge(sems["x2b_ready"], n)
                        in_bank(dve, "x2T", n - 1)
                    normalise(x2, sems["x2_ready"], n)
                if stage == "x2T":
                    dve.wait_ge(sems["x2T_ready"], n + 1)
                    if n >= 1:
                        in_bank(dve, "up", (n - 1, FC // 2 - 1))
                    dve.tensor_copy(x2_hi[:, :, :], x2T).then_inc(sems["x2_hi_done"], 1)
                if stage == "up":
                    b, j = n
                    i = b * (FC // 2) + j
                    dve.wait_ge(sems["yf_ready"], 2 * (i + 1))
                    if b >= 1 and j == 0:
                        in_bank(dve, "down", (b - 1, ST - 1))
                    dve.tensor_copy(y_hi[:, 2 * j:2 * j + 2].rearrange("p c t -> p (c t)"), yf[:, i % 2])\
                        .then_inc(sems["y_hi_done"], 1)
                if stage == "down":
                    b, t = n
                    ps = in_bank(dve, stage, n)
                    dve.wait_ge(sems["x2b_ready"], b + 1)
                    dve.wait_ge(sems["x2_ready"], ST * (b + 1))
                    dve.tensor_tensor(pre[:, t], ps[:, 0:D], x2b[:, t], ALU.add).then_inc(sems["down_added"], 1)
                if stage == "ln3_stats":
                    dve.wait_ge(sems["down_added"], ST * (n + 1))
                    statistics()
                if stage == "ln3":
                    if n >= 1:
                        dve.wait_ge(stored, 16 * n)
                    normalise(x3, sems["x3_ready"], n)


_INS = ["x", "ctx_1024", "L0_attn_Wq", "L0_attn_Wk", "L0_attn_Wv", "L0_attn_memory", "L0_attn_memory_norm",
        "L0_attn_memory_weight", "L0_xattn_Wq", "L0_xattn_bq", "L0_xattn_Wk", "L0_xattn_bk",
        "L0_ffn_w_up_q", "L0_ffn_w_up_scale", "L0_ffn_b_up", "L0_ffn_w_up_lora_a", "L0_ffn_w_up_lora_b",
        "L0_ffn_w_down_q", "L0_ffn_w_down_scale", "L0_ffn_b_down", "L0_ffn_w_down_lora_a", "L0_ffn_w_down_lora_b"]


def kernel(**inputs):
    import numpy as _np
    import concourse.bacc as _bacc
    from concourse import mybir as _mybir
    from concourse.bass_utils import run_bass_kernel_spmd as _run

    nc = _bacc.Bacc("TRN2", target_bir_lowering=False, num_devices=1)
    arrays, args = {}, []
    for name in _INS:
        a = _np.ascontiguousarray(inputs[name])
        arrays[f"in_{name}"] = a
        args.append(nc.dram_tensor(f"in_{name}", a.shape, _mybir.dt.from_np(a.dtype), kind="ExternalInput").ap())
    shape = inputs["x"].shape
    args.append(nc.dram_tensor("out_0", shape, _mybir.dt.float32, kind="ExternalOutput").ap())
    build_decoder(nc, *args)
    r = _run(nc, [arrays], core_ids=[0])
    return r.results[0]["out_0"]
```

```python
import concourse.bass as bass
from concourse import mybir
from contextlib import ExitStack

import numpy as np


def build_decoder(nc, x, ctx, wq, wk, wv, memory, memory_norm, memory_weight, xwq, xbq, xwk, xbk,
                  up_q, up_scale, up_bias, up_a, up_b, dn_q, dn_scale, dn_bias, dn_a, dn_b, out):
    fp32, fp32r, bf16, i32 = mybir.dt.float32, mybir.dt.float32r, mybir.dt.bfloat16, mybir.dt.int32
    ALU = mybir.AluOpType
    ACT = mybir.ActivationFunctionType
    X = mybir.AxisListType.X

    P = 128
    B, S, D = x.shape
    KV = wk.shape[0]
    G, H = D // KV, 8
    DH = KV // H
    C = ctx.shape[2]
    F = up_q.shape[0]
    R = up_a.shape[1]
    QB = D // up_scale.shape[1]
    HP, HH = H // 2, 2
    QP, QQ = G // 2, 2
    ST, CC = S // P, D // P
    FC = F // P
    TERM_Q = (0, 0, 0, 1, 1, 2)
    TERM_K = (0, 1, 2, 0, 1, 0)
    TERMS = len(TERM_Q)
    HD = HH * DH
    ROWS = TERMS * HD
    MROWS = HH * 2
    UNITS = B * HP
    SUB = 8
    VC = 32
    EPS = 1e-5
    SCALE = float(np.float32(1.0 / np.sqrt(np.float32(DH))))

    q_scratch = nc.dram_tensor("q_scratch", [B, 3, QP, HD, HP * QQ * S], bf16, kind="Internal").ap()
    k_scratch = nc.dram_tensor("k_scratch", [B, 3, HD, HP * HH * S], bf16, kind="Internal").ap()

    stack = ExitStack()
    with stack:
        def sb(name, shape, dt):
            return stack.enter_context(nc.sbuf_tensor(name, shape, dt))

        def sem(name):
            return stack.enter_context(nc.semaphore(name))

        ident = sb("ident", [P, P], fp32)
        identb = sb("identb", [P, P], bf16)
        pick = sb("pick", [KV, P], fp32)
        group_mask = sb("group_mask", [P, QQ], fp32)
        head_mask = sb("head_mask", [2 * 32, HH], fp32)
        xs = sb("xs", [P, B, ST, D], fp32)
        wq_nat = sb("wq_nat", [P, CC, D], fp32)
        wkv_nat = sb("wkv_nat", [P, D], fp32)
        wqT = sb("wqT", [P, CC, QP, P], fp32)
        wkvT = sb("wkvT", [P, CC, P], fp32)
        mem_nat = sb("mem_nat", [KV, KV + 1], fp32)
        mem_rhs = sb("mem_rhs", [P, QQ, KV + 1], fp32)
        mix = sb("mix", [P, 8], fp32)
        QT = sb("QT", [P, B, QP, HP, QQ, S], bf16)
        KT = sb("KT", [P, B, HP, HH, S], bf16)
        k_pattern = sb("k_pattern", [MROWS, HH, S], bf16)
        V = sb("V", [P, B, ST, H, VC], fp32)
        xattnT = sb("xattnT", [P, B, ST, S], fp32)
        energy = sb("energy", [P, ST, S], fp32)
        energy_stat = sb("energy_stat", [P, B, 3, ST], fp32)
        xw_nat = sb("xw_nat", [P, 2, C], fp32)
        xwT = sb("xwT", [P, 2, C], fp32)
        xb = sb("xb", [P, 2], fp32)
        upscale = sb("upscale", [P, FC, D // QB], fp32)
        dnscale = sb("dnscale", [P, CC, F // QB], fp32)
        upbias = sb("upbias", [P, FC], fp32)
        dnbias = sb("dnbias", [P, D], fp32)
        lora_up_a = sb("lora_up_a", [P, CC, R], fp32)
        lora_dn_a = sb("lora_dn_a", [P, FC, R], fp32)
        lora_up_b = sb("lora_up_b", [R, F], fp32)
        up_hi = sb("up_hi", [P, CC, F], fp32r)
        up_lo = sb("up_lo", [P, CC, F], fp32r)
        x2_hi = sb("x2_hi", [P, CC, S], fp32r)
        x2_lo = sb("x2_lo", [P, CC, S], fp32r)
        maxes = sb("maxes", [P, 2, ST, QP, QQ, HH], fp32)
        max_parts = sb("max_parts", [P, 2, ST, G, HH, 2], bf16)
        maxT = sb("maxT", [G * MROWS, 2, S], bf16)
        rec = sb("rec", [P, 2, 16], fp32)
        memrec = sb("memrec", [P, G], fp32)
        memterm = sb("memterm", [P, D], fp32)
        stats = sb("stats", [P, ST, 6], fp32)
        moments = sb("moments", [P, ST, 2], fp32)
        rstd = sb("rstd", [P, ST, 1], fp32)
        half = sb("half", [P, ST, 1], fp32)

        probs = sb("probs", [P, 3 * (SUB // 2), 512], fp32)
        avT = sb("avT", [P, 2, 512], fp32)
        adot = sb("adot", [P, 2, ST, D], fp32)

        with nc.sbuf_tensor("early", [P, 2 * (FC * S + FC * D)], fp32) as early:
            up_raw = early[:, 0:FC * D].rearrange("p (a b) -> p a b", a=FC)
            dn_raw = early[:, FC * S:FC * S + CC * F].rearrange("p (a b) -> p a b", a=CC)
            late = 2 * FC * S
            ctx_nat = early[:, late:late + 1024].rearrange("p (a b) -> p a b", a=B * ST)
            ctxT = early[:, late + 1024:late + 2048]
            xq = early[:, late + 2048:late + 3072]
            xk = early[:, late + 3072:late + 4096]
        y_hi = sb("y_hi", [P, FC, S], fp32r)
        y_lo = sb("y_lo", [P, FC, S], fp32r)
        dn_hi = sb("dn_hi", [P, FC, D], fp32r)
        dn_lo = sb("dn_lo", [P, FC, D], fp32r)

        arena_b = sb("arena_b", [P, 6656], fp32)
        xT = arena_b[:, 0:1024].rearrange("p (n c s) -> p n c s", n=2, c=CC)
        qf = arena_b[:, 1024:2048].rearrange("p (n c s) -> p n c s", n=2, c=QP)
        q_neg = arena_b[:, 2048:2560].rearrange("p (c s) -> p c s", c=QP)
        sigma = arena_b[:, 2560:3072].rearrange("p (c s) -> p c s", c=QP)
        kf = arena_b[0:KV, 3072:3584].rearrange("p (c s) -> p c s", c=HH)
        q_parts = arena_b[:, 3584:4352].bitcast(bf16).rearrange("p (n c s) -> p n c s", n=3, c=QP)
        k_parts = arena_b[0:KV, 4352:5120].bitcast(bf16).rearrange("p (n c s) -> p n c s", n=3, c=HH)
        lora_dn_aT = arena_b[0:R, 5120:6144]
        lora_up_aT = arena_b[0:R, 6144:6400]
        lora_dn_b = arena_b[0:R, 6400:6656]
        x1 = arena_b[:, 2048:2560].rearrange("p (t d) -> p t d", t=ST)
        x1T = arena_b[:, 2560:3072].rearrange("p (c s) -> p c s", c=CC)
        x2 = arena_b[:, 3072:3584].rearrange("p (t d) -> p t d", t=ST)
        x2T = arena_b[:, 3584:4096].rearrange("p (c s) -> p c s", c=CC)
        yf = arena_b[:, 4096:5120].rearrange("p (n f) -> p n f", n=2)
        x3 = arena_b[:, 5120:5632].rearrange("p (t d) -> p t d", t=ST)
        pre = arena_b[:, 5632:6144].rearrange("p (t d) -> p t d", t=ST)
        pre3 = sb("pre3", [P, ST, D], fp32)
        x2b = arena_b[:, 6144:6656].rearrange("p (t d) -> p t d", t=ST)
        rest = sb("rest", [P, 512], fp32)

        def bank(name):
            return stack.enter_context(nc.psum_tensor(name, [P, 512], fp32))

        exp_bank = [bank(f"exp_bank{i}") for i in range(3)]
        max_bank = [bank(f"max_bank{i}") for i in range(2)]
        pv_bank = bank("pv_bank")
        shared = [bank(f"shared{i}") for i in range(2)]

        HALVED = ("q", "up", "down", "cross")

        def filling(stages):
            for key in stages:
                if key[0] in HALVED:
                    yield ("begin", key)
                yield key

        def norms(b):
            return [("ln1_stats", b), ("ln1", b), ("x1T", b), ("cross", b), ("ln2_stats", b), ("ln2", b), ("x2T", b)]

        def ffn(b):
            return [*[("up", (b, j)) for j in range(FC // 2)],
                    *[("down", (b, t)) for t in range(ST)], ("ln3_stats", b), ("ln3", b)]

        def between(a, b):
            return [*a[:3], b[0], b[1], *a[3:5], *b[2:5], *a[5:], *b[5:]]

        fill = [
            ("wqT", 0), ("xT", 0), ("wkvT", 0), ("begin", ("q", 0)), ("q", 0), ("kv", 0), ("mem_rhs", 0), ("xT", 1),
            ("mem", (0, 0)), ("xwT", 0), ("ctxT", 0), ("xq", 0), ("ctxT", 1), ("mem", (0, 1)), ("begin", ("q", 1)),
            ("q", 1), ("kv", 1), ("xk", 0), ("mem", (1, 0)), ("energy", 0), ("xT", 2), ("xattnT", 0), ("xq", 1),
            ("mem", (1, 1)), ("begin", ("q", 2)), ("q", 2), ("kv", 2), ("xk", 1), ("xT", 3), ("energy", 1),
            ("loraT", 0), ("xattnT", 1), ("mem", (2, 0)), ("energy", 2), ("xattnT", 2), ("mem", (2, 1)),
            ("begin", ("q", 3)), ("q", 3), ("loraT", 1), ("kv", 3), ("loraT", 2), ("energy", 3), ("up_w", 0),
            ("mem", (3, 0)), ("up_w", 1), ("xattnT", 3), ("mem", (3, 1)), ("up_w", 2), ("up_w", 3), ("dn_w", 0),
            ("dn_w", 1), ("dn_w", 2), ("dn_w", 3), ("ln1_stats", 0), ("ln1", 0), ("x1T", 0), ("begin", ("cross", 0)),
            ("cross", 0), ("ln2_stats", 0), ("ln2", 0), ("x2T", 0), ("begin", ("up", (0, 0))), ("up", (0, 0)),
            ("begin", ("up", (0, 1))), ("up", (0, 1)), ("begin", ("up", (0, 2))), ("up", (0, 2)),
            ("begin", ("up", (0, 3))), ("up", (0, 3)), ("ln1_stats", 1), ("ln1", 1), ("x1T", 1),
            ("begin", ("cross", 1)), ("cross", 1), ("begin", ("down", (0, 0))), ("down", (0, 0)),
            ("begin", ("down", (0, 1))), ("ln2_stats", 1), ("down", (0, 1)), ("ln2", 1), ("ln3_stats", 0),
            ("x2T", 1), ("ln3", 0), ("begin", ("up", (1, 0))), ("up", (1, 0)), ("ln1_stats", 2),
            ("begin", ("up", (1, 1))), ("up", (1, 1)), ("begin", ("up", (1, 2))), ("up", (1, 2)),
            ("begin", ("up", (1, 3))), ("ln1", 2), ("up", (1, 3)), ("x1T", 2), ("begin", ("cross", 2)), ("cross", 2),
            ("begin", ("down", (1, 0))), ("down", (1, 0)), ("ln2_stats", 2), ("begin", ("down", (1, 1))),
            ("down", (1, 1)), ("ln2", 2), ("x2T", 2), ("ln3_stats", 1), ("ln3", 1), ("begin", ("up", (2, 0))),
            ("up", (2, 0)), ("ln1_stats", 3), ("begin", ("up", (2, 1))), ("up", (2, 1)), ("ln1", 3),
            ("begin", ("up", (2, 2))), ("up", (2, 2)), ("x1T", 3), ("begin", ("up", (2, 3))), ("up", (2, 3)),
            ("begin", ("cross", 3)), ("cross", 3), ("begin", ("down", (2, 0))), ("ln2_stats", 3), ("down", (2, 0)),
            ("begin", ("down", (2, 1))), ("down", (2, 1)), ("ln2", 3), ("x2T", 3), ("begin", ("up", (3, 0))),
            ("ln3_stats", 2), ("ln3", 2), ("up", (3, 0)), ("begin", ("up", (3, 1))), ("up", (3, 1)),
            ("begin", ("up", (3, 2))), ("up", (3, 2)), ("begin", ("up", (3, 3))), ("up", (3, 3)),
            ("begin", ("down", (3, 0))), ("down", (3, 0)), ("begin", ("down", (3, 1))), ("down", (3, 1)),
            ("ln3_stats", 3), ("ln3", 3),]
        start = 13
        lead = 12
        pace = [int(c) for c in (
            "020001011020 30110400 12022411 11010011 00014120 11321001 10110111 00001003 "
            "00101030 10031001 10020011 00130002 00100012 00011411 00020012 01010020 "
            "10210001 ").replace(" ", "")]
        tail = 3
        at = {"pv1": 1, "pv0": 6, "maxT": 5, "spread": 4}

        order = fill[:start]
        del fill[:start]

        def take(n=1):
            for _ in range(n):
                if not fill or fill[0][0] == "ln1_stats" and fill[0][1] * HP + HP - 1 not in spread_out:
                    break
                order.append(fill.pop(0))

        spread_out = []
        for k in range(-lead, UNITS * SUB):
            u, i = divmod(k, SUB)
            if u >= 0:
                order.append(("exp", (u, i)))
            if k + lead < UNITS * SUB:
                order.append(("max", divmod(k + lead, SUB)))
            if i == at["pv1"] and u >= 1:
                order.append(("pv", (u - 1, 1)))
            if i == at["pv0"] and u >= 0:
                order.append(("pv", (u, 0)))
            if i == at["maxT"] and 0 <= u + 1 < UNITS:
                order.append(("maxT", u + 1))
            if i == at["spread"] and u >= 1:
                order.append(("spread", u - 1))
                spread_out.append(u - 1)
            take(pace[k + lead])
        order.append(("pv", (UNITS - 1, 1)))
        take(tail)
        order.append(("spread", UNITS - 1))
        spread_out.append(UNITS - 1)
        take(len(fill))

        sems = {}
        loads = ("wq", "wkv", "weight", "memory", "context", "cross_w", "up_w", "dn_w", "lora", "biases")
        by_pool = ("pool_step", "identities", "constants", "v_zeroed", "up_dequant", "dn_dequant",
                   "q_split", "residual", "max_split", "rstd_ready", "x2_lo_done", "y_lo_done", "x2b_ready")
        by_act = ("wqT_ready", "wkvT_ready", "xT_ready", "qf_ready", "q_exp", "kf_ready", "v_ready", "xwT_ready",
                  "ctxT_ready", "xq_ready", "xk_ready", "loraT_ready", "energy_exp", "xattnT_ready", "w_hi_ready",
                  "mix_exp", "probs_ready", "maxT_ready", "avT_ready", "x1T_ready", "x2T_ready", "yf_ready")
        by_dve = ("dve_step", "masks", "k_pattern_ready", "mix_ready", "mem_rhs_ready", "q_parts_ready", "k_parts_ready", "sigma_ready",
                  "memterm_ready", "energy_max", "xattn_ready", "w_ready", "max_taken", "adot_ready", "attn_added", "moments_ready",
                  "x1_ready", "x2_ready", "cross_added", "x2_lo_last", "y_lo_last", "x2_hi_done", "y_hi_done", "down_added", "x3_ready")
        by_pe = ("exp_scores", "max_scores", "pv_done")
        for name in (*("ld_" + n for n in loads), "k_rows", *by_pool, *by_act, *by_dve, *by_pe):
            sems[name] = sem(name)
        ld_x = [sem(f"ld_x{b}") for b in range(B)]
        q_written = [sem(f"q_written{b}") for b in range(B)]
        k_written = [sem(f"k_written{b}") for b in range(B)]
        qk_loaded = [sem(f"qk_loaded{b}") for b in range(B)]
        max_loaded = [sem(f"max_loaded{i}") for i in range(2)]
        stored = sem("stored")

        shared_full = [sem(f"shared_full{i}") for i in range(2)]
        release = {
            "wqT": lambda n: (sems["wqT_ready"], CC * QP), "wkvT": lambda n: (sems["wkvT_ready"], CC + 1),
            "xT": lambda b: (sems["xT_ready"], b + 1), "q": lambda b: (sems["qf_ready"], b + 1),
            "kv": lambda b: (sems["v_ready"], ST * (b + 1)), "mem_rhs": lambda n: (sems["mem_rhs_ready"], 2 * QQ),
            "mem": lambda n: (sems["memterm_ready"], ST * n[0] + n[1] + 1), "xwT": lambda n: (sems["xwT_ready"], 1),
            "ctxT": lambda n: (sems["ctxT_ready"], n + 1), "xq": lambda n: (sems["xq_ready"], n + 1),
            "xk": lambda n: (sems["xk_ready"], n + 1), "loraT": lambda n: (sems["loraT_ready"], n + 1),
            "energy": lambda b: (sems["energy_exp"], ST * (b + 1)), "xattnT": lambda b: (sems["xattnT_ready"], b + 1),
            "up_w": lambda j: (sems["w_ready"], j + 1), "dn_w": lambda j: (sems["w_ready"], 4 + j + 1),
            "maxT": lambda u: (sems["maxT_ready"], u + 1), "spread": lambda u: (sems["adot_ready"], ST * (u + 1)),
            "x1T": lambda b: (sems["x1T_ready"], b + 1), "cross": lambda b: (sems["cross_added"], b + 1),
            "x2T": lambda b: (sems["x2T_ready"], b + 1), "up": lambda n: (sems["yf_ready"], 2 * (n[0] * (FC // 2) + n[1] + 1)),
            "down": lambda n: (sems["down_added"], ST * n[0] + n[1] + 1),
        }
        in_turn = [k[1] if k[0] == "begin" else k for k in order if k[0] in release and k[0] not in HALVED or k[0] == "begin"]
        SLOT = {key: i for i, key in enumerate(in_turn)}

        def in_bank(eng, stage, n=0):
            i = SLOT[stage, n]
            eng.wait_ge(shared_full[i % 2], i // 2 + 1)
            return shared[i % 2]

        block = stack.enter_context(nc.Block())

        @block.sync
        def _(sp):
            sp.dma_start(wq_nat[:, :, :], wq.rearrange("(c p) d -> p c d", p=P)).then_inc(sems["ld_wq"], 16)
            sp.dma_start(xs[:, 0], x[0].rearrange("(t p) d -> p t d", p=P)).then_inc(ld_x[0], 16)
            sp.dma_start(wkv_nat[0:KV, :], wk).then_inc(sems["ld_wkv"], 16)
            sp.dma_start(wkv_nat[KV:2 * KV, :], wv).then_inc(sems["ld_wkv"], 16)
            sp.dma_start(mix[:, 0:1], memory_weight.partition_broadcast(P)).then_inc(sems["ld_weight"], 16)
            sp.dma_start(mem_nat[:, 0:KV], memory).then_inc(sems["ld_memory"], 16)
            sp.dma_start(mem_nat[:, KV:KV + 1], memory_norm).then_inc(sems["ld_memory"], 16)
            sp.dma_start(xs[:, 1], x[1].rearrange("(t p) d -> p t d", p=P)).then_inc(ld_x[1], 16)
            sp.dma_start(xw_nat[:, 0, :], xwq).then_inc(sems["ld_cross_w"], 16)
            sp.dma_start(xw_nat[:, 1, :], xwk).then_inc(sems["ld_cross_w"], 16)
            sp.dma_start(ctx_nat, ctx.rearrange("b (t p) c -> p (b t) c", p=P)).then_inc(sems["ld_context"], 16)
            sp.dma_start(xb[:, 0:1], xbq.rearrange("(p o) -> p o", o=1)).then_inc(sems["ld_cross_w"], 16)
            sp.dma_start(xb[:, 1:2], xbk.rearrange("(p o) -> p o", o=1)).then_inc(sems["ld_cross_w"], 16)
            sp.wait_ge(sems["k_pattern_ready"], 2 * HH)
            sp.dma_start(KT[ROWS:ROWS + MROWS].rearrange("p b a h t -> p (b a) (h t)"),
                         k_pattern[:, :, :].rearrange("p h t -> p (h t)").unsqueeze(1)
                         .broadcast_to([MROWS, B * HP, HH * S])).then_inc(sems["k_rows"], 16)
            for b in range(2, B):
                sp.dma_start(xs[:, b], x[b].rearrange("(t p) d -> p t d", p=P)).then_inc(ld_x[b], 16)
            for stage, n in order:
                if stage == "kv":
                    b = n
                    sp.wait_ge(sems["q_parts_ready"], b + 1)
                    for g in range(QP):
                        sp.dma_start(q_scratch[b, :, g].rearrange("n r (a t) -> (r a) n t", t=S),
                                     q_parts[:, :, g, :]).then_inc(q_written[b], 16)
                    sp.wait_ge(sems["k_parts_ready"], b + 1)
                    sp.dma_start(k_scratch[b].rearrange("n r (a t) -> (r a) n t", a=HP),
                                 k_parts.rearrange("p n c t -> p n (c t)")).then_inc(k_written[b], 16)
                if stage == "mem" and n[1] == 0:
                    b = n[0]
                    sp.wait_ge(q_written[b], 16 * QP)
                    sp.wait_ge(k_written[b], 16)
                    for part in range(3):
                        terms = TERM_Q.count(part)
                        rows = slice(TERM_Q.index(part) * HD, (TERM_Q.index(part) + terms) * HD)
                        for g in range(QP):
                            sp.dma_start(QT[rows, b, g].rearrange("p a c t -> p (a c t)"),
                                         q_scratch[b, part, g].unsqueeze(0).broadcast_to([terms, HD, HP * QQ * S]))\
                                .then_inc(qk_loaded[b], 16)
                        sp.dma_start(KT[rows, b].rearrange("p a c t -> p (a c t)"),
                                     k_scratch[b, 0:terms].rearrange("n r t -> (n r) t")).then_inc(qk_loaded[b], 16)
                if stage == "mem" and n == (1, 0):
                    sp.dma_start(up_raw.bitcast(i32), up_q.rearrange("(c p) d -> p c d", p=P)).then_inc(sems["ld_up_w"], 16)
                    sp.dma_start(upscale[:, :, :], up_scale.rearrange("(c p) k -> p c k", p=P)).then_inc(sems["ld_up_w"], 16)
                    sp.dma_start(dn_raw.bitcast(i32), dn_q.rearrange("(c p) f -> p c f", p=P)).then_inc(sems["ld_dn_w"], 16)
                    sp.dma_start(dnscale[:, :, :], dn_scale.rearrange("(c p) k -> p c k", p=P)).then_inc(sems["ld_dn_w"], 16)
                    sp.dma_start(lora_up_a[:, :, :], up_a.rearrange("(c p) r -> p c r", p=P)).then_inc(sems["ld_lora"], 16)
                    sp.dma_start(lora_dn_a[:, :, :], dn_a.rearrange("(c p) r -> p c r", p=P)).then_inc(sems["ld_lora"], 16)
                    sp.dma_start(lora_up_b[:, :], up_b).then_inc(sems["ld_lora"], 16)
                    sp.dma_start(lora_dn_b, dn_b).then_inc(sems["ld_lora"], 16)
                    sp.dma_start(upbias[:, :], up_bias.rearrange("(c p) -> p c", p=P),
                                 allow_slow_non_contiguous=True).then_inc(sems["ld_biases"], 16)
                    sp.dma_start(dnbias[:, :], dn_bias.partition_broadcast(P)).then_inc(sems["ld_biases"], 16)
                if stage == "maxT":
                    u = n
                    b, hp = divmod(u, HP)
                    sp.wait_ge(sems["maxT_ready"], u + 1)
                    for g in range(G):
                        sp.dma_start(QT[ROWS:ROWS + MROWS, b, g // QQ, hp, g % QQ, :],
                                     maxT[g * MROWS:(g + 1) * MROWS, u % 2, :]).then_inc(max_loaded[u % 2], 16)
                if stage == "ln3":
                    sp.wait_ge(sems["x3_ready"], ST * (n + 1))
                    sp.dma_start(out[n].rearrange("(t p) d -> p t d", p=P), x3).then_inc(stored, 16)
            sp.wait_ge(stored, 16 * B)

        @block.gpsimd
        def _(pool):
            steps = [0]

            def step(ins):
                steps[0] += 1
                ins.then_inc(sems["pool_step"], 1)
                pool.wait_ge(sems["pool_step"], steps[0])

            for m in (ident, identb):
                step(pool.memset(m[:, :], 0.0))
                pool.affine_select(out=m[:, :], in_=m[:, :], compare_op=ALU.not_equal, fill=1.0, base=0,
                                   pattern=[[-1, P]], channel_multiplier=1).then_inc(sems["identities"], 1)
            pool.memset(half[:, :, :], -0.5).then_inc(sems["constants"], 1)

            def dequantise(raw, scale, loaded, done):
                pool.wait_ge(loaded, 32)
                flat = raw.rearrange("p a b -> p (a b)")
                step(pool.tensor_scalar(flat, flat.bitcast(i32), -7.5, 1.0, ALU.add, ALU.mult))
                blocks = flat.rearrange("p (k q) -> p k q", q=QB)
                sc = scale[:, :, :].rearrange("p a k -> p (a k)").unsqueeze(2)
                pool.tensor_tensor(blocks, blocks, sc.broadcast_to(blocks.shape), ALU.mult).then_inc(done, 1)

            norms = [0]

            def inverse_root():
                norms[0] += 1
                pool.wait_ge(sems["moments_ready"], norms[0])
                step(pool.tensor_scalar(rstd[:, :, :], moments[:, :, 1:2], EPS, 1.0, ALU.add, ALU.mult))
                pool.tensor_tensor(rstd[:, :, :], rstd[:, :, :], half[:, :, :], ALU.pow).then_inc(sems["rstd_ready"], 1)

            pool.wait_ge(sems["constants"], 1)
            for stage, n in order:
                if stage == "q":
                    b = n
                    pool.wait_ge(sems["qf_ready"], b + 1)
                    if b >= 1:
                        in_bank(pool, "mem", (b - 1, ST - 1))
                    step(pool.tensor_scalar(q_neg, qf[:, b % 2], 0.0, 1.0, ALU.min, ALU.mult))
                    pool.tensor_tensor(sigma, qf[:, b % 2], q_neg, ALU.subtract).then_inc(sems["q_split"], 1)
                if stage == "mem":
                    b, t = n
                    pool.wait_ge(sems["memterm_ready"], ST * b + t + 1)
                    in_bank(pool, "xT", b)
                    pool.tensor_tensor(xs[:, b, t], xs[:, b, t], memterm[:, :], ALU.add).then_inc(sems["residual"], 1)
                if stage == "mem" and n == (2, 0):
                    dequantise(up_raw, upscale, sems["ld_up_w"], sems["up_dequant"])
                if stage == "mem" and n == (3, 1):
                    dequantise(dn_raw, dnscale, sems["ld_dn_w"], sems["dn_dequant"])
                if stage == "max" and n[1] == SUB - 1:
                    u = n[0]
                    pool.wait_ge(sems["max_taken"], SUB * (u + 1))
                    if u >= 2:
                        in_bank(pool, "maxT", u - 2)
                    parts = max_parts[:, u % 2].rearrange("p t g h n -> p (t g h) n")
                    m = maxes[:, u % 2].rearrange("p t g q h -> p (t g q h)")
                    step(pool.tensor_copy(parts[:, :, 0], m))
                    pool.tensor_tensor(parts[:, :, 1], m, parts[:, :, 0], ALU.subtract).then_inc(sems["max_split"], 1)
                if stage in ("ln1_stats", "ln2_stats", "ln3_stats"):
                    inverse_root()
                if stage == "ln2":
                    b = n
                    pool.wait_ge(sems["x2_ready"], ST * (b + 1))
                    pool.wait_ge(sems["ld_biases"], 32)
                    pool.tensor_tensor(x2b, x2, dnbias[:, :].unsqueeze(1).broadcast_to([P, ST, D]), ALU.add)\
                        .then_inc(sems["x2b_ready"], 1)
                if stage == "x2T" and n < B - 1:
                    pool.wait_ge(sems["x2_hi_done"], n + 1)
                    pool.tensor_tensor(x2_lo[:, :, :], x2T, x2_hi[:, :, :].bitcast(fp32), ALU.subtract)\
                        .then_inc(sems["x2_lo_done"], 1)
                if stage == "up" and n[0] < B - 1:
                    b, j = n
                    i = b * (FC // 2) + j
                    pool.wait_ge(sems["y_hi_done"], i + 1)
                    pool.tensor_tensor(y_lo[:, 2 * j:2 * j + 2].rearrange("p c t -> p (c t)"), yf[:, i % 2],
                                       y_hi[:, 2 * j:2 * j + 2].rearrange("p c t -> p (c t)").bitcast(fp32),
                                       ALU.subtract).then_inc(sems["y_lo_done"], 1)

        @block.scalar
        def _(act):
            for stage, n in order:
                if stage == "wqT":
                    src = in_bank(act, stage)[:, :].rearrange("p (c g q a r) -> p c g r a q", c=CC, g=QP, q=QQ, a=HP)
                    for c in range(CC):
                        for g in range(QP):
                            act.activation(wqT[:, c, g].rearrange("p (r a q) -> p r a q", a=HP, q=QQ),
                                           src[:, c, g], ACT.Copy).then_inc(sems["wqT_ready"], 1)
                if stage == "wkvT":
                    src = in_bank(act, stage)[:, 0:CC * P].rearrange("p (c o) -> p c o", c=CC)
                    for c in range(CC):
                        act.activation(wkvT[:, c, 0:KV].rearrange("p (r a) -> p r a", a=HP),
                                       src[:, c, 0:KV].rearrange("p (a r) -> p r a", a=HP), ACT.Copy)\
                            .then_inc(sems["wkvT_ready"], 1)
                    act.activation(wkvT[:, :, KV:P], src[:, :, KV:P], ACT.Copy).then_inc(sems["wkvT_ready"], 1)
                if stage == "xT":
                    if n >= 2:
                        in_bank(act, "kv", n - 2)
                    ps = in_bank(act, stage, n)
                    act.activation(xT[:, n % 2].rearrange("p c t -> p (c t)"), ps[:, :], ACT.Copy)\
                        .then_inc(sems["xT_ready"], 1)
                if stage == "xT" and n == 0:
                    act.wait_ge(sems["ld_weight"], 16)
                    act.activation(mix[:, 1:2], mix[:, 0:1], ACT.Exp, scale=-1.0).then_inc(sems["mix_exp"], 1)
                if stage == "q":
                    if n >= 2:
                        act.wait_ge(sems["q_parts_ready"], n - 1)
                        act.wait_ge(sems["q_split"], n - 1)
                    ps = in_bank(act, stage, n)
                    act.activation(qf[:, n % 2].rearrange("p c t -> p (c t)"), ps[:, :], ACT.Copy)\
                        .then_inc(sems["qf_ready"], 1)
                if stage == "kv":
                    ps = in_bank(act, stage, n)
                    if n == 0:
                        act.wait_ge(sems["masks"], 5)
                        act.wait_ge(sems["mix_ready"], 3)
                        act.wait_ge(sems["v_zeroed"], 1)
                    if n >= 1:
                        act.wait_ge(sems["k_parts_ready"], n)
                    for hh in range(HH):
                        act.activation(kf[:, hh], ps[0:KV, 0:S], ACT.Copy, scale=head_mask[:, hh:hh + 1])\
                            .then_inc(sems["kf_ready"], 1)
                    for t in range(ST):
                        act.activation(V[:, n, t, :, 0:DH],
                                       ps[:, S + t * KV:S + (t + 1) * KV].rearrange("p (h d) -> p h d", h=H),
                                       ACT.Copy, scale=mix[:, 4:5]).then_inc(sems["v_ready"], 1)
                    act.wait_ge(sems["q_split"], n + 1)
                    act.activation(q_neg, q_neg, ACT.Exp).then_inc(sems["q_exp"], 1)
                if stage == "xwT":
                    ps = in_bank(act, stage)
                    act.activation(xwT[:, :, :].rearrange("p c t -> p (c t)"), ps[:, 0:2 * C], ACT.Copy)\
                        .then_inc(sems["xwT_ready"], 1)
                if stage == "ctxT":
                    ps = in_bank(act, stage, n)
                    act.activation(ctxT[:, n * 512:(n + 1) * 512], ps[:, :], ACT.Copy).then_inc(sems["ctxT_ready"], 1)
                if stage in ("xq", "xk"):
                    ps = in_bank(act, stage, n)
                    to, k, done = (xq, 0, sems["xq_ready"]) if stage == "xq" else (xk, 1, sems["xk_ready"])
                    act.activation(to[:, n * 512:(n + 1) * 512], ps[:, :], ACT.Identity, bias=xb[:, k:k + 1])\
                        .then_inc(done, 1)
                if stage == "loraT":
                    ps = in_bank(act, stage, n)
                    to = lora_up_aT if n == 0 else lora_dn_aT[:, (n - 1) * 512:n * 512]
                    act.activation(to, ps[0:R, 0:to.shape[1]], ACT.Copy).then_inc(sems["loraT_ready"], 1)
                if stage == "energy":
                    b = n
                    act.wait_ge(sems["energy_max"], b + 1)
                    if b >= 1:
                        in_bank(act, "xattnT", b - 1)
                    ps = in_bank(act, stage, b)
                    for t in range(ST):
                        act.activation(energy[:, t], ps[:, t * S:(t + 1) * S], ACT.Exp,
                                       bias=energy_stat[:, b, 0, t:t + 1],
                                       accum_out=energy_stat[:, b, 1, t:t + 1]).then_inc(sems["energy_exp"], 1)
                if stage == "xattnT":
                    ps = in_bank(act, stage, n)
                    act.activation(xattnT[:, n].rearrange("p c t -> p (c t)"), ps[:, :], ACT.Copy)\
                        .then_inc(sems["xattnT_ready"], 1)
                if stage == "up_w":
                    ps = in_bank(act, stage, n)
                    c, half_f = divmod(n, 2)
                    act.activation(up_hi[:, c, half_f * 512:(half_f + 1) * 512], ps[:, :], ACT.Copy)\
                        .then_inc(sems["w_hi_ready"], 1)
                if stage == "dn_w":
                    ps = in_bank(act, stage, n)
                    act.activation(dn_hi[:, 2 * n:2 * n + 2].rearrange("p c t -> p (c t)"), ps[:, :], ACT.Copy)\
                        .then_inc(sems["w_hi_ready"], 1)
                if stage == "maxT":
                    u = n
                    ps = in_bank(act, stage, u)
                    if u >= 2:
                        act.wait_ge(max_loaded[u % 2], 16 * G * (u // 2))
                    act.activation(maxT[:, u % 2, :], ps[0:G * MROWS, :].bitcast(bf16)[:, 0:S], ACT.Copy)\
                        .then_inc(sems["maxT_ready"], 1)
                if stage == "exp":
                    u, i = n
                    k = u * SUB + i
                    act.wait_ge(sems["exp_scores"], k + 1)
                    h, j = divmod(k, QP * HH)
                    if h >= 3 and j == 0:
                        act.wait_ge(sems["pv_done"], h - 2)
                    act.activation(probs[:, (h % 3) * QP * HH + j], exp_bank[k % 3][:, :], ACT.Exp, scale=SCALE)\
                        .then_inc(sems["probs_ready"], 1)
                if stage == "pv" and n[1] == ST - 1:
                    u = n[0]
                    act.wait_ge(sems["pv_done"], ST * (u + 1))
                    if u >= 2:
                        in_bank(act, "spread", u - 2)
                    act.activation(avT[:, u % 2], pv_bank[:, :], ACT.Copy).then_inc(sems["avT_ready"], 1)
                if stage == "x1T":
                    if n >= 1:
                        in_bank(act, "cross", n - 1)
                    ps = in_bank(act, stage, n)
                    act.activation(x1T.rearrange("p c t -> p (c t)"), ps[:, :], ACT.Copy).then_inc(sems["x1T_ready"], 1)
                if stage == "x2T":
                    if n >= 1:
                        act.wait_ge(sems["x2_lo_done"], n)
                    ps = in_bank(act, stage, n)
                    act.activation(x2T.rearrange("p c t -> p (c t)"), ps[:, :], ACT.Copy).then_inc(sems["x2T_ready"], 1)
                if stage == "up":
                    b, j = n
                    i = b * (FC // 2) + j
                    if i == 0:
                        act.wait_ge(sems["ld_biases"], 32)
                    if b == B - 1 and j >= 2:
                        act.wait_ge(sems["y_lo_last"], j - 1)
                    elif i >= 2:
                        act.wait_ge(sems["y_lo_done"], i - 1)
                    ps = in_bank(act, stage, n)
                    for a in range(2):
                        act.activation(yf[:, i % 2, a * S:(a + 1) * S], ps[:, a * S:(a + 1) * S], ACT.Relu,
                                       bias=upbias[:, 2 * j + a:2 * j + a + 1]).then_inc(sems["yf_ready"], 1)

        @block.tensor
        def _(pe):
            def claim(stage, n=0, first=True):
                i = SLOT[stage, n]
                if first and i >= 2:
                    before, m = in_turn[i - 2]
                    pe.wait_ge(*release[before](m))
                return shared[i % 2], shared_full[i % 2]

            def turn(to, src, n=P):
                return pe.transpose(to, src, ident[0:n, 0:n])

            pe.wait_ge(sems["identities"], 2)
            for stage, n in order:
                begin = stage == "begin"
                halves = (0,) if begin else (1,)
                if begin:
                    stage, n = n
                if stage == "wqT":
                    pe.wait_ge(sems["ld_wq"], 16)
                    ps, full = claim(stage)
                    for c in range(CC):
                        for o in range(CC):
                            last = turn(ps[:, c * D + o * P:c * D + (o + 1) * P], wq_nat[:, o, c * P:(c + 1) * P])
                    last.then_inc(full, 1)
                if stage == "wkvT":
                    pe.wait_ge(sems["ld_wkv"], 32)
                    ps, full = claim(stage)
                    for c in range(CC):
                        last = turn(ps[:, c * P:(c + 1) * P], wkv_nat[:, c * P:(c + 1) * P])
                    last.then_inc(full, 1)
                if stage == "xT":
                    pe.wait_ge(ld_x[n], 16)
                    ps, full = claim(stage, n)
                    for c in range(CC):
                        for t in range(ST):
                            last = turn(ps[:, c * S + t * P:c * S + (t + 1) * P], xs[:, n, t, c * P:(c + 1) * P])
                    last.then_inc(full, 1)
                if stage == "q":
                    if begin:
                        pe.wait_ge(sems["xT_ready"], n + 1)
                        pe.wait_ge(sems["wqT_ready"], CC * QP)
                    ps, full = claim(stage, n, begin)
                    for g in halves:
                        for c in range(CC):
                            last = pe.matmul(ps[:, g * S:(g + 1) * S], wqT[:, c, g, :], xT[:, n % 2, c, :],
                                             start=c == 0, stop=c == CC - 1)
                    if not begin:
                        last.then_inc(full, 1)
                if stage == "kv":
                    pe.wait_ge(sems["wkvT_ready"], CC + 1)
                    ps, full = claim(stage, n)
                    for c in range(CC):
                        pe.matmul(ps[0:KV, 0:S], wkvT[:, c, 0:KV], xT[:, n % 2, c, :], start=c == 0, stop=c == CC - 1)
                    for t in range(ST):
                        for c in range(CC):
                            last = pe.matmul(ps[:, S + t * KV:S + (t + 1) * KV], xT[:, n % 2, c, t * P:(t + 1) * P],
                                             wkvT[:, c, KV:P], start=c == 0, stop=c == CC - 1)
                    last.then_inc(full, 1)
                if stage == "mem_rhs":
                    pe.wait_ge(sems["ld_memory"], 32)
                    ps, full = claim(stage)
                    pe.wait_ge(sems["masks"], 6)
                    pe.matmul(ps[:, 0:KV + 1], pick[:, :], mem_nat[:, :], start=True, stop=True).then_inc(full, 1)
                if stage == "mem":
                    b, t = n
                    pe.wait_ge(sems["mem_rhs_ready"], 2 * QQ)
                    pe.wait_ge(sems["sigma_ready"], b + 1)
                    ps, full = claim(stage, n)
                    width = QQ * (KV + 1)
                    for g in range(QP):
                        last = pe.matmul(ps[:, g * width:(g + 1) * width], sigma[:, g, t * P:(t + 1) * P],
                                         mem_rhs[:, :, :].rearrange("p q e -> p (q e)"), start=True, stop=True)
                    last.then_inc(full, 1)
                if stage == "xwT":
                    pe.wait_ge(sems["ld_cross_w"], 64)
                    ps, full = claim(stage)
                    for k in range(2):
                        last = turn(ps[:, k * C:(k + 1) * C], xw_nat[:, k, :])
                    last.then_inc(full, 1)
                if stage == "ctxT":
                    pe.wait_ge(sems["ld_context"], 16)
                    ps, full = claim(stage, n)
                    for k in range(4):
                        last = turn(ps[:, k * P:(k + 1) * P], ctx_nat[:, 4 * n + k, :])
                    last.then_inc(full, 1)
                if stage in ("xq", "xk"):
                    pe.wait_ge(sems["xwT_ready"], 1)
                    pe.wait_ge(sems["ctxT_ready"], n + 1)
                    ps, full = claim(stage, n)
                    pe.matmul(ps[:, :], xwT[:, 0 if stage == "xq" else 1, :], ctxT[:, n * 512:(n + 1) * 512],
                              start=True, stop=True).then_inc(full, 1)
                if stage == "loraT":
                    pe.wait_ge(sems["ld_lora"], 64)
                    ps, full = claim(stage, n)
                    tiles = [lora_up_a[:, c, :] for c in range(CC)] if n == 0 else \
                        [lora_dn_a[:, 4 * (n - 1) + k, :] for k in range(4)]
                    for k, tile in enumerate(tiles):
                        last = turn(ps[0:R, k * P:(k + 1) * P], tile)
                    last.then_inc(full, 1)
                if stage == "energy":
                    pe.wait_ge(sems["xq_ready"], n // 2 + 1)
                    pe.wait_ge(sems["xk_ready"], n // 2 + 1)
                    ps, full = claim(stage, n)
                    for t in range(ST):
                        last = pe.matmul(ps[:, t * S:(t + 1) * S], xq[:, n * S + t * P:n * S + (t + 1) * P],
                                         xk[:, n * S:(n + 1) * S], start=True, stop=True)
                    last.then_inc(full, 1)
                if stage == "xattnT":
                    pe.wait_ge(sems["xattn_ready"], ST * (n + 1))
                    ps, full = claim(stage, n)
                    for c in range(ST):
                        for t in range(ST):
                            last = turn(ps[:, c * S + t * P:c * S + (t + 1) * P], energy[:, t, c * P:(c + 1) * P])
                    last.then_inc(full, 1)
                if stage == "up_w":
                    c, half_f = divmod(n, 2)
                    pe.wait_ge(sems["loraT_ready"], 3)
                    pe.wait_ge(sems["up_dequant"], 1)
                    ps, full = claim(stage, n)
                    pe.matmul(ps[:, :], lora_up_aT[:, c * P:(c + 1) * P], lora_up_b[:, half_f * 512:(half_f + 1) * 512],
                              start=True, stop=False)
                    for k in range(4):
                        last = pe.matmul(ps[:, k * P:(k + 1) * P], up_raw[:, 4 * half_f + k, c * P:(c + 1) * P],
                                         ident[:, :], start=False, stop=k == 3)
                    last.then_inc(full, 1)
                if stage == "dn_w":
                    pe.wait_ge(sems["dn_dequant"], 1)
                    ps, full = claim(stage, n)
                    for a in range(2):
                        f = slice((2 * n + a) * P, (2 * n + a + 1) * P)
                        pe.matmul(ps[:, a * D:(a + 1) * D], lora_dn_aT[:, f], lora_dn_b, start=True, stop=False)
                        for c in range(CC):
                            last = pe.matmul(ps[:, a * D + c * P:a * D + (c + 1) * P], dn_raw[:, c, f], ident[:, :],
                                             start=False, stop=c == CC - 1)
                    last.then_inc(full, 1)
                if stage == "max":
                    u, i = n
                    b, hp = divmod(u, HP)
                    k = u * SUB + i
                    gq, t = divmod(i, ST)
                    if i == 0 and hp == 0:
                        pe.wait_ge(qk_loaded[b], 16 * 3 * (QP + 1))
                    if k >= 2:
                        pe.wait_ge(sems["max_taken"], k - 1)
                    pe.matmul(max_bank[k % 2][:, :], QT[0:ROWS, b, gq // QQ, hp, gq % QQ, t * P:(t + 1) * P],
                              KT[0:ROWS, b, hp].rearrange("p h t -> p (h t)"), start=True, stop=True)\
                        .then_inc(sems["max_scores"], 1)
                if stage == "maxT":
                    u = n
                    pe.wait_ge(sems["max_split"], u + 1)
                    ps, full = claim(stage, u)
                    for t in range(ST):
                        last = pe.transpose(ps[0:G * MROWS, :].bitcast(bf16)[:, t * P:(t + 1) * P],
                                            max_parts[:, u % 2, t].rearrange("p g h n -> p (g h n)"), identb[:, :])
                    last.then_inc(full, 1)
                if stage == "exp":
                    u, i = n
                    b, hp = divmod(u, HP)
                    k = u * SUB + i
                    t, g, hh = i // (QP * HH), i // HH % QP, i % HH
                    if i == 0:
                        pe.wait_ge(max_loaded[u % 2], 16 * G * (u // 2 + 1))
                        pe.wait_ge(sems["k_rows"], 16)
                    if k >= 3:
                        pe.wait_ge(sems["probs_ready"], k - 2)
                    pe.matmul(exp_bank[k % 3][:, :], KT[0:ROWS + MROWS, b, hp, hh, t * P:(t + 1) * P],
                              QT[0:ROWS + MROWS, b, g, hp].rearrange("p q t -> p (q t)"), start=True, stop=True)\
                        .then_inc(sems["exp_scores"], 1)
                if stage == "pv":
                    u, t = n
                    b, hp = divmod(u, HP)
                    h = ST * u + t
                    pe.wait_ge(sems["probs_ready"], QP * HH * (h + 1))
                    if t == 0:
                        pe.wait_ge(sems["v_ready"], ST * (b + 1))
                    if u >= 1 and t == 0:
                        pe.wait_ge(sems["avT_ready"], u)
                    for hh in range(HH):
                        for g in range(QP):
                            j = hh * QP + g
                            last = pe.matmul(pv_bank[j * VC:(j + 1) * VC, :], V[:, b, t, HH * hp + hh, :],
                                             probs[:, (h % 3) * QP * HH + g * HH + hh],
                                             start=t == 0, stop=t == ST - 1)
                    last.then_inc(sems["pv_done"], 1)
                if stage == "spread":
                    u = n
                    pe.wait_ge(sems["avT_ready"], u + 1)
                    ps, full = claim(stage, u)
                    cols = ps[:, :].rearrange("p (t j q c) -> p t q j c", t=ST, j=HH * QP, q=QQ)
                    for q in range(QQ):
                        for t in range(ST):
                            last = turn(cols[:, t, q], avT[:, u % 2, (q * ST + t) * P:(q * ST + t + 1) * P])
                    last.then_inc(full, 1)
                if stage in ("x1T", "x2T"):
                    src, ready = (x1, sems["x1_ready"]) if stage == "x1T" else (x2, sems["x2_ready"])
                    pe.wait_ge(ready, ST * (n + 1))
                    ps, full = claim(stage, n)
                    for c in range(CC):
                        for t in range(ST):
                            last = turn(ps[:, c * S + t * P:c * S + (t + 1) * P], src[:, t, c * P:(c + 1) * P])
                    last.then_inc(full, 1)
                if stage == "cross":
                    if begin:
                        pe.wait_ge(sems["x1T_ready"], n + 1)
                        pe.wait_ge(sems["xattnT_ready"], n + 1)
                    ps, full = claim(stage, n, begin)
                    for t in halves:
                        for c in range(CC):
                            last = pe.matmul(ps[:, t * S:(t + 1) * S], x1T[:, c, t * P:(t + 1) * P], xattnT[:, n, c, :],
                                             start=c == 0, stop=c == CC - 1)
                    if not begin:
                        last.then_inc(full, 1)
                if stage == "up":
                    b, j = n
                    if begin:
                        pe.wait_ge(sems["x2_lo_done"] if b < B - 1 else sems["x2_lo_last"], b + 1 if b < B - 1 else 1)
                        pe.wait_ge(sems["w_ready"], 8)
                    ps, full = claim(stage, n, begin)
                    for a in halves:
                        f = slice((2 * j + a) * P, (2 * j + a + 1) * P)
                        products = [(w, xx, c) for c in range(CC)
                                    for w, xx in ((up_hi, x2_hi), (up_hi, x2_lo), (up_lo, x2_hi))]
                        for m, (w, xx, c) in enumerate(products):
                            last = pe.matmul(ps[:, a * S:(a + 1) * S], w[:, c, f], xx[:, c, :],
                                             start=m == 0, stop=m == len(products) - 1)
                    if not begin:
                        last.then_inc(full, 1)
                if stage == "down":
                    b, t = n
                    if begin and b < B - 1:
                        pe.wait_ge(sems["y_lo_done"], (FC // 2) * (b + 1))
                    elif begin:
                        pe.wait_ge(sems["y_lo_last"], FC // 2)
                    ps, full = claim(stage, n, begin)
                    for f in range(FC // 2 * halves[0], FC // 2 * (halves[0] + 1)):
                        for m, (yy, w) in enumerate(((y_hi, dn_hi), (y_hi, dn_lo), (y_lo, dn_hi))):
                            last = pe.matmul(ps[:, 0:D], yy[:, f, t * P:(t + 1) * P], w[:, f, :],
                                             start=(f, m) == (0, 0), stop=(f, m) == (FC - 1, 2))
                    if not begin:
                        last.then_inc(full, 1)

        @block.vector
        def _(dve):
            steps = [0]

            def step(ins):
                steps[0] += 1
                ins.then_inc(sems["dve_step"], 1)
                dve.wait_ge(sems["dve_step"], steps[0])

            for hh in range(HH):
                own, other = (0.0, -1.0) if hh else (-1.0, 0.0)
                step(dve.memset(k_pattern[:, hh, :], other))
                dve.memset(k_pattern[0:2, hh, :], own).then_inc(sems["k_pattern_ready"], 2)
            for hh in range(HH):
                for row in range(HH):
                    dve.memset(head_mask[row * 32:(row + 1) * 32, hh:hh + 1], float(row == hh)).then_inc(sems["masks"], 1)
            dve.wait_ge(sems["identities"], 1)
            dve.tensor_reduce(group_mask[:, :], ident[:, :].rearrange("p (j q) -> p q j", q=QQ), X, ALU.add)\
                .then_inc(sems["masks"], 1)
            dve.tensor_copy(pick[:, :].rearrange("k (r a q) -> k r a q", a=HP, q=QQ),
                            ident[0:KV, 0:KV].rearrange("k (a r) -> k r a", a=HP).unsqueeze(3)
                            .broadcast_to([KV, HD, HP, QQ])).then_inc(sems["masks"], 1)
            step(dve.memset(V[:, :, :, :, :], 0.0))
            dve.memset(V[:, :, :, :, DH:DH + 1], 1.0).then_inc(sems["v_zeroed"], 1)
            def split3(parts, src, spare, done):
                step(dve.tensor_copy(parts[:, 0], src))
                step(dve.tensor_tensor(spare, src, parts[:, 0], ALU.subtract))
                step(dve.tensor_copy(parts[:, 1], spare))
                dve.tensor_tensor(parts[:, 2], spare, parts[:, 1], ALU.subtract).then_inc(done, 1)

            norms, normalised = [0], []

            def statistics(src):
                if normalised:
                    dve.wait_ge(*normalised.pop())
                for t in range(ST):
                    last = dve.bn_stats(stats[:, t, :], src[:, t])
                step(last)
                norms[0] += 1
                for t in range(ST):
                    last = dve.bn_aggr(moments[:, t, :], stats[:, t, :])
                last.then_inc(sems["moments_ready"], 1)

            def normalise(to, src, done, b):
                dve.wait_ge(sems["rstd_ready"], norms[0])
                dve.wait_ge(sems["moments_ready"], norms[0])
                for t in range(ST):
                    dve.tensor_scalar(to[:, t], src[:, t], moments[:, t, 0:1], rstd[:, t, :],
                                      ALU.subtract, ALU.mult).then_inc(done, 1)
                normalised.append((done, ST * (b + 1)))

            for stage, n in order:
                if stage == "q" and n == 0:
                    dve.wait_ge(sems["mix_exp"], 1)
                    dve.tensor_scalar(mix[:, 2:3], mix[:, 1:2], 1.0, None, ALU.add).then_inc(sems["mix_ready"], 1)
                    dve.wait_ge(sems["mix_ready"], 1)
                    dve.reciprocal(mix[:, 3:4], mix[:, 2:3]).then_inc(sems["mix_ready"], 1)
                    dve.wait_ge(sems["mix_ready"], 2)
                    dve.tensor_scalar(mix[:, 4:5], mix[:, 3:4], -1.0, 1.0, ALU.mult, ALU.add).then_inc(sems["mix_ready"], 1)
                if stage == "q":
                    dve.wait_ge(sems["qf_ready"], n + 1)
                    if n >= 1:
                        dve.wait_ge(sems["k_parts_ready"], n)
                        dve.wait_ge(q_written[n - 1], 16 * QP)
                    split3(q_parts, qf[:, n % 2], rest[:, :].rearrange("p (c t) -> p c t", c=QP), sems["q_parts_ready"])
                if stage == "kv":
                    dve.wait_ge(sems["kf_ready"], HH * (n + 1))
                    if n >= 1:
                        dve.wait_ge(k_written[n - 1], 16)
                    dve.wait_ge(sems["q_parts_ready"], n + 1)
                    split3(k_parts, kf, rest[0:KV, :].rearrange("p (c t) -> p c t", c=HH), sems["k_parts_ready"])
                    dve.wait_ge(sems["q_exp"], n + 1)
                    dve.scalar_tensor_tensor(out=sigma, in0=q_neg, scalar=-1.0, in1=sigma, op0=ALU.add, op1=ALU.add)\
                        .then_inc(sems["sigma_ready"], 1)
                if stage == "mem_rhs":
                    ps = in_bank(dve, stage)
                    dve.wait_ge(sems["mix_ready"], 3)
                    dve.wait_ge(sems["masks"], 5)
                    for q in range(QQ):
                        dve.tensor_scalar(mem_rhs[:, q, 0:KV], ps[:, 0:KV], group_mask[:, q:q + 1], mix[:, 3:4],
                                          ALU.mult, ALU.mult).then_inc(sems["mem_rhs_ready"], 1)
                        dve.tensor_scalar(mem_rhs[:, q, KV:KV + 1], ps[:, KV:KV + 1], group_mask[:, q:q + 1], None,
                                          ALU.mult).then_inc(sems["mem_rhs_ready"], 1)
                if stage == "mem":
                    b, t = n
                    ps = in_bank(dve, stage, n)[:, 0:G * (KV + 1)].rearrange("p (g e) -> p g e", g=G)
                    if n != (0, 0):
                        dve.wait_ge(sems["memterm_ready"], ST * b + t)
                    step(dve.reciprocal(memrec[:, :], ps[:, :, KV]))
                    if n != (0, 0):
                        dve.wait_ge(sems["residual"], ST * b + t)
                    dve.tensor_tensor(memterm[:, :].rearrange("p (g e) -> p g e", g=G), ps[:, :, 0:KV],
                                      memrec[:, :].unsqueeze(2).broadcast_to([P, G, KV]), ALU.mult)\
                        .then_inc(sems["memterm_ready"], 1)
                if stage == "energy":
                    ps = in_bank(dve, stage, n)
                    dve.tensor_reduce(energy_stat[:, n, 0, :], ps[:, :].rearrange("p (t c) -> p t c", t=ST), X, ALU.max,
                                      negate=True).then_inc(sems["energy_max"], 1)
                if stage == "xattnT":
                    dve.wait_ge(sems["energy_exp"], ST * (n + 1))
                    step(dve.reciprocal(energy_stat[:, n, 2, :], energy_stat[:, n, 1, :]))
                    for t in range(ST):
                        dve.tensor_scalar(energy[:, t], energy[:, t], energy_stat[:, n, 2, t:t + 1], None, ALU.mult)\
                            .then_inc(sems["xattn_ready"], 1)
                if stage in ("up_w", "dn_w"):
                    i = n + (4 if stage == "dn_w" else 0)
                    dve.wait_ge(sems["w_hi_ready"], i + 1)
                    ps = in_bank(dve, stage, n)
                    if stage == "up_w":
                        c, half_f = divmod(n, 2)
                        hi, lo = (m[:, c, half_f * 512:(half_f + 1) * 512] for m in (up_hi, up_lo))
                    else:
                        hi, lo = (m[:, 2 * n:2 * n + 2].rearrange("p c t -> p (c t)") for m in (dn_hi, dn_lo))
                    dve.tensor_tensor(lo, ps[:, :], hi.bitcast(fp32), ALU.subtract).then_inc(sems["w_ready"], 1)
                if stage == "max":
                    u, i = n
                    k = u * SUB + i
                    gq, t = divmod(i, ST)
                    if u >= 2 and i == 0:
                        dve.wait_ge(sems["max_split"], u - 1)
                    dve.wait_ge(sems["max_scores"], k + 1)
                    dve.tensor_reduce(maxes[:, u % 2, t, gq // QQ, gq % QQ, :],
                                      max_bank[k % 2][:, :].rearrange("p (h t) -> p h t", h=HH), X, ALU.max)\
                        .then_inc(sems["max_taken"], 1)
                if stage == "spread":
                    u = n
                    b, hp = divmod(u, HP)
                    ps = in_bank(dve, stage, u)[:, :].rearrange("p (t h g c) -> p t h g c", t=ST, h=HH, g=G)
                    r = rec[:, u % 2, :].rearrange("p (t h g) -> p t h g", t=ST, h=HH)
                    if u >= 2:
                        dve.wait_ge(sems["adot_ready"], ST * (u - 1))
                    step(dve.reciprocal(r.rearrange("p t h g -> p (t h g)"),
                                        ps.rearrange("p t h g c -> p (t h g) c")[:, :, DH]))
                    if b >= 2 and hp == 0:
                        dve.wait_ge(sems["attn_added"], b - 1)
                    for t in range(ST):
                        to = adot[:, b % 2, t].rearrange("p (g a h d) -> p a h g d", g=G, a=HP, h=HH)[:, hp]
                        dve.tensor_tensor(to, ps[:, t, :, :, 0:DH], r[:, t].unsqueeze(3).broadcast_to([P, HH, G, DH]),
                                          ALU.mult).then_inc(sems["adot_ready"], 1)
                if stage == "ln1_stats":
                    dve.wait_ge(sems["adot_ready"], ST * HP * (n + 1))
                    dve.wait_ge(sems["residual"], ST * (n + 1))
                    if n >= 1:
                        dve.wait_ge(sems["x2_ready"], ST * n)
                    dve.tensor_tensor(pre, xs[:, n], adot[:, n % 2], ALU.add).then_inc(sems["attn_added"], 1)
                    dve.wait_ge(sems["attn_added"], n + 1)
                    statistics(pre)
                if stage == "ln1":
                    if n >= 1:
                        dve.wait_ge(sems["cross_added"], n)
                    normalise(x1, pre, sems["x1_ready"], n)
                if stage == "cross":
                    ps = in_bank(dve, stage, n)
                    dve.wait_ge(sems["x1_ready"], ST * (n + 1))
                    dve.tensor_tensor(pre.rearrange("p t d -> p (t d)"), ps[:, :], x1.rearrange("p t d -> p (t d)"),
                                      ALU.add).then_inc(sems["cross_added"], 1)
                if stage == "ln2_stats":
                    dve.wait_ge(sems["cross_added"], n + 1)
                    statistics(pre)
                if stage == "ln2":
                    if n >= 1:
                        dve.wait_ge(sems["x2b_ready"], n)
                        in_bank(dve, "x2T", n - 1)
                    normalise(x2, pre, sems["x2_ready"], n)
                if stage == "x2T":
                    dve.wait_ge(sems["x2T_ready"], n + 1)
                    if n >= 1:
                        in_bank(dve, "up", (n - 1, FC // 2 - 1))
                    dve.tensor_copy(x2_hi[:, :, :], x2T).then_inc(sems["x2_hi_done"], 1)
                    if n == B - 1:
                        dve.wait_ge(sems["x2_hi_done"], n + 1)
                        dve.tensor_tensor(x2_lo[:, :, :], x2T, x2_hi[:, :, :].bitcast(fp32), ALU.subtract)\
                            .then_inc(sems["x2_lo_last"], 1)
                if stage == "up":
                    b, j = n
                    i = b * (FC // 2) + j
                    dve.wait_ge(sems["yf_ready"], 2 * (i + 1))
                    if b >= 1 and j == 0:
                        in_bank(dve, "down", (b - 1, ST - 1))
                    dve.tensor_copy(y_hi[:, 2 * j:2 * j + 2].rearrange("p c t -> p (c t)"), yf[:, i % 2])\
                        .then_inc(sems["y_hi_done"], 1)
                    if b == B - 1:
                        dve.wait_ge(sems["y_hi_done"], i + 1)
                        dve.tensor_tensor(y_lo[:, 2 * j:2 * j + 2].rearrange("p c t -> p (c t)"), yf[:, i % 2],
                                          y_hi[:, 2 * j:2 * j + 2].rearrange("p c t -> p (c t)").bitcast(fp32),
                                          ALU.subtract).then_inc(sems["y_lo_last"], 1)
                if stage == "down":
                    b, t = n
                    ps = in_bank(dve, stage, n)
                    dve.wait_ge(sems["x2b_ready"], b + 1)
                    dve.wait_ge(sems["x2_ready"], ST * (b + 1))
                    if b >= 1 and t == 0:
                        dve.wait_ge(sems["x3_ready"], ST * b)
                    dve.tensor_tensor(pre3[:, t], ps[:, 0:D], x2b[:, t], ALU.add).then_inc(sems["down_added"], 1)
                if stage == "ln3_stats":
                    dve.wait_ge(sems["down_added"], ST * (n + 1))
                    statistics(pre3)
                if stage == "ln3":
                    if n >= 1:
                        dve.wait_ge(stored, 16 * n)
                    normalise(x3, pre3, sems["x3_ready"], n)


_INS = ["x", "ctx_1024", "L0_attn_Wq", "L0_attn_Wk", "L0_attn_Wv", "L0_attn_memory", "L0_attn_memory_norm",
        "L0_attn_memory_weight", "L0_xattn_Wq", "L0_xattn_bq", "L0_xattn_Wk", "L0_xattn_bk",
        "L0_ffn_w_up_q", "L0_ffn_w_up_scale", "L0_ffn_b_up", "L0_ffn_w_up_lora_a", "L0_ffn_w_up_lora_b",
        "L0_ffn_w_down_q", "L0_ffn_w_down_scale", "L0_ffn_b_down", "L0_ffn_w_down_lora_a", "L0_ffn_w_down_lora_b"]


def kernel(**inputs):
    import numpy as _np
    import concourse.bacc as _bacc
    from concourse import mybir as _mybir
    from concourse.bass_utils import run_bass_kernel_spmd as _run

    nc = _bacc.Bacc("TRN2", target_bir_lowering=False, num_devices=1)
    arrays, args = {}, []
    for name in _INS:
        a = _np.ascontiguousarray(inputs[name])
        arrays[f"in_{name}"] = a
        args.append(nc.dram_tensor(f"in_{name}", a.shape, _mybir.dt.from_np(a.dtype), kind="ExternalInput").ap())
    shape = inputs["x"].shape
    args.append(nc.dram_tensor("out_0", shape, _mybir.dt.float32, kind="ExternalOutput").ap())
    build_decoder(nc, *args)
    r = _run(nc, [arrays], core_ids=[0])
    return r.results[0]["out_0"]
```

```python
import concourse.bass as bass
from concourse import mybir
from contextlib import ExitStack

import numpy as np


def build_decoder(nc, x, ctx, wq, wk, wv, memory, memory_norm, memory_weight, xwq, xbq, xwk, xbk,
                  up_q, up_scale, up_bias, up_a, up_b, dn_q, dn_scale, dn_bias, dn_a, dn_b, out):
    fp32, fp32r, bf16, i32 = mybir.dt.float32, mybir.dt.float32r, mybir.dt.bfloat16, mybir.dt.int32
    ALU = mybir.AluOpType
    ACT = mybir.ActivationFunctionType
    X = mybir.AxisListType.X

    P = 128
    B, S, D = x.shape
    KV = wk.shape[0]
    G, H = D // KV, 8
    DH = KV // H
    C = ctx.shape[2]
    F = up_q.shape[0]
    R = up_a.shape[1]
    QB = D // up_scale.shape[1]
    HP, HH = H // 2, 2
    QP, QQ = G // 2, 2
    ST, CC = S // P, D // P
    FC = F // P
    TERM_Q = (0, 0, 0, 1, 1, 2)
    TERM_K = (0, 1, 2, 0, 1, 0)
    TERMS = len(TERM_Q)
    HD = HH * DH
    ROWS = TERMS * HD
    MROWS = HH * 2
    LORA_TERM_A = (0, 1, 2, None, 0, 1, 0, None)
    LORA_TERMS = len(LORA_TERM_A)
    UNITS = B * HP
    SUB = 8
    RING = 3
    EXP_BANKS, MAX_BANKS, SHARED_BANKS = 2, 3, 2
    VC = 32
    EPS = 1e-5
    SCALE = float(np.float32(1.0 / np.sqrt(np.float32(DH))))

    q_scratch = nc.dram_tensor("q_scratch", [B, 3, QP, HD, HP * QQ * S], bf16, kind="Internal").ap()
    k_scratch = nc.dram_tensor("k_scratch", [B, 3, HD, HP * HH * S], bf16, kind="Internal").ap()

    stack = ExitStack()
    with stack:
        def sb(name, shape, dt):
            return stack.enter_context(nc.sbuf_tensor(name, shape, dt))

        def sem(name):
            return stack.enter_context(nc.semaphore(name))

        ident = sb("ident", [P, P], fp32)
        identb = sb("identb", [P, P], bf16)
        pick = sb("pick", [KV, P], fp32)
        group_mask = sb("group_mask", [P, QQ], fp32)
        head_mask = sb("head_mask", [2 * 32, HH], fp32)
        xs = sb("xs", [P, B, ST, D], fp32)
        wq_nat = sb("wq_nat", [P, CC, D], fp32)
        wkv_nat = sb("wkv_nat", [P, D], fp32)
        wqT = sb("wqT", [P, CC, QP, P], fp32)
        wkvT = sb("wkvT", [P, CC, P], fp32)
        mem_nat = sb("mem_nat", [KV, KV + 1], fp32)
        mem_rhs = sb("mem_rhs", [P, QQ, KV + 1], fp32)
        mix = sb("mix", [P, 8], fp32)
        QT = sb("QT", [P, B, QP, HP, QQ, S], bf16)
        KT = sb("KT", [P, B, HP, HH, S], bf16)
        k_pattern = sb("k_pattern", [MROWS, HH, S], bf16)
        V = sb("V", [P, B, ST, H, VC], fp32)
        xattnT = sb("xattnT", [P, B, ST, S], fp32)
        energy = sb("energy", [P, ST, S], fp32)
        energy_stat = sb("energy_stat", [P, B, 3, ST], fp32)
        xw_nat = sb("xw_nat", [P, 2, C], fp32)
        xwT = sb("xwT", [P, 2, C], fp32)
        xb = sb("xb", [P, 2], fp32)
        upscale = sb("upscale", [P, FC, D // QB], fp32)
        dnscale = sb("dnscale", [P, CC, F // QB], fp32)
        upbias = sb("upbias", [P, FC], fp32)
        dnbias = sb("dnbias", [P, D], fp32)
        lora_a = sb("lora_a", [P, CC + FC, R], fp32)
        lora_b_parts = sb("lora_b_parts", [P, F + D], bf16)
        lora_aT = sb("lora_aT", [P, CC + FC, P], bf16)
        up_hi = sb("up_hi", [P, CC, F], fp32r)
        up_lo = sb("up_lo", [P, CC, F], fp32r)
        x2_hi = sb("x2_hi", [P, CC, S], fp32r)
        x2_lo = sb("x2_lo", [P, CC, S], fp32r)
        maxes = sb("maxes", [P, 2, ST, QP, QQ, HH], fp32)
        max_parts = sb("max_parts", [P, 2, ST, G, HH, 2], bf16)
        rec = sb("rec", [P, 2, 16], fp32)
        memrec = sb("memrec", [P, G], fp32)
        memterm = sb("memterm", [P, D], fp32)
        stats = sb("stats", [P, ST, 6], fp32)
        moments = sb("moments", [P, ST, 2], fp32)
        rstd = sb("rstd", [P, ST, 1], fp32)
        half = sb("half", [P, ST, 1], fp32)

        probs = sb("probs", [P, RING * QP * HH, 512], fp32)
        avT = sb("avT", [P, 2, 512], fp32)
        adot = sb("adot", [P, 2, ST, D], fp32)

        with nc.sbuf_tensor("early", [P, 2 * (FC * S + FC * D)], fp32) as early:
            up_raw = early[:, 0:FC * D].rearrange("p (a b) -> p a b", a=FC)
            dn_raw = early[:, FC * S:FC * S + CC * F].rearrange("p (a b) -> p a b", a=CC)
            late = 2 * FC * S
            ctx_nat = early[:, late:late + 1024].rearrange("p (a b) -> p a b", a=B * ST)
            lora_a_parts = early[:, late:late + 640].bitcast(bf16).rearrange("p (k n r) -> p k n r", n=LORA_TERMS, r=R)
            ctxT = early[:, late + 1024:late + 2048]
            xq = early[:, late + 2048:late + 3072]
            xk = early[:, late + 3072:late + 4096]
        y_hi = sb("y_hi", [P, FC, S], fp32r)
        y_lo = sb("y_lo", [P, FC, S], fp32r)
        dn_hi = sb("dn_hi", [P, FC, D], fp32r)
        dn_lo = sb("dn_lo", [P, FC, D], fp32r)

        arena_b = sb("arena_b", [P, 6656], fp32)
        xT = arena_b[:, 0:1024].rearrange("p (n c s) -> p n c s", n=2, c=CC)
        qf = arena_b[:, 1024:2048].rearrange("p (n c s) -> p n c s", n=2, c=QP)
        q_neg = arena_b[:, 2048:2560].rearrange("p (c s) -> p c s", c=QP)
        sigma = arena_b[:, 2560:3072].rearrange("p (c s) -> p c s", c=QP)
        kf = arena_b[0:KV, 3072:3584].rearrange("p (c s) -> p c s", c=HH)
        q_parts = arena_b[:, 3584:4352].bitcast(bf16).rearrange("p (n c s) -> p n c s", n=3, c=QP)
        k_parts = arena_b[0:KV, 4352:5120].bitcast(bf16).rearrange("p (n c s) -> p n c s", n=3, c=HH)
        lora_b = arena_b[:, 5120:6400]
        x1 = arena_b[:, 2048:2560].rearrange("p (t d) -> p t d", t=ST)
        x1T = arena_b[:, 2560:3072].rearrange("p (c s) -> p c s", c=CC)
        x2 = arena_b[:, 3072:3584].rearrange("p (t d) -> p t d", t=ST)
        yf = arena_b[:, 4096:5120].rearrange("p (n f) -> p n f", n=2)
        x3 = arena_b[:, 5120:5632].rearrange("p (t d) -> p t d", t=ST)
        pre = arena_b[:, 5632:6144].rearrange("p (t d) -> p t d", t=ST)
        pre3 = sb("pre3", [P, ST, D], fp32)
        x2b = arena_b[:, 6144:6656].rearrange("p (t d) -> p t d", t=ST)
        rest = pre3[:, :, :].rearrange("p t d -> p (t d)")

        def bank(name):
            return stack.enter_context(nc.psum_tensor(name, [P, 512], fp32))

        exp_bank = [bank(f"exp_bank{i}") for i in range(EXP_BANKS)]
        max_bank = [bank(f"max_bank{i}") for i in range(MAX_BANKS)]
        pv_bank = bank("pv_bank")
        shared = [bank(f"shared{i}") for i in range(SHARED_BANKS)]

        HALVED = ("q", "up", "down", "cross")

        fill = [
            ("wqT", 0), ("xT", 0), ("wkvT", 0), ("begin", ("q", 0)), ("q", 0), ("mem_rhs", 0), ("kv", 0),
            ("fetch", 0), ("sigma", 0), ("ctxT", 0), ("xT", 1), ("xwT", 0), ("mem", (0, 0)), ("begin", ("q", 1)),
            ("q", 1), ("mem", (0, 1)), ("kv", 1), ("xq", 0), ("xk", 0), ("sigma", 1), ("energy", 0), ("load_ffn", 0),
            ("ctxT", 1), ("mem", (1, 0)), ("xT", 2), ("xT", 3), ("xattnT", 0), ("fetch", 1), ("mem", (1, 1)),
            ("lora_a", 0), ("begin", ("q", 2)), ("dequant", 0), ("lora_b", 0), ("q", 2), ("sigma", 2), ("kv", 2),
            ("xq", 1), ("loraT", 0), ("dequant", 1), ("energy", 1), ("mem", (2, 0)), ("loraT", 1), ("xk", 1),
            ("dequant", 2), ("xattnT", 1), ("lora_b", 1), ("mem", (2, 1)), ("dequant", 3), ("fetch", 2),
            ("lora_b", 2), ("begin", ("q", 3)), ("q", 3), ("loraT", 2), ("energy", 2), ("sigma", 3), ("kv", 3),
            ("xattnT", 2), ("dequant", 4), ("up_w", 0), ("up_w", 1), ("mem", (3, 0)), ("up_w", 2), ("dequant", 5),
            ("energy", 3), ("dequant", 6), ("mem", (3, 1)), ("up_w", 3), ("dn_w", 0), ("xattnT", 3), ("fetch", 3),
            ("dn_w", 1), ("dn_w", 2), ("dequant", 7), ("dn_w", 3), ("ln1_stats", 0), ("ln1", 0), ("x1T", 0),
            ("begin", ("cross", 0)), ("cross", 0), ("ln2_stats", 0), ("ln2", 0), ("x2T", 0),
            ("begin", ("up", (0, 0))), ("up", (0, 0)), ("begin", ("up", (0, 1))), ("up", (0, 1)),
            ("begin", ("up", (0, 2))), ("up", (0, 2)), ("begin", ("up", (0, 3))), ("up", (0, 3)), ("ln1_stats", 1),
            ("ln1", 1), ("x1T", 1), ("begin", ("cross", 1)), ("cross", 1), ("begin", ("down", (0, 0))),
            ("down", (0, 0)), ("ln2_stats", 1), ("begin", ("down", (0, 1))), ("down", (0, 1)), ("ln2", 1),
            ("x2T", 1), ("ln3_stats", 0), ("ln3", 0), ("begin", ("up", (1, 0))), ("up", (1, 0)), ("ln1_stats", 2),
            ("ln1", 2), ("begin", ("up", (1, 1))), ("up", (1, 1)), ("begin", ("up", (1, 2))), ("up", (1, 2)),
            ("x1T", 2), ("begin", ("up", (1, 3))), ("up", (1, 3)), ("begin", ("cross", 2)), ("cross", 2),
            ("ln2_stats", 2), ("begin", ("down", (1, 0))), ("down", (1, 0)), ("ln2", 2), ("begin", ("down", (1, 1))),
            ("down", (1, 1)), ("ln3_stats", 1), ("x2T", 2), ("ln3", 1), ("ln1_stats", 3), ("begin", ("up", (2, 0))),
            ("up", (2, 0)), ("begin", ("up", (2, 1))), ("up", (2, 1)), ("begin", ("up", (2, 2))), ("ln1", 3),
            ("up", (2, 2)), ("x1T", 3), ("begin", ("up", (2, 3))), ("up", (2, 3)), ("begin", ("cross", 3)),
            ("cross", 3), ("ln2_stats", 3), ("ln2", 3), ("begin", ("down", (2, 0))), ("down", (2, 0)), ("x2T", 3),
            ("begin", ("down", (2, 1))), ("down", (2, 1)), ("ln3_stats", 2), ("begin", ("up", (3, 0))),
            ("up", (3, 0)), ("begin", ("up", (3, 1))), ("up", (3, 1)), ("begin", ("up", (3, 2))), ("up", (3, 2)),
            ("begin", ("up", (3, 3))), ("up", (3, 3)), ("begin", ("down", (3, 0))), ("begin", ("down", (3, 1))),
            ("ln3", 2), ("down", (3, 0)), ("down", (3, 1)), ("ln3_stats", 3), ("ln3", 3),]
        start = 6
        lead = 18
        pace = [int(c) for c in (
            "132431011103103020 00023111 10124211 00203021 11020202 02102002 10010110 10000101 "
            "00123002 22340011 00010012 01001011 10010124 31200121 10010102 10020003 "
            "01001234 ").replace(" ", "")]
        max_pace = [int(c) for c in (
            "000003001101020121 02110011 32020201 00023111 11012103 00202111 11112121 01210011 "
            "00202112 11211202 00202200 21013101 00300102 31111010 11120120 02120000 "
            "00000000 ").replace(" ", "")]
        tail = 3
        pv_at = [1, 0, 0, 0, 1, 3, 1, 1, 2, 0, 0, 1, 1, 1, 1, 3]
        maxT_at = [6, 6, 7, 5, 6, 6, 6, 4, 7, 5, 5, 4, 5, 5, 6, 6]
        spread_at = [1, 6, 3, 4, 5, 4, 3, 5, 4, 2, 3, 3, 3, 4, 3, 6]
        act_late = (
            "ctxT", "xq", "xk", "mem", "mem_rhs", "spread", ("up", (0, 3)), ("xT", 0), ("down", (2, 0)),
            ("up", (2, 2)), ("ln3", 1), ("loraT", 1), ("x1T", 0), ("xT", 1), ("xT", 2), ("ln2_stats",
            1), ("energy", 1), ("spread", 9), ("mem", (1, 0)), ("ln2", 1), ("ctxT", 1), ("ln1", 0),
            ("up", (2, 3)), ("up", (3, 1)), ("sigma", 0), ("down", (2, 1)), ("ln3", 3), ("xq", 0),
            ("up", (0, 2)), ("sigma", 1), ("down", (0, 1)), ("cross", 3), ("ln2", 2), ("spread", 5),
            ("xk", 0), ("up", (3, 3)), ("up_w", 0), ("mem", (2, 1)), ("down", (3, 1)), ("mem", (0, 0)),
            ("energy", 3), ("x2T", 3), ("xattnT", 0), ("up", (2, 1)), ("up", (3, 0)), ("spread", 0),
            ("ln1_stats", 1), ("spread", 13), ("q", 1),)
        dve_late = (
            "pv", "maxT", "up", "down", "ctxT", "xq", "xk", ("cross", 3), ("x1T", 1), ("ln3_stats", 2),
            ("loraT", 2), ("xk", 0), ("up_w", 3), ("mem", (3, 0)), ("down", (0, 1)), ("xT", 0), ("down",
            (1, 1)), ("up", (3, 0)), ("dn_w", 3), ("up", (2, 2)), ("up", (1, 3)), ("xq", 1), ("up", (0,
            0)), ("up", (0, 3)), ("kv", 3), ("q", 3), ("ln3_stats", 0), ("up", (2, 3)), ("sigma", 2),
            ("wkvT", 0), ("xT", 1), ("spread", 12), ("spread", 1), ("ln1", 1), ("sigma", 1), ("xwT", 0),
            ("down", (3, 0)), ("ln3", 2), ("up", (3, 2)), ("up", (2, 1)), ("ln2_stats", 2), ("spread",
            8), ("sigma", 3), ("down", (2, 1)),)

        order = fill[:start]
        del fill[:start]

        def take(n=1):
            for _ in range(n):
                if not fill or fill[0][0] == "ln1_stats" and fill[0][1] * HP + HP - 1 not in spread_out:
                    break
                order.append(fill.pop(0))

        spread_out, max_banks = [], 0
        for k in range(-lead, UNITS * SUB):
            u, i = divmod(k, SUB)
            if u >= 0:
                order.append(("exp", (u, i)))
            for _ in range(max_pace[k + lead]):
                order.append(("max", divmod(max_banks, SUB)))
                max_banks += 1
            if u >= 1 and i == pv_at[u]:
                order.append(("pv", (u - 1, 1)))
            if u >= 0 and i == pv_at[u] + 4:
                order.append(("pv", (u, 0)))
            if 0 <= u + 1 < UNITS and i == maxT_at[u + 1]:
                order.append(("maxT", u + 1))
            if u >= 1 and i == spread_at[u]:
                order.append(("spread", u - 1))
                spread_out.append(u - 1)
            take(pace[k + lead])
        order.append(("pv", (UNITS - 1, 1)))
        take(tail)
        order.append(("spread", UNITS - 1))
        spread_out.append(UNITS - 1)
        take(len(fill))

        def behind(watch, late):
            stages, held = [], []
            for i, key in enumerate(order):
                if (key in late or key[0] in late) and watch in [near[0] for near in order[i + 1:i + 5]]:
                    held.append(key)
                    continue
                stages.append(key)
                if key[0] == watch:
                    stages += held
                    held = []
            return stages + held

        act_order, dve_order = behind("exp", act_late), behind("max", dve_late)

        sems = {}
        loads = ("wq", "wkv", "weight", "memory", "context", "cross_w", "up_w", "dn_w", "lora_a", "lora_b", "biases")
        by_pool = ("pool_step", "identities", "constants", "v_zeroed", "up_dequant", "dn_dequant",
                   "lora_a_split", "lora_b_split", "residual", "max_split", "rstd_ready", "y_lo_done",
                   "x2b_ready")
        by_act = ("wqT_ready", "wkvT_ready", "xT_ready", "qf_ready", "q_split", "q_exp", "kf_ready", "v_ready",
                  "xwT_ready", "ctxT_ready", "xq_ready", "xk_ready", "loraT_ready", "energy_exp",
                  "xattnT_ready", "w_hi_ready", "mix_exp", "probs_ready", "maxT_ready", "avT_ready",
                  "x1T_ready", "x2_hi_done", "yf_ready", "y_hi_done")
        by_dve = ("dve_step", "masks", "k_pattern_ready", "mix_ready", "mem_rhs_ready", "q_parts_ready",
                  "k_parts_ready", "sigma_ready", "memterm_ready", "energy_max", "xattn_ready", "w_ready",
                  "max_taken", "adot_ready", "attn_added", "moments_ready", "x1_ready", "x2_ready",
                  "cross_added", "x2_lo_done", "y_lo_last", "down_added", "x3_ready")
        by_pe = ("exp_scores", "max_scores", "pv_done")
        for name in (*("ld_" + n for n in loads), "k_rows", *by_pool, *by_act, *by_dve, *by_pe):
            sems[name] = sem(name)
        ld_x = [sem(f"ld_x{b}") for b in range(B)]
        q_written = [sem(f"q_written{b}") for b in range(B)]
        k_written = [sem(f"k_written{b}") for b in range(B)]
        qk_loaded = [sem(f"qk_loaded{b}") for b in range(B)]
        q_rest_loaded = [sem(f"q_rest_loaded{b}") for b in range(B)]
        stored = sem("stored")

        shared_full = [sem(f"shared_full{i}") for i in range(SHARED_BANKS)]
        release = {
            "wqT": lambda n: (sems["wqT_ready"], CC * QP), "wkvT": lambda n: (sems["wkvT_ready"], CC + 1),
            "xT": lambda b: (sems["xT_ready"], b + 1), "q": lambda b: (sems["qf_ready"], b + 1),
            "kv": lambda b: (sems["v_ready"], ST * (b + 1)), "mem_rhs": lambda n: (sems["mem_rhs_ready"], 2 * QQ),
            "mem": lambda n: (sems["memterm_ready"], ST * n[0] + n[1] + 1), "xwT": lambda n: (sems["xwT_ready"], 1),
            "ctxT": lambda n: (sems["ctxT_ready"], n + 1), "xq": lambda n: (sems["xq_ready"], n + 1),
            "xk": lambda n: (sems["xk_ready"], n + 1), "loraT": lambda n: (sems["loraT_ready"], n + 1),
            "energy": lambda b: (sems["energy_exp"], ST * (b + 1)), "xattnT": lambda b: (sems["xattnT_ready"], b + 1),
            "up_w": lambda j: (sems["w_ready"], j + 1), "dn_w": lambda j: (sems["w_ready"], 4 + j + 1),
            "maxT": lambda u: (sems["maxT_ready"], u + 1), "spread": lambda u: (sems["adot_ready"], ST * (u + 1)),
            "x1T": lambda b: (sems["x1T_ready"], b + 1), "cross": lambda b: (sems["cross_added"], b + 1),
            "x2T": lambda b: (sems["x2_lo_done"], b + 1), 
            "up": lambda n: (sems["y_hi_done"] if n[0] < B - 1 else sems["yf_ready"], 2 * (n[0] * (FC // 2) + n[1] + 1)),
            "down": lambda n: (sems["down_added"], ST * n[0] + n[1] + 1),
        }
        in_turn = [key[1] if key[0] == "begin" else key for key in order
                   if key[0] == "begin" or key[0] in release and key[0] not in HALVED]
        SLOT = {key: i for i, key in enumerate(in_turn)}

        def in_bank(eng, stage, n=0):
            i = SLOT[stage, n]
            eng.wait_ge(shared_full[i % SHARED_BANKS], i // SHARED_BANKS + 1)
            return shared[i % SHARED_BANKS]

        block = stack.enter_context(nc.Block())

        @block.sync
        def _(sp):
            sp.dma_start(wq_nat[:, :, :], wq.rearrange("(c p) d -> p c d", p=P)).then_inc(sems["ld_wq"], 16)
            sp.dma_start(xs[:, 0], x[0].rearrange("(t p) d -> p t d", p=P)).then_inc(ld_x[0], 16)
            sp.dma_start(wkv_nat[0:KV, :], wk).then_inc(sems["ld_wkv"], 16)
            sp.dma_start(wkv_nat[KV:2 * KV, :], wv).then_inc(sems["ld_wkv"], 16)
            sp.dma_start(mix[:, 0:1], memory_weight.partition_broadcast(P)).then_inc(sems["ld_weight"], 16)
            sp.dma_start(mem_nat[:, 0:KV], memory).then_inc(sems["ld_memory"], 16)
            sp.dma_start(mem_nat[:, KV:KV + 1], memory_norm).then_inc(sems["ld_memory"], 16)
            sp.dma_start(xs[:, 1], x[1].rearrange("(t p) d -> p t d", p=P)).then_inc(ld_x[1], 16)
            sp.dma_start(xw_nat[:, 0, :], xwq).then_inc(sems["ld_cross_w"], 16)
            sp.dma_start(xw_nat[:, 1, :], xwk).then_inc(sems["ld_cross_w"], 16)
            sp.dma_start(ctx_nat, ctx.rearrange("b (t p) c -> p (b t) c", p=P)).then_inc(sems["ld_context"], 16)
            sp.dma_start(xb[:, 0:1], xbq.rearrange("(p o) -> p o", o=1)).then_inc(sems["ld_cross_w"], 16)
            sp.dma_start(xb[:, 1:2], xbk.rearrange("(p o) -> p o", o=1)).then_inc(sems["ld_cross_w"], 16)
            sp.wait_ge(sems["k_pattern_ready"], 2 * HH)
            sp.dma_start(KT[ROWS:ROWS + MROWS].rearrange("p b a h t -> p (b a) (h t)"),
                         k_pattern[:, :, :].rearrange("p h t -> p (h t)").unsqueeze(1)
                         .broadcast_to([MROWS, B * HP, HH * S])).then_inc(sems["k_rows"], 16)
            for b in range(2, B):
                sp.dma_start(xs[:, b], x[b].rearrange("(t p) d -> p t d", p=P)).then_inc(ld_x[b], 16)
            for stage, n in order:
                if stage == "q":
                    sp.wait_ge(sems["q_parts_ready"], n + 1)
                    for g in range(QP):
                        sp.dma_start(q_scratch[n, :, g].rearrange("n r (a t) -> (r a) n t", t=S),
                                     q_parts[:, :, g, :]).then_inc(q_written[n], 16)
                if stage == "kv":
                    sp.wait_ge(sems["k_parts_ready"], n + 1)
                    sp.dma_start(k_scratch[n].rearrange("n r (a t) -> (r a) n t", a=HP),
                                 k_parts.rearrange("p n c t -> p n (c t)")).then_inc(k_written[n], 16)
                if stage == "fetch":
                    b = n
                    of_part = [slice(TERM_Q.index(part) * HD, (TERM_Q.index(part) + TERM_Q.count(part)) * HD)
                               for part in range(3)]
                    sp.wait_ge(k_written[b], 16)
                    for part, rows in enumerate(of_part):
                        sp.dma_start(KT[rows, b].rearrange("p a c t -> p (a c t)"),
                                     k_scratch[b, 0:TERM_Q.count(part)].rearrange("n r t -> (n r) t"))\
                            .then_inc(qk_loaded[b], 16)
                    sp.wait_ge(q_written[b], 16 * QP)
                    for g in range(QP):
                        for part, rows in enumerate(of_part):
                            sp.dma_start(QT[rows, b, g].rearrange("p a c t -> p (a c t)"),
                                         q_scratch[b, part, g].unsqueeze(0)
                                         .broadcast_to([TERM_Q.count(part), HD, HP * QQ * S]))\
                                .then_inc(q_rest_loaded[b] if g else qk_loaded[b], 16)
                if stage == "load_ffn":
                    sp.dma_start(up_raw.bitcast(i32), up_q.rearrange("(c p) d -> p c d", p=P))\
                        .then_inc(sems["ld_up_w"], 16)
                    sp.dma_start(upscale[:, :, :], up_scale.rearrange("(c p) k -> p c k", p=P))\
                        .then_inc(sems["ld_up_w"], 16)
                    sp.dma_start(dn_raw.bitcast(i32), dn_q.rearrange("(c p) f -> p c f", p=P))\
                        .then_inc(sems["ld_dn_w"], 16)
                    sp.dma_start(dnscale[:, :, :], dn_scale.rearrange("(c p) k -> p c k", p=P))\
                        .then_inc(sems["ld_dn_w"], 16)
                    sp.dma_start(lora_a[:, 0:CC], up_a.rearrange("(c p) r -> p c r", p=P))\
                        .then_inc(sems["ld_lora_a"], 16)
                    sp.dma_start(lora_a[:, CC:], dn_a.rearrange("(c p) r -> p c r", p=P))\
                        .then_inc(sems["ld_lora_a"], 16)
                    sp.dma_start(lora_b[:, 0:F], up_b.unsqueeze(0).broadcast_to([LORA_TERMS, R, F]))\
                        .then_inc(sems["ld_lora_b"], 16)
                    sp.dma_start(lora_b[:, F:], dn_b.unsqueeze(0).broadcast_to([LORA_TERMS, R, D]))\
                        .then_inc(sems["ld_lora_b"], 16)
                    sp.dma_start(upbias[:, :], up_bias.rearrange("(c p) -> p c", p=P),
                                 allow_slow_non_contiguous=True).then_inc(sems["ld_biases"], 16)
                    sp.dma_start(dnbias[:, :], dn_bias.partition_broadcast(P)).then_inc(sems["ld_biases"], 16)
                if stage == "ln3":
                    for t in range(ST):
                        sp.wait_ge(sems["x3_ready"], ST * n + t + 1)
                        sp.dma_start(out[n, t * P:(t + 1) * P, :], x3[:, t]).then_inc(stored, 16)
            sp.wait_ge(stored, 16 * ST * B)

        @block.gpsimd
        def _(pool):
            steps = [0]

            def step(ins):
                steps[0] += 1
                ins.then_inc(sems["pool_step"], 1)
                pool.wait_ge(sems["pool_step"], steps[0])

            for m in (ident, identb):
                step(pool.memset(m[:, :], 0.0))
                pool.affine_select(out=m[:, :], in_=m[:, :], compare_op=ALU.not_equal, fill=1.0, base=0,
                                   pattern=[[-1, P]], channel_multiplier=1).then_inc(sems["identities"], 1)
            pool.memset(half[:, :, :], -0.5).then_inc(sems["constants"], 1)

            def dequantise(raw, scale, done):
                step(pool.tensor_scalar(raw, raw.bitcast(i32), -7.5, 1.0, ALU.add, ALU.mult))
                blocks = raw.rearrange("p a (k q) -> p a k q", q=QB)
                pool.tensor_tensor(blocks, blocks, scale.unsqueeze(3).broadcast_to(blocks.shape), ALU.mult)\
                    .then_inc(done, 1)

            norms = [0]

            def inverse_root():
                norms[0] += 1
                pool.wait_ge(sems["moments_ready"], norms[0])
                step(pool.tensor_scalar(rstd[:, :, :], moments[:, :, 1:2], EPS, 1.0, ALU.add, ALU.mult))
                pool.tensor_tensor(rstd[:, :, :], rstd[:, :, :], half[:, :, :], ALU.pow).then_inc(sems["rstd_ready"], 1)

            pool.wait_ge(sems["constants"], 1)
            for stage, n in order:
                if stage == "mem":
                    b, t = n
                    pool.wait_ge(sems["memterm_ready"], ST * b + t + 1)
                    in_bank(pool, "xT", b)
                    pool.tensor_tensor(xs[:, b, t], xs[:, b, t], memterm[:, :], ALU.add).then_inc(sems["residual"], 1)
                if stage == "dequant" and n < 4:
                    pool.wait_ge(sems["ld_up_w"], 32)
                    dequantise(up_raw[:, 2 * n:2 * n + 2], upscale[:, 2 * n:2 * n + 2], sems["up_dequant"])
                if stage == "dequant" and n >= 4:
                    j, wide = n - 4, F // 4
                    pool.wait_ge(sems["ld_dn_w"], 32)
                    dequantise(dn_raw[:, :, j * wide:(j + 1) * wide],
                               dnscale[:, :, j * wide // QB:(j + 1) * wide // QB], sems["dn_dequant"])
                if stage == "lora_a":
                    pool.wait_ge(sems["ld_lora_a"], 32)
                    in_bank(pool, "ctxT", 1)
                    step(pool.memset(lora_a_parts, 0.0))
                    first = {part: LORA_TERM_A.index(part) for part in range(3)}
                    step(pool.tensor_copy(lora_a_parts[:, :, first[0]], lora_a[:, :, :]))
                    step(pool.tensor_tensor(lora_a[:, :, :], lora_a[:, :, :], lora_a_parts[:, :, first[0]], ALU.subtract))
                    step(pool.tensor_copy(lora_a_parts[:, :, first[1]], lora_a[:, :, :]))
                    pool.tensor_tensor(lora_a_parts[:, :, first[2]], lora_a[:, :, :], lora_a_parts[:, :, first[1]],
                                       ALU.subtract).then_inc(sems["lora_a_split"], 1)
                    for j, part in enumerate(LORA_TERM_A):
                        if part is not None and j != first[part]:
                            pool.tensor_copy(lora_a_parts[:, :, j], lora_a_parts[:, :, first[part]])\
                                .then_inc(sems["lora_a_split"], 1)
                if stage == "lora_b":
                    cols = slice(n * 512, min((n + 1) * 512, F + D))
                    pool.wait_ge(sems["ld_lora_b"], 32)
                    step(pool.tensor_copy(lora_b_parts[:, cols], lora_b[:, cols]))
                    step(pool.tensor_tensor(lora_b[64:P, cols], lora_b[64:P, cols], lora_b_parts[64:P, cols],
                                           ALU.subtract))
                    step(pool.tensor_copy(lora_b_parts[64:P, cols], lora_b[64:P, cols]))
                    pool.tensor_tensor(lora_b_parts[96:P, cols], lora_b[96:P, cols], lora_b_parts[96:P, cols],
                                      ALU.subtract).then_inc(sems["lora_b_split"], 1)
                    pool.wait_ge(sems["lora_b_split"], n + 1)
                if stage == "max" and n[1] == SUB - 1:
                    u = n[0]
                    pool.wait_ge(sems["max_taken"], SUB * (u + 1))
                    if u >= 2:
                        in_bank(pool, "maxT", u - 2)
                    parts = max_parts[:, u % 2].rearrange("p t g h n -> p (t g h) n")
                    m = maxes[:, u % 2].rearrange("p t g q h -> p (t g q h)")
                    step(pool.tensor_copy(parts[:, :, 0], m))
                    pool.tensor_tensor(parts[:, :, 1], m, parts[:, :, 0], ALU.subtract).then_inc(sems["max_split"], 1)
                if stage == "ln1_stats" and n < B - 1:
                    pool.wait_ge(sems["adot_ready"], ST * HP * (n + 1))
                    pool.wait_ge(sems["residual"], ST * (n + 1))
                    if n >= 1:
                        pool.wait_ge(sems["x2_ready"], ST * n)
                    pool.tensor_tensor(pre, xs[:, n], adot[:, n % 2], ALU.add).then_inc(sems["attn_added"], 1)
                if stage in ("ln1_stats", "ln2_stats", "ln3_stats"):
                    inverse_root()
                if stage == "ln3" and n < B - 1:
                    pool.wait_ge(sems["rstd_ready"], norms[0])
                    if n >= 1:
                        pool.wait_ge(stored, 16 * ST * n)
                    for t in range(ST):
                        pool.tensor_scalar(x3[:, t], pre3[:, t], moments[:, t, 0:1], rstd[:, t, :],
                                           ALU.subtract, ALU.mult).then_inc(sems["x3_ready"], 1)
                if stage == "ln2":
                    b = n
                    pool.wait_ge(sems["x2_ready"], ST * (b + 1))
                    if b >= 1:
                        pool.wait_ge(sems["down_added"], ST * b)
                    pool.wait_ge(sems["ld_biases"], 32)
                    pool.tensor_tensor(x2b, x2, dnbias[:, :].unsqueeze(1).broadcast_to([P, ST, D]), ALU.add)\
                        .then_inc(sems["x2b_ready"], 1)
                if stage == "up" and n[0] < B - 1:
                    b, j = n
                    i = b * (FC // 2) + j
                    pool.wait_ge(sems["yf_ready"], 2 * (i + 1))
                    pool.wait_ge(sems["y_hi_done"], 2 * (i + 1))
                    pool.tensor_tensor(y_lo[:, 2 * j:2 * j + 2].rearrange("p c t -> p (c t)"), yf[:, i % 2],
                                       y_hi[:, 2 * j:2 * j + 2].rearrange("p c t -> p (c t)").bitcast(fp32),
                                       ALU.subtract).then_inc(sems["y_lo_done"], 1)

        @block.scalar
        def _(act):
            for stage, n in act_order:
                if stage == "wqT":
                    src = in_bank(act, stage)[:, :].rearrange("p (c g q a r) -> p c g r a q", c=CC, g=QP, q=QQ, a=HP)
                    for c in range(CC):
                        for g in range(QP):
                            act.activation(wqT[:, c, g].rearrange("p (r a q) -> p r a q", a=HP, q=QQ),
                                           src[:, c, g], ACT.Copy).then_inc(sems["wqT_ready"], 1)
                if stage == "wkvT":
                    src = in_bank(act, stage)[:, 0:CC * P].rearrange("p (c o) -> p c o", c=CC)
                    for c in range(CC):
                        act.activation(wkvT[:, c, 0:KV].rearrange("p (r a) -> p r a", a=HP),
                                       src[:, c, 0:KV].rearrange("p (a r) -> p r a", a=HP), ACT.Copy)\
                            .then_inc(sems["wkvT_ready"], 1)
                    act.activation(wkvT[:, :, KV:P], src[:, :, KV:P], ACT.Copy).then_inc(sems["wkvT_ready"], 1)
                if stage == "xT":
                    if n >= 2:
                        in_bank(act, "q", n - 2)
                        in_bank(act, "kv", n - 2)
                    ps = in_bank(act, stage, n)
                    act.activation(xT[:, n % 2].rearrange("p c t -> p (c t)"), ps[:, :], ACT.Copy)\
                        .then_inc(sems["xT_ready"], 1)
                if stage == "xT" and n == 0:
                    act.wait_ge(sems["ld_weight"], 16)
                    act.activation(mix[:, 1:2], mix[:, 0:1], ACT.Exp, scale=-1.0).then_inc(sems["mix_exp"], 1)
                if stage == "q":
                    if n >= 2:
                        act.wait_ge(sems["q_parts_ready"], n - 1)
                    ps = in_bank(act, stage, n)
                    act.activation(qf[:, n % 2].rearrange("p c t -> p (c t)"), ps[:, :], ACT.Copy)\
                        .then_inc(sems["qf_ready"], 1)
                if stage == "kv":
                    ps = in_bank(act, stage, n)
                    if n == 0:
                        act.wait_ge(sems["masks"], 5)
                        act.wait_ge(sems["mix_ready"], 3)
                        act.wait_ge(sems["v_zeroed"], 1)
                    if n >= 1:
                        act.wait_ge(sems["k_parts_ready"], n)
                    for hh in range(HH):
                        act.activation(kf[:, hh], ps[0:KV, 0:S], ACT.Copy, scale=head_mask[:, hh:hh + 1])\
                            .then_inc(sems["kf_ready"], 1)
                    for t in range(ST):
                        act.activation(V[:, n, t, :, 0:DH],
                                       ps[:, S + t * KV:S + (t + 1) * KV].rearrange("p (h d) -> p h d", h=H),
                                       ACT.Copy, scale=mix[:, 4:5]).then_inc(sems["v_ready"], 1)
                if stage == "sigma":
                    if n >= 1:
                        in_bank(act, "mem", (n - 1, ST - 1))
                    act.wait_ge(sems["qf_ready"], n + 1)
                    act.activation(q_neg, qf[:, n % 2], ACT.Relu, scale=-1.0).then_inc(sems["q_split"], 1)
                    act.activation(sigma, qf[:, n % 2], ACT.Relu).then_inc(sems["q_split"], 1)
                    act.wait_ge(sems["q_split"], 2 * n + 1)
                    act.activation(q_neg, q_neg, ACT.Exp, scale=-1.0).then_inc(sems["q_exp"], 1)
                if stage == "xwT":
                    ps = in_bank(act, stage)
                    act.activation(xwT[:, :, :].rearrange("p c t -> p (c t)"), ps[:, 0:2 * C], ACT.Copy)\
                        .then_inc(sems["xwT_ready"], 1)
                if stage == "ctxT":
                    ps = in_bank(act, stage, n)
                    act.activation(ctxT[:, n * 512:(n + 1) * 512], ps[:, :], ACT.Copy).then_inc(sems["ctxT_ready"], 1)
                if stage in ("xq", "xk"):
                    ps = in_bank(act, stage, n)
                    to, k, done = (xq, 0, sems["xq_ready"]) if stage == "xq" else (xk, 1, sems["xk_ready"])
                    act.activation(to[:, n * 512:(n + 1) * 512], ps[:, :], ACT.Identity, bias=xb[:, k:k + 1])\
                        .then_inc(done, 1)
                if stage == "loraT":
                    ps = in_bank(act, stage, n)
                    to = lora_aT[:, 4 * n:min(4 * n + 4, CC + FC)].rearrange("p k t -> p (k t)")
                    act.activation(to, ps[:, :].bitcast(bf16)[:, 0:to.shape[1]], ACT.Copy)\
                        .then_inc(sems["loraT_ready"], 1)
                if stage == "energy":
                    b = n
                    act.wait_ge(sems["energy_max"], b + 1)
                    if b >= 1:
                        in_bank(act, "xattnT", b - 1)
                    ps = in_bank(act, stage, b)
                    for t in range(ST):
                        act.activation(energy[:, t], ps[:, t * S:(t + 1) * S], ACT.Exp,
                                       bias=energy_stat[:, b, 0, t:t + 1],
                                       accum_out=energy_stat[:, b, 1, t:t + 1]).then_inc(sems["energy_exp"], 1)
                if stage == "xattnT":
                    ps = in_bank(act, stage, n)
                    act.activation(xattnT[:, n].rearrange("p c t -> p (c t)"), ps[:, :], ACT.Copy)\
                        .then_inc(sems["xattnT_ready"], 1)
                if stage == "up_w":
                    ps = in_bank(act, stage, n)
                    c, half_f = divmod(n, 2)
                    act.activation(up_hi[:, c, half_f * 512:(half_f + 1) * 512], ps[:, :], ACT.Copy)\
                        .then_inc(sems["w_hi_ready"], 1)
                if stage == "dn_w":
                    ps = in_bank(act, stage, n)
                    act.activation(dn_hi[:, 2 * n:2 * n + 2].rearrange("p c t -> p (c t)"), ps[:, :], ACT.Copy)\
                        .then_inc(sems["w_hi_ready"], 1)
                if stage == "maxT":
                    b, hp = divmod(n, HP)
                    rows = slice(ROWS, ROWS + MROWS)
                    ps = in_bank(act, stage, n)[rows, :].bitcast(bf16).rearrange("p (g q t) -> p g q t", g=QP, q=QQ)
                    act.activation(QT[rows, b, :, hp], ps, ACT.Copy).then_inc(sems["maxT_ready"], 1)
                if stage == "exp":
                    u, i = n
                    k = u * SUB + i
                    act.wait_ge(sems["exp_scores"], k + 1)
                    h, j = divmod(k, QP * HH)
                    if h >= RING and j == 0:
                        act.wait_ge(sems["pv_done"], h - RING + 1)
                    act.activation(probs[:, (h % RING) * QP * HH + j], exp_bank[k % EXP_BANKS][:, :], ACT.Exp, scale=SCALE)\
                        .then_inc(sems["probs_ready"], 1)
                if stage == "pv" and n[1] == ST - 1:
                    u = n[0]
                    act.wait_ge(sems["pv_done"], ST * (u + 1))
                    if u >= 2:
                        in_bank(act, "spread", u - 2)
                    act.activation(avT[:, u % 2], pv_bank[:, :], ACT.Copy).then_inc(sems["avT_ready"], 1)
                if stage == "x1T":
                    if n >= 1:
                        in_bank(act, "cross", n - 1)
                    ps = in_bank(act, stage, n)
                    act.activation(x1T.rearrange("p c t -> p (c t)"), ps[:, :], ACT.Copy).then_inc(sems["x1T_ready"], 1)
                if stage == "x2T":
                    if n >= 1:
                        in_bank(act, "up", (n - 1, FC // 2 - 1))
                    ps = in_bank(act, stage, n)
                    act.activation(x2_hi[:, :, :].rearrange("p c t -> p (c t)"), ps[:, :], ACT.Copy)\
                        .then_inc(sems["x2_hi_done"], 1)
                if stage == "up":
                    b, j = n
                    i = b * (FC // 2) + j
                    if i == 0:
                        act.wait_ge(sems["ld_biases"], 32)
                        act.wait_ge(q_written[B - 1], 16 * QP)
                        act.wait_ge(k_written[B - 1], 16)
                    if b == B - 1 and j >= 2:
                        act.wait_ge(sems["y_lo_last"], j - 1)
                    elif i >= 2:
                        act.wait_ge(sems["y_lo_done"], i - 1)
                    ps = in_bank(act, stage, n)
                    for a in range(2):
                        act.activation(yf[:, i % 2, a * S:(a + 1) * S], ps[:, a * S:(a + 1) * S], ACT.Relu,
                                       bias=upbias[:, 2 * j + a:2 * j + a + 1]).then_inc(sems["yf_ready"], 1)
                    if b < B - 1:
                        if b >= 1 and j == 0:
                            in_bank(act, "down", (b - 1, ST - 1))
                        for a in range(2):
                            act.activation(y_hi[:, 2 * j + a], ps[:, a * S:(a + 1) * S], ACT.Relu,
                                           bias=upbias[:, 2 * j + a:2 * j + a + 1]).then_inc(sems["y_hi_done"], 1)

        @block.tensor
        def _(pe):
            def claim(stage, n=0, first=True):
                i = SLOT[stage, n]
                if first and i >= SHARED_BANKS:
                    before, m = in_turn[i - SHARED_BANKS]
                    pe.wait_ge(*release[before](m))
                return shared[i % SHARED_BANKS], shared_full[i % SHARED_BANKS]

            def turn(to, src, n=P):
                return pe.transpose(to, src, ident[0:n, 0:n])

            pe.wait_ge(sems["identities"], 2)
            for stage, n in order:
                begin = stage == "begin"
                halves = (0,) if begin else (1,)
                if begin:
                    stage, n = n
                if stage == "wqT":
                    pe.wait_ge(sems["ld_wq"], 16)
                    ps, full = claim(stage)
                    for c in range(CC):
                        for o in range(CC):
                            last = turn(ps[:, c * D + o * P:c * D + (o + 1) * P], wq_nat[:, o, c * P:(c + 1) * P])
                    last.then_inc(full, 1)
                if stage == "wkvT":
                    pe.wait_ge(sems["ld_wkv"], 32)
                    ps, full = claim(stage)
                    for c in range(CC):
                        last = turn(ps[:, c * P:(c + 1) * P], wkv_nat[:, c * P:(c + 1) * P])
                    last.then_inc(full, 1)
                if stage == "xT":
                    pe.wait_ge(ld_x[n], 16)
                    ps, full = claim(stage, n)
                    for c in range(CC):
                        for t in range(ST):
                            last = turn(ps[:, c * S + t * P:c * S + (t + 1) * P], xs[:, n, t, c * P:(c + 1) * P])
                    last.then_inc(full, 1)
                if stage == "q":
                    if begin:
                        pe.wait_ge(sems["xT_ready"], n + 1)
                        pe.wait_ge(sems["wqT_ready"], CC * QP)
                    ps, full = claim(stage, n, begin)
                    for g in halves:
                        for c in range(CC):
                            last = pe.matmul(ps[:, g * S:(g + 1) * S], wqT[:, c, g, :], xT[:, n % 2, c, :],
                                             start=c == 0, stop=c == CC - 1)
                    if not begin:
                        last.then_inc(full, 1)
                if stage == "kv":
                    pe.wait_ge(sems["wkvT_ready"], CC + 1)
                    pe.wait_ge(sems["xT_ready"], n + 1)
                    ps, full = claim(stage, n)
                    for c in range(CC):
                        pe.matmul(ps[0:KV, 0:S], wkvT[:, c, 0:KV], xT[:, n % 2, c, :], start=c == 0, stop=c == CC - 1)
                    for t in range(ST):
                        for c in range(CC):
                            last = pe.matmul(ps[:, S + t * KV:S + (t + 1) * KV], xT[:, n % 2, c, t * P:(t + 1) * P],
                                             wkvT[:, c, KV:P], start=c == 0, stop=c == CC - 1)
                    last.then_inc(full, 1)
                if stage == "mem_rhs":
                    pe.wait_ge(sems["ld_memory"], 32)
                    ps, full = claim(stage)
                    pe.wait_ge(sems["masks"], 6)
                    pe.matmul(ps[:, 0:KV + 1], pick[:, :], mem_nat[:, :], start=True, stop=True).then_inc(full, 1)
                if stage == "mem":
                    b, t = n
                    pe.wait_ge(sems["mem_rhs_ready"], 2 * QQ)
                    pe.wait_ge(sems["sigma_ready"], b + 1)
                    ps, full = claim(stage, n)
                    width = QQ * (KV + 1)
                    for g in range(QP):
                        last = pe.matmul(ps[:, g * width:(g + 1) * width], sigma[:, g, t * P:(t + 1) * P],
                                         mem_rhs[:, :, :].rearrange("p q e -> p (q e)"), start=True, stop=True)
                    last.then_inc(full, 1)
                if stage == "xwT":
                    pe.wait_ge(sems["ld_cross_w"], 64)
                    ps, full = claim(stage)
                    for k in range(2):
                        last = turn(ps[:, k * C:(k + 1) * C], xw_nat[:, k, :])
                    last.then_inc(full, 1)
                if stage == "ctxT":
                    pe.wait_ge(sems["ld_context"], 16)
                    ps, full = claim(stage, n)
                    for k in range(4):
                        last = turn(ps[:, k * P:(k + 1) * P], ctx_nat[:, 4 * n + k, :])
                    last.then_inc(full, 1)
                if stage in ("xq", "xk"):
                    pe.wait_ge(sems["xwT_ready"], 1)
                    pe.wait_ge(sems["ctxT_ready"], n + 1)
                    ps, full = claim(stage, n)
                    pe.matmul(ps[:, :], xwT[:, 0 if stage == "xq" else 1, :], ctxT[:, n * 512:(n + 1) * 512],
                              start=True, stop=True).then_inc(full, 1)
                if stage == "loraT":
                    pe.wait_ge(sems["lora_a_split"], 4)
                    ps, full = claim(stage, n)
                    for k in range(4 * n, min(4 * n + 4, CC + FC)):
                        last = pe.transpose(ps[:, :].bitcast(bf16)[:, k % 4 * P:(k % 4 + 1) * P],
                                            lora_a_parts[:, k].rearrange("p n r -> p (n r)"), identb[:, :])
                    last.then_inc(full, 1)
                if stage == "energy":
                    pe.wait_ge(sems["xq_ready"], n // 2 + 1)
                    pe.wait_ge(sems["xk_ready"], n // 2 + 1)
                    ps, full = claim(stage, n)
                    for t in range(ST):
                        last = pe.matmul(ps[:, t * S:(t + 1) * S], xq[:, n * S + t * P:n * S + (t + 1) * P],
                                         xk[:, n * S:(n + 1) * S], start=True, stop=True)
                    last.then_inc(full, 1)
                if stage == "xattnT":
                    pe.wait_ge(sems["xattn_ready"], ST * (n + 1))
                    ps, full = claim(stage, n)
                    for c in range(ST):
                        for t in range(ST):
                            last = turn(ps[:, c * S + t * P:c * S + (t + 1) * P], energy[:, t, c * P:(c + 1) * P])
                    last.then_inc(full, 1)
                if stage == "up_w":
                    c, half_f = divmod(n, 2)
                    pe.wait_ge(sems["loraT_ready"], 3)
                    pe.wait_ge(sems["lora_b_split"], 3)
                    pe.wait_ge(sems["up_dequant"], 2 * (half_f + 1))
                    ps, full = claim(stage, n)
                    pe.matmul(ps[:, :], lora_aT[:, c], lora_b_parts[:, half_f * 512:(half_f + 1) * 512],
                              start=True, stop=False)
                    for k in range(4):
                        last = pe.matmul(ps[:, k * P:(k + 1) * P], up_raw[:, 4 * half_f + k, c * P:(c + 1) * P],
                                         ident[:, :], start=False, stop=k == 3)
                    last.then_inc(full, 1)
                if stage == "dn_w":
                    pe.wait_ge(sems["dn_dequant"], n + 1)
                    ps, full = claim(stage, n)
                    for a in range(2):
                        f = 2 * n + a
                        pe.matmul(ps[:, a * D:(a + 1) * D], lora_aT[:, CC + f], lora_b_parts[:, F:],
                                  start=True, stop=False)
                        for c in range(CC):
                            last = pe.matmul(ps[:, a * D + c * P:a * D + (c + 1) * P], dn_raw[:, c, f * P:(f + 1) * P],
                                             ident[:, :], start=False, stop=c == CC - 1)
                    last.then_inc(full, 1)
                if stage == "max":
                    u, i = n
                    b, hp = divmod(u, HP)
                    k = u * SUB + i
                    gq, t = divmod(i, ST)
                    if i == 0 and hp == 0:
                        pe.wait_ge(qk_loaded[b], 16 * 6)
                    if hp == 0 and gq == QQ and t == 0:
                        pe.wait_ge(q_rest_loaded[b], 16 * 3 * (QP - 1))
                    if k >= MAX_BANKS:
                        pe.wait_ge(sems["max_taken"], k - MAX_BANKS + 1)
                    pe.matmul(max_bank[k % MAX_BANKS][:, :], QT[0:ROWS, b, gq // QQ, hp, gq % QQ, t * P:(t + 1) * P],
                              KT[0:ROWS, b, hp].rearrange("p h t -> p (h t)"), start=True, stop=True)\
                        .then_inc(sems["max_scores"], 1)
                if stage == "maxT":
                    u = n
                    pe.wait_ge(sems["max_split"], u + 1)
                    ps, full = claim(stage, u)
                    for g in range(G):
                        for t in range(ST):
                            last = pe.transpose(
                                ps[ROWS:ROWS + MROWS, :].bitcast(bf16)[:, (g * ST + t) * P:(g * ST + t + 1) * P],
                                max_parts[:, u % 2, t, g].rearrange("p h n -> p (h n)"), identb[:, :])
                    last.then_inc(full, 1)
                if stage == "exp":
                    u, i = n
                    b, hp = divmod(u, HP)
                    k = u * SUB + i
                    t, g, hh = i // (QP * HH), i // HH % QP, i % HH
                    if i == 0:
                        pe.wait_ge(sems["maxT_ready"], u + 1)
                        pe.wait_ge(sems["k_rows"], 16)
                    if k >= EXP_BANKS:
                        pe.wait_ge(sems["probs_ready"], k - EXP_BANKS + 1)
                    pe.matmul(exp_bank[k % EXP_BANKS][:, :], KT[0:ROWS + MROWS, b, hp, hh, t * P:(t + 1) * P],
                              QT[0:ROWS + MROWS, b, g, hp].rearrange("p q t -> p (q t)"), start=True, stop=True)\
                        .then_inc(sems["exp_scores"], 1)
                if stage == "pv":
                    u, t = n
                    b, hp = divmod(u, HP)
                    h = ST * u + t
                    pe.wait_ge(sems["probs_ready"], QP * HH * (h + 1))
                    if t == 0:
                        pe.wait_ge(sems["v_ready"], ST * (b + 1))
                    if u >= 1 and t == 0:
                        pe.wait_ge(sems["avT_ready"], u)
                    for hh in range(HH):
                        for g in range(QP):
                            j = hh * QP + g
                            last = pe.matmul(pv_bank[j * VC:(j + 1) * VC, :], V[:, b, t, HH * hp + hh, :],
                                             probs[:, (h % RING) * QP * HH + g * HH + hh],
                                             start=t == 0, stop=t == ST - 1)
                    last.then_inc(sems["pv_done"], 1)
                if stage == "spread":
                    u = n
                    pe.wait_ge(sems["avT_ready"], u + 1)
                    ps, full = claim(stage, u)
                    cols = ps[:, :].rearrange("p (t j q c) -> p t q j c", t=ST, j=HH * QP, q=QQ)
                    for q in range(QQ):
                        for t in range(ST):
                            last = turn(cols[:, t, q], avT[:, u % 2, (q * ST + t) * P:(q * ST + t + 1) * P])
                    last.then_inc(full, 1)
                if stage in ("x1T", "x2T"):
                    src, ready = (x1, sems["x1_ready"]) if stage == "x1T" else (x2, sems["x2_ready"])
                    pe.wait_ge(ready, ST * (n + 1))
                    ps, full = claim(stage, n)
                    for c in range(CC):
                        for t in range(ST):
                            last = turn(ps[:, c * S + t * P:c * S + (t + 1) * P], src[:, t, c * P:(c + 1) * P])
                    last.then_inc(full, 1)
                if stage == "cross":
                    if begin:
                        pe.wait_ge(sems["x1T_ready"], n + 1)
                        pe.wait_ge(sems["xattnT_ready"], n + 1)
                    ps, full = claim(stage, n, begin)
                    for t in halves:
                        for c in range(CC):
                            last = pe.matmul(ps[:, t * S:(t + 1) * S], x1T[:, c, t * P:(t + 1) * P], xattnT[:, n, c, :],
                                             start=c == 0, stop=c == CC - 1)
                    if not begin:
                        last.then_inc(full, 1)
                if stage == "up":
                    b, j = n
                    if begin:
                        pe.wait_ge(sems["x2_lo_done"], b + 1)
                        pe.wait_ge(sems["w_ready"], 8)
                    ps, full = claim(stage, n, begin)
                    for a in halves:
                        f = slice((2 * j + a) * P, (2 * j + a + 1) * P)
                        products = [(w, xx, c) for c in range(CC)
                                    for w, xx in ((up_hi, x2_hi), (up_hi, x2_lo), (up_lo, x2_hi))]
                        for m, (w, xx, c) in enumerate(products):
                            last = pe.matmul(ps[:, a * S:(a + 1) * S], w[:, c, f], xx[:, c, :],
                                             start=m == 0, stop=m == len(products) - 1)
                    if not begin:
                        last.then_inc(full, 1)
                if stage == "down":
                    b, t = n
                    ready = FC // 4 if begin else FC // 2
                    if b < B - 1:
                        pe.wait_ge(sems["y_lo_done"], (FC // 2) * b + ready)
                    else:
                        pe.wait_ge(sems["y_lo_last"], ready)
                    ps, full = claim(stage, n, begin)
                    for f in range(FC // 2 * halves[0], FC // 2 * (halves[0] + 1)):
                        for m, (yy, w) in enumerate(((y_hi, dn_hi), (y_hi, dn_lo), (y_lo, dn_hi))):
                            last = pe.matmul(ps[:, 0:D], yy[:, f, t * P:(t + 1) * P], w[:, f, :],
                                             start=(f, m) == (0, 0), stop=(f, m) == (FC - 1, 2))
                    if not begin:
                        last.then_inc(full, 1)

        @block.vector
        def _(dve):
            steps = [0]

            def step(ins):
                steps[0] += 1
                ins.then_inc(sems["dve_step"], 1)
                dve.wait_ge(sems["dve_step"], steps[0])

            for hh in range(HH):
                own, other = (0.0, -1.0) if hh else (-1.0, 0.0)
                step(dve.memset(k_pattern[:, hh, :], other))
                dve.memset(k_pattern[0:2, hh, :], own).then_inc(sems["k_pattern_ready"], 2)
            for hh in range(HH):
                for row in range(HH):
                    dve.memset(head_mask[row * 32:(row + 1) * 32, hh:hh + 1], float(row == hh)).then_inc(sems["masks"], 1)
            dve.wait_ge(sems["identities"], 1)
            dve.tensor_reduce(group_mask[:, :], ident[:, :].rearrange("p (j q) -> p q j", q=QQ), X, ALU.add)\
                .then_inc(sems["masks"], 1)
            dve.tensor_copy(pick[:, :].rearrange("k (r a q) -> k r a q", a=HP, q=QQ),
                            ident[0:KV, 0:KV].rearrange("k (a r) -> k r a", a=HP).unsqueeze(3)
                            .broadcast_to([KV, HD, HP, QQ])).then_inc(sems["masks"], 1)
            step(dve.memset(V[:, :, :, :, :], 0.0))
            dve.memset(V[:, :, :, :, DH:DH + 1], 1.0).then_inc(sems["v_zeroed"], 1)
            splits = []

            def split3(parts, src, spare, done, b):
                if splits:
                    dve.wait_ge(*splits.pop())
                step(dve.tensor_copy(parts[:, 0], src))
                step(dve.tensor_tensor(spare, src, parts[:, 0], ALU.subtract))
                step(dve.tensor_copy(parts[:, 1], spare))
                dve.tensor_tensor(parts[:, 2], spare, parts[:, 1], ALU.subtract).then_inc(done, 1)
                splits.append((done, b + 1))

            norms, normalised = [0], []

            def statistics(src):
                if normalised:
                    dve.wait_ge(*normalised.pop())
                for t in range(ST):
                    last = dve.bn_stats(stats[:, t, :], src[:, t])
                step(last)
                norms[0] += 1
                for t in range(ST):
                    last = dve.bn_aggr(moments[:, t, :], stats[:, t, :])
                last.then_inc(sems["moments_ready"], 1)

            def normalise(to, src, done, b):
                dve.wait_ge(sems["rstd_ready"], norms[0])
                dve.wait_ge(sems["moments_ready"], norms[0])
                for t in range(ST):
                    dve.tensor_scalar(to[:, t], src[:, t], moments[:, t, 0:1], rstd[:, t, :],
                                      ALU.subtract, ALU.mult).then_inc(done, 1)
                normalised.append((done, ST * (b + 1)))

            for stage, n in dve_order:
                if stage == "xT" and n == 0:
                    dve.wait_ge(sems["mix_exp"], 1)
                    dve.tensor_scalar(mix[:, 2:3], mix[:, 1:2], 1.0, None, ALU.add).then_inc(sems["mix_ready"], 1)
                    dve.wait_ge(sems["mix_ready"], 1)
                    dve.reciprocal(mix[:, 3:4], mix[:, 2:3]).then_inc(sems["mix_ready"], 1)
                    dve.wait_ge(sems["mix_ready"], 2)
                    dve.tensor_scalar(mix[:, 4:5], mix[:, 3:4], -1.0, 1.0, ALU.mult, ALU.add).then_inc(sems["mix_ready"], 1)
                if stage == "q":
                    dve.wait_ge(sems["qf_ready"], n + 1)
                    if n >= 1:
                        dve.wait_ge(q_written[n - 1], 16 * QP)
                    split3(q_parts, qf[:, n % 2], rest.rearrange("p (c t) -> p c t", c=QP), sems["q_parts_ready"], n)
                if stage == "kv":
                    dve.wait_ge(sems["kf_ready"], HH * (n + 1))
                    if n >= 1:
                        dve.wait_ge(k_written[n - 1], 16)
                    split3(k_parts, kf, rest[0:KV].rearrange("p (c t) -> p c t", c=HH), sems["k_parts_ready"], n)
                if stage == "sigma":
                    dve.wait_ge(sems["q_exp"], n + 1)
                    dve.wait_ge(sems["q_split"], 2 * (n + 1))
                    dve.scalar_tensor_tensor(out=sigma, in0=q_neg, scalar=-1.0, in1=sigma, op0=ALU.add, op1=ALU.add)\
                        .then_inc(sems["sigma_ready"], 1)
                if stage == "mem_rhs":
                    ps = in_bank(dve, stage)
                    dve.wait_ge(sems["mix_ready"], 3)
                    dve.wait_ge(sems["masks"], 5)
                    for q in range(QQ):
                        dve.tensor_scalar(mem_rhs[:, q, 0:KV], ps[:, 0:KV], group_mask[:, q:q + 1], mix[:, 3:4],
                                          ALU.mult, ALU.mult).then_inc(sems["mem_rhs_ready"], 1)
                        dve.tensor_scalar(mem_rhs[:, q, KV:KV + 1], ps[:, KV:KV + 1], group_mask[:, q:q + 1], None,
                                          ALU.mult).then_inc(sems["mem_rhs_ready"], 1)
                if stage == "mem":
                    b, t = n
                    ps = in_bank(dve, stage, n)[:, 0:G * (KV + 1)].rearrange("p (g e) -> p g e", g=G)
                    if n != (0, 0):
                        dve.wait_ge(sems["memterm_ready"], ST * b + t)
                    step(dve.reciprocal(memrec[:, :], ps[:, :, KV]))
                    if n != (0, 0):
                        dve.wait_ge(sems["residual"], ST * b + t)
                    dve.tensor_tensor(memterm[:, :].rearrange("p (g e) -> p g e", g=G), ps[:, :, 0:KV],
                                      memrec[:, :].unsqueeze(2).broadcast_to([P, G, KV]), ALU.mult)\
                        .then_inc(sems["memterm_ready"], 1)
                if stage == "energy":
                    ps = in_bank(dve, stage, n)
                    dve.tensor_reduce(energy_stat[:, n, 0, :], ps[:, :].rearrange("p (t c) -> p t c", t=ST), X, ALU.max,
                                      negate=True).then_inc(sems["energy_max"], 1)
                if stage == "xattnT":
                    dve.wait_ge(sems["energy_exp"], ST * (n + 1))
                    step(dve.reciprocal(energy_stat[:, n, 2, :], energy_stat[:, n, 1, :]))
                    for t in range(ST):
                        dve.tensor_scalar(energy[:, t], energy[:, t], energy_stat[:, n, 2, t:t + 1], None, ALU.mult)\
                            .then_inc(sems["xattn_ready"], 1)
                if stage in ("up_w", "dn_w"):
                    i = n + (4 if stage == "dn_w" else 0)
                    dve.wait_ge(sems["w_hi_ready"], i + 1)
                    ps = in_bank(dve, stage, n)
                    if stage == "up_w":
                        c, half_f = divmod(n, 2)
                        hi, lo = (m[:, c, half_f * 512:(half_f + 1) * 512] for m in (up_hi, up_lo))
                    else:
                        hi, lo = (m[:, 2 * n:2 * n + 2].rearrange("p c t -> p (c t)") for m in (dn_hi, dn_lo))
                    dve.tensor_tensor(lo, ps[:, :], hi.bitcast(fp32), ALU.subtract).then_inc(sems["w_ready"], 1)
                if stage == "max":
                    u, i = n
                    k = u * SUB + i
                    gq, t = divmod(i, ST)
                    if u >= 2 and i == 0:
                        dve.wait_ge(sems["max_split"], u - 1)
                    dve.wait_ge(sems["max_scores"], k + 1)
                    dve.tensor_reduce(maxes[:, u % 2, t, gq // QQ, gq % QQ, :],
                                      max_bank[k % MAX_BANKS][:, :].rearrange("p (h t) -> p h t", h=HH), X, ALU.max)\
                        .then_inc(sems["max_taken"], 1)
                if stage == "spread":
                    u = n
                    b, hp = divmod(u, HP)
                    ps = in_bank(dve, stage, u)[:, :].rearrange("p (t h g c) -> p t h g c", t=ST, h=HH, g=G)
                    r = rec[:, u % 2, :].rearrange("p (t h g) -> p t h g", t=ST, h=HH)
                    if u >= 2:
                        dve.wait_ge(sems["adot_ready"], ST * (u - 1))
                    step(dve.reciprocal(r.rearrange("p t h g -> p (t h g)"),
                                        ps.rearrange("p t h g c -> p (t h g) c")[:, :, DH]))
                    if b >= 2 and hp == 0:
                        dve.wait_ge(sems["attn_added"], b - 1)
                    for t in range(ST):
                        to = adot[:, b % 2, t].rearrange("p (g a h d) -> p a h g d", g=G, a=HP, h=HH)[:, hp]
                        dve.tensor_tensor(to, ps[:, t, :, :, 0:DH], r[:, t].unsqueeze(3).broadcast_to([P, HH, G, DH]),
                                          ALU.mult).then_inc(sems["adot_ready"], 1)
                if stage == "ln1_stats" and n == B - 1:
                    dve.wait_ge(sems["adot_ready"], ST * HP * (n + 1))
                    dve.wait_ge(sems["residual"], ST * (n + 1))
                    if n >= 1:
                        dve.wait_ge(sems["x2_ready"], ST * n)
                    dve.tensor_tensor(pre, xs[:, n], adot[:, n % 2], ALU.add).then_inc(sems["attn_added"], 1)
                if stage == "ln1_stats":
                    dve.wait_ge(sems["attn_added"], n + 1)
                    statistics(pre)
                if stage == "ln1":
                    if n >= 1:
                        dve.wait_ge(sems["cross_added"], n)
                    normalise(x1, pre, sems["x1_ready"], n)
                if stage == "cross":
                    ps = in_bank(dve, stage, n)
                    dve.wait_ge(sems["x1_ready"], ST * (n + 1))
                    dve.tensor_tensor(pre.rearrange("p t d -> p (t d)"), ps[:, :], x1.rearrange("p t d -> p (t d)"),
                                      ALU.add).then_inc(sems["cross_added"], 1)
                if stage == "ln2_stats":
                    dve.wait_ge(sems["cross_added"], n + 1)
                    statistics(pre)
                if stage == "ln2":
                    if n >= 1:
                        dve.wait_ge(sems["x2b_ready"], n)
                        in_bank(dve, "x2T", n - 1)
                    normalise(x2, pre, sems["x2_ready"], n)
                if stage == "x2T":
                    ps = in_bank(dve, stage, n)
                    dve.wait_ge(sems["x2_hi_done"], n + 1)
                    dve.tensor_tensor(x2_lo[:, :, :].rearrange("p c t -> p (c t)"), ps[:, :],
                                      x2_hi[:, :, :].rearrange("p c t -> p (c t)").bitcast(fp32), ALU.subtract)\
                        .then_inc(sems["x2_lo_done"], 1)
                if stage == "up" and n[0] == B - 1:
                    b, j = n
                    i = b * (FC // 2) + j
                    dve.wait_ge(sems["yf_ready"], 2 * (i + 1))
                    if j == 0:
                        in_bank(dve, "down", (b - 1, ST - 1))
                    hi, lo = (m[:, 2 * j:2 * j + 2].rearrange("p c t -> p (c t)") for m in (y_hi, y_lo))
                    step(dve.tensor_copy(hi, yf[:, i % 2]))
                    dve.tensor_tensor(lo, yf[:, i % 2], hi.bitcast(fp32), ALU.subtract).then_inc(sems["y_lo_last"], 1)
                if stage == "down":
                    b, t = n
                    ps = in_bank(dve, stage, n)
                    dve.wait_ge(sems["x2b_ready"], b + 1)
                    dve.wait_ge(sems["x2_ready"], ST * (b + 1))
                    if b >= 1 and t == 0:
                        dve.wait_ge(sems["x3_ready"], ST * b)
                    dve.tensor_tensor(pre3[:, t], ps[:, 0:D], x2b[:, t], ALU.add).then_inc(sems["down_added"], 1)
                if stage == "ln3_stats":
                    dve.wait_ge(sems["down_added"], ST * (n + 1))
                    statistics(pre3)
                if stage == "ln3" and n < B - 1:
                    normalised.append((sems["x3_ready"], ST * (n + 1)))
                if stage == "ln3" and n == B - 1:
                    dve.wait_ge(stored, 16 * ST * n)
                    normalise(x3, pre3, sems["x3_ready"], n)


_INS = ["x", "ctx_1024", "L0_attn_Wq", "L0_attn_Wk", "L0_attn_Wv", "L0_attn_memory", "L0_attn_memory_norm",
        "L0_attn_memory_weight", "L0_xattn_Wq", "L0_xattn_bq", "L0_xattn_Wk", "L0_xattn_bk",
        "L0_ffn_w_up_q", "L0_ffn_w_up_scale", "L0_ffn_b_up", "L0_ffn_w_up_lora_a", "L0_ffn_w_up_lora_b",
        "L0_ffn_w_down_q", "L0_ffn_w_down_scale", "L0_ffn_b_down", "L0_ffn_w_down_lora_a", "L0_ffn_w_down_lora_b"]


def kernel(**inputs):
    import numpy as _np
    import concourse.bacc as _bacc
    from concourse import mybir as _mybir
    from concourse.bass_utils import run_bass_kernel_spmd as _run

    nc = _bacc.Bacc("TRN2", target_bir_lowering=False, num_devices=1)
    arrays, args = {}, []
    for name in _INS:
        a = _np.ascontiguousarray(inputs[name])
        arrays[f"in_{name}"] = a
        args.append(nc.dram_tensor(f"in_{name}", a.shape, _mybir.dt.from_np(a.dtype), kind="ExternalInput").ap())
    shape = inputs["x"].shape
    args.append(nc.dram_tensor("out_0", shape, _mybir.dt.float32, kind="ExternalOutput").ap())
    build_decoder(nc, *args)
    r = _run(nc, [arrays], core_ids=[0])
    return r.results[0]["out_0"]
```
